# Optimizing a Trainium2 kernel written in Bass

```python
import numpy as np
import jax
import jax.numpy as jnp

def _softmax(x, axis=-1):
    return jax.nn.softmax(x, axis=axis)

def _gelu(x):
    return jax.nn.gelu(x, approximate=True)

def _silu(x):
    return jax.nn.silu(x)

def _sigmoid(x):
    return jax.nn.sigmoid(x)

def _layernorm(x, axis=-1, eps=1e-05):
    m = jnp.mean(x, axis=axis, keepdims=True)
    v = jnp.var(x, axis=axis, keepdims=True)
    return (x - m) / jnp.sqrt(v + eps)

def _scatter_add(tgt, idx, src, axis=0):
    return tgt.at[idx].add(src)

def _segment_sum(src, seg, n):
    return jax.ops.segment_sum(src, seg, n)
kernel_name = 'mk_gnn_ffn_d4_gnn_r32_ba5d95'

def setup_inputs(seed: int=0):
    np.random.seed(seed)
    _w = jnp.asarray

    def _rec_inputs():
        import jax
        import jax.numpy as jnp
        _gk = jax.random.key(seed)
        x = -0.0003713 + 1 * jax.random.normal(jax.random.fold_in(_gk, 1), (3125, 256), jnp.float32)
        _s = jax.random.randint(jax.random.fold_in(_gk, 2), (25000,), 0, 3125, jnp.int32)
        _d = jax.random.randint(jax.random.fold_in(_gk, 3), (25000,), 0, 3125, jnp.int32)
        _loop = jnp.arange(3125, dtype=jnp.int32)
        src = jnp.concatenate([_s, _d, _loop])
        dst = jnp.concatenate([_d, _s, _loop])
        _o = jnp.argsort(dst, stable=True)
        src = src[_o]
        dst = dst[_o]
        edge_type_7 = jax.random.randint(jax.random.fold_in(_gk, 12), (53125,), 0, 7, jnp.int32)
        edge_weight = jax.random.uniform(jax.random.fold_in(_gk, 13), (53125,), jnp.float32, 0.0, 0.999998)
        return (x, src, dst, edge_type_7, edge_weight)
    x, src, dst, edge_type_7, edge_weight = _rec_inputs()

    def _L0_gnn_setup():
        import jax, jax.numpy as jnp
        import numpy as np
        N_NODES = 50000
        N_EDGES = 25000
        IN_F = 256
        OUT_F = 64
        HEADS = 4
        NEG_SLOPE = 0.2
        key = jax.random.key(seed)
        ks = jax.random.split(key, 6)
        x = jax.random.normal(ks[0], (N_NODES, IN_F), dtype=jnp.float32)
        edge_index = jax.random.randint(ks[1], (2, N_EDGES), 0, N_NODES, dtype=jnp.int32)
        edge_weight = jax.random.uniform(ks[2], (N_EDGES,), dtype=jnp.float32)
        gain = float(np.sqrt(2.0 / (1.0 + NEG_SLOPE ** 2)))
        w_bound = gain * np.sqrt(6.0 / (IN_F + OUT_F))
        a_bound = gain * np.sqrt(6.0 / (OUT_F + 1))
        W = jax.random.uniform(ks[3], (HEADS, IN_F, OUT_F), minval=-w_bound, maxval=w_bound, dtype=jnp.float32)
        a_src = jax.random.uniform(ks[4], (HEADS, OUT_F, 1), minval=-a_bound, maxval=a_bound, dtype=jnp.float32)
        a_dst = jax.random.uniform(ks[5], (HEADS, OUT_F, 1), minval=-a_bound, maxval=a_bound, dtype=jnp.float32)
        return {'x': x, 'edge_index': edge_index, 'edge_weight': edge_weight, 'W': W, 'a_src': a_src, 'a_dst': a_dst}
    _L0_gnn_all = _L0_gnn_setup()
    _L0_gnn_in = {k: v for k, v in _L0_gnn_all.items() if k in ('W', 'a_src', 'a_dst')}
    del _L0_gnn_all

    def _L0_ffn_setup():
        import jax, jax.numpy as jnp
        import numpy as np
        B, K, D = (512, 16, 256)
        E = 32
        H = int(D * 0.25)
        key = jax.random.key(seed)
        ks = jax.random.split(key, 7)
        d_rs = D ** (-0.5)
        h_rs = H ** (-0.5)
        x = jax.random.normal(ks[0], (B, K, D), dtype=jnp.float32)
        router_w = jax.random.uniform(ks[1], (E, D), jnp.float32, -d_rs, d_rs)
        router_b = jax.random.uniform(ks[2], (E,), jnp.float32, -d_rs, d_rs)
        W1 = jax.random.uniform(ks[3], (E, D, H), jnp.float32, -h_rs, h_rs)
        b1 = jax.random.uniform(ks[4], (E, H), jnp.float32, -h_rs, h_rs)
        W2 = jax.random.uniform(ks[5], (E, H, D), jnp.float32, -d_rs, d_rs)
        b2 = jax.random.uniform(ks[6], (E, D), jnp.float32, -d_rs, d_rs)
        return {'x': x, 'router_w': router_w, 'router_b': router_b, 'W1': W1, 'b1': b1, 'W2': W2, 'b2': b2}
    _L0_ffn_all = _L0_ffn_setup()
    _L0_ffn_in = {k: v for k, v in _L0_ffn_all.items() if k in ('router_w', 'router_b', 'W1', 'b1', 'W2', 'b2')}
    del _L0_ffn_all

    def _L1_gnn_setup():
        import jax, jax.numpy as jnp
        import numpy as np
        N_EDGE_TYPE = 7
        key = jax.random.key(seed)
        k1, k2, k3, k4, k5 = jax.random.split(key, 5)
        N, E, C_in, C_out = (50000, 350000, 256, 256)
        x = jax.random.normal(k1, (N, C_in), dtype=jnp.float32)
        edge_index = jax.random.randint(k2, (2, E), 0, N, dtype=jnp.int64)
        edge_type = jax.random.randint(k3, (E,), 0, N_EDGE_TYPE, dtype=jnp.int64)
        import math
        avg_degree = 7
        std = math.sqrt(2.0 / float(avg_degree * C_in + avg_degree * C_out))
        a = math.sqrt(3.0) * std
        weights = jax.random.uniform(k4, (N_EDGE_TYPE * C_in, C_out), dtype=jnp.float32, minval=-a, maxval=a)
        return {'x': x, 'edge_index': edge_index, 'edge_type': edge_type, 'weights': weights}
    _L1_gnn_all = _L1_gnn_setup()
    _L1_gnn_in = {k: v for k, v in _L1_gnn_all.items() if k in ('weights',)}
    del _L1_gnn_all

    def _L1_ffn_setup():
        import jax, jax.numpy as jnp
        import numpy as np
        B, A = (128, 8)
        IN, OUT = (256, 256)
        SH1, SH2 = (256, 128)
        EH1, EH2 = (128, 64)
        E, TOPK = (4, 2)

        def _shared_mlp(x, W1, b1, W2, b2, W3, b3):
            h = jax.nn.relu(x @ W1 + b1)
            h = jax.nn.relu(h @ W2 + b2)
            return h @ W3 + b3

        def _experts_mlp(x, eW1, eb1, eW2, eb2, eW3, eb3):
            h = jax.nn.relu(jnp.einsum('baf,efh->ebah', x, eW1) + eb1[:, None, None, :])
            h = jax.nn.relu(jnp.einsum('ebah,ehg->ebag', h, eW2) + eb2[:, None, None, :])
            o = jnp.einsum('ebag,ego->ebao', h, eW3) + eb3[:, None, None, :]
            return jnp.moveaxis(o, 0, -1)
        key = jax.random.key(seed)
        ks = jax.random.split(key, 16)
        s = 0.05
        return {'x': jax.random.normal(ks[0], (B, A, IN), jnp.float32), 'sW1': jax.random.normal(ks[1], (IN, SH1), jnp.float32) * s, 'sb1': jnp.zeros((SH1,), jnp.float32), 'sW2': jax.random.normal(ks[2], (SH1, SH2), jnp.float32) * s, 'sb2': jnp.zeros((SH2,), jnp.float32), 'sW3': jax.random.normal(ks[3], (SH2, OUT), jnp.float32) * s, 'sb3': jnp.zeros((OUT,), jnp.float32), 'eW1': jax.random.normal(ks[4], (E, IN, EH1), jnp.float32) * s, 'eb1': jnp.zeros((E, EH1), jnp.float32), 'eW2': jax.random.normal(ks[5], (E, EH1, EH2), jnp.float32) * s, 'eb2': jnp.zeros((E, EH2), jnp.float32), 'eW3': jax.random.normal(ks[6], (E, EH2, OUT), jnp.float32) * s, 'eb3': jnp.zeros((E, OUT), jnp.float32), 'gW': jax.random.normal(ks[7], (IN, E), jnp.float32) * s, 'gb': jnp.zeros((E,), jnp.float32)}
    _L1_ffn_all = _L1_ffn_setup()
    _L1_ffn_in = {k: v for k, v in _L1_ffn_all.items() if k in ('sW1', 'sb1', 'sW2', 'sb2', 'sW3', 'sb3', 'eW1', 'eb1', 'eW2', 'eb2', 'eW3', 'eb3', 'gW', 'gb')}
    del _L1_ffn_all

    def _L2_gnn_setup():
        import jax, jax.numpy as jnp
        import numpy as np
        N_NODES = 3125
        N_EDGES = 50000
        D_IN = 256
        D_OUT = 256
        key = jax.random.key(seed)
        k1, k2, k3, k4 = jax.random.split(key, 4)
        x = jax.random.normal(k1, (N_NODES, D_IN), dtype=jnp.float32)
        edge_index = jax.random.randint(k2, (2, N_EDGES), 0, N_NODES, dtype=jnp.int64)
        W = jax.random.normal(k3, (D_OUT, D_IN), dtype=jnp.float32) * (1.0 / np.sqrt(D_IN))
        b = jax.random.normal(k4, (D_OUT,), dtype=jnp.float32) * 0.01
        return {'x': x, 'edge_index': edge_index, 'W': W, 'b': b}
    _L2_gnn_all = _L2_gnn_setup()
    _L2_gnn_in = {k: v for k, v in _L2_gnn_all.items() if k in ('W', 'b')}
    del _L2_gnn_all

    def _L2_ffn_setup():
        import jax, jax.numpy as jnp
        import numpy as np
        NUM_EXPERTS = 8
        TOP_K = 2
        B, S, D = (8, 256, 256)

        def _moe(tokens, router_w, w1, b1, w2, b2):
            N = tokens.shape[0]
            E = router_w.shape[0]
            logits = tokens.astype(jnp.float32) @ router_w.astype(jnp.float32).T
            probs = jax.nn.softmax(logits, axis=-1)
            rw, re = jax.lax.top_k(probs, TOP_K)
            if TOP_K > 1:
                rw = rw / jnp.maximum(rw.sum(-1, keepdims=True), 1e-12)
            rw = rw.astype(tokens.dtype)
            combine = jnp.zeros((N, E), tokens.dtype).at[jnp.arange(N)[:, None], re].set(rw)
            out = tokens
            for e in range(E):
                h = jax.nn.gelu(tokens @ w1[e] + b1[e], approximate=False)
                y = h @ w2[e] + b2[e]
                out = out + combine[:, e:e + 1] * y
            return out
        key = jax.random.key(seed)
        ks = jax.random.split(key, 4)
        scale = 1.0 / np.sqrt(D).astype(np.float32)
        return {'input_embeddings': jax.random.normal(ks[0], (B, S, D), jnp.float32), 'router_w': jax.random.normal(ks[1], (NUM_EXPERTS, D), jnp.float32) * scale, 'w1': jax.random.normal(ks[2], (NUM_EXPERTS, D, D), jnp.float32) * scale, 'b1': jnp.zeros((NUM_EXPERTS, D), jnp.float32), 'w2': jax.random.normal(ks[3], (NUM_EXPERTS, D, D), jnp.float32) * scale, 'b2': jnp.zeros((NUM_EXPERTS, D), jnp.float32)}
    _L2_ffn_all = _L2_ffn_setup()
    _L2_ffn_in = {k: v for k, v in _L2_ffn_all.items() if k in ('router_w', 'w1', 'b1', 'w2', 'b2')}
    del _L2_ffn_all

    def _L3_gnn_setup():
        import jax, jax.numpy as jnp
        import numpy as np
        N_NODES = 3125
        F_DIM = 256
        NNZ = 50000

        def _prelu(x, a):
            return jnp.where(x >= 0, x, a * x)

        def _hconv(x, W, b, src, dst, n):
            xt = x @ W
            ones = jnp.ones(src.shape, xt.dtype)
            D = jax.ops.segment_sum(ones, src, num_segments=n)
            B = jax.ops.segment_sum(ones, dst, num_segments=n)
            Dinv = jnp.where(D > 0, 1.0 / D, 0.0)
            Binv = jnp.where(B > 0, 1.0 / B, 0.0)
            m = jax.ops.segment_sum(xt[src], dst, num_segments=n) * Binv[:, None]
            out = jax.ops.segment_sum(m[dst], src, num_segments=n) * Dinv[:, None]
            return out + b
        key = jax.random.key(seed)
        k0, k1, k2, k3 = jax.random.split(key, 4)
        x = jax.random.normal(k0, (N_NODES, F_DIM), dtype=jnp.float32)
        edge_index = jax.random.randint(k1, (2, NNZ), 0, N_NODES, dtype=jnp.int32)
        scale = (2.0 / F_DIM) ** 0.5
        W1 = jax.random.normal(k2, (F_DIM, F_DIM), dtype=jnp.float32) * scale
        W2 = jax.random.normal(k3, (F_DIM, F_DIM), dtype=jnp.float32) * scale
        b1 = jnp.zeros((F_DIM,), jnp.float32)
        b2 = jnp.zeros((F_DIM,), jnp.float32)
        a = jnp.full((1,), 0.25, jnp.float32)
        return {'x': x, 'edge_index': edge_index, 'W1': W1, 'b1': b1, 'W2': W2, 'b2': b2, 'a': a}
    _L3_gnn_all = _L3_gnn_setup()
    _L3_gnn_in = {k: v for k, v in _L3_gnn_all.items() if k in ('W1', 'b1', 'W2', 'b2', 'a')}
    del _L3_gnn_all

    def _L3_ffn_setup():
        import jax, jax.numpy as jnp
        import numpy as np
        B, S, D = (8, 128, 256)
        H = 4 * D
        CAPACITY = 0.5
        key = jax.random.key(seed)
        ks = jax.random.split(key, 6)
        x = jax.random.normal(ks[0], (B, S, D), dtype=jnp.float32)
        attention_mask = jnp.zeros((B, 1, 1, S), dtype=jnp.float32)
        wr = jax.random.normal(ks[1], (D, 1), dtype=jnp.float32) * 0.02
        br = jnp.zeros((1,), dtype=jnp.float32)
        w1 = jax.random.normal(ks[2], (D, H), dtype=jnp.float32) * 0.02
        b1 = jnp.zeros((H,), dtype=jnp.float32)
        w2 = jax.random.normal(ks[3], (H, D), dtype=jnp.float32) * 0.02
        b2 = jnp.zeros((D,), dtype=jnp.float32)
        return {'x': x, 'attention_mask': attention_mask, 'wr': wr, 'br': br, 'w1': w1, 'b1': b1, 'w2': w2, 'b2': b2}
    _L3_ffn_all = _L3_ffn_setup()
    _L3_ffn_in = {k: v for k, v in _L3_ffn_all.items() if k in ('attention_mask', 'wr', 'br', 'w1', 'b1', 'w2', 'b2')}
    del _L3_ffn_all
    return {'x': x, 'src': src, 'dst': dst, 'edge_type_7': edge_type_7, 'edge_weight': edge_weight, 'L0_gnn_W': _L0_gnn_in['W'], 'L0_gnn_a_src': _L0_gnn_in['a_src'], 'L0_gnn_a_dst': _L0_gnn_in['a_dst'], 'L0_ffn_router_w': _L0_ffn_in['router_w'], 'L0_ffn_router_b': _L0_ffn_in['router_b'], 'L0_ffn_W1': _L0_ffn_in['W1'], 'L0_ffn_b1': _L0_ffn_in['b1'], 'L0_ffn_W2': _L0_ffn_in['W2'], 'L0_ffn_b2': _L0_ffn_in['b2'], 'L1_gnn_weights': _L1_gnn_in['weights'], 'L1_ffn_sW1': _L1_ffn_in['sW1'], 'L1_ffn_sb1': _L1_ffn_in['sb1'], 'L1_ffn_sW2': _L1_ffn_in['sW2'], 'L1_ffn_sb2': _L1_ffn_in['sb2'], 'L1_ffn_sW3': _L1_ffn_in['sW3'], 'L1_ffn_sb3': _L1_ffn_in['sb3'], 'L1_ffn_eW1': _L1_ffn_in['eW1'], 'L1_ffn_eb1': _L1_ffn_in['eb1'], 'L1_ffn_eW2': _L1_ffn_in['eW2'], 'L1_ffn_eb2': _L1_ffn_in['eb2'], 'L1_ffn_eW3': _L1_ffn_in['eW3'], 'L1_ffn_eb3': _L1_ffn_in['eb3'], 'L1_ffn_gW': _L1_ffn_in['gW'], 'L1_ffn_gb': _L1_ffn_in['gb'], 'L2_gnn_W': _L2_gnn_in['W'], 'L2_gnn_b': _L2_gnn_in['b'], 'L2_ffn_router_w': _L2_ffn_in['router_w'], 'L2_ffn_w1': _L2_ffn_in['w1'], 'L2_ffn_b1': _L2_ffn_in['b1'], 'L2_ffn_w2': _L2_ffn_in['w2'], 'L2_ffn_b2': _L2_ffn_in['b2'], 'L3_gnn_W1': _L3_gnn_in['W1'], 'L3_gnn_b1': _L3_gnn_in['b1'], 'L3_gnn_W2': _L3_gnn_in['W2'], 'L3_gnn_b2': _L3_gnn_in['b2'], 'L3_gnn_a': _L3_gnn_in['a'], 'L3_ffn_attention_mask': _L3_ffn_in['attention_mask'], 'L3_ffn_wr': _L3_ffn_in['wr'], 'L3_ffn_br': _L3_ffn_in['br'], 'L3_ffn_w1': _L3_ffn_in['w1'], 'L3_ffn_b1': _L3_ffn_in['b1'], 'L3_ffn_w2': _L3_ffn_in['w2'], 'L3_ffn_b2': _L3_ffn_in['b2']}

def reference(x, src, dst, edge_type_7, edge_weight, L0_gnn_W, L0_gnn_a_src, L0_gnn_a_dst, L0_ffn_router_w, L0_ffn_router_b, L0_ffn_W1, L0_ffn_b1, L0_ffn_W2, L0_ffn_b2, L1_gnn_weights, L1_ffn_sW1, L1_ffn_sb1, L1_ffn_sW2, L1_ffn_sb2, L1_ffn_sW3, L1_ffn_sb3, L1_ffn_eW1, L1_ffn_eb1, L1_ffn_eW2, L1_ffn_eb2, L1_ffn_eW3, L1_ffn_eb3, L1_ffn_gW, L1_ffn_gb, L2_gnn_W, L2_gnn_b, L2_ffn_router_w, L2_ffn_w1, L2_ffn_b1, L2_ffn_w2, L2_ffn_b2, L3_gnn_W1, L3_gnn_b1, L3_gnn_W2, L3_gnn_b2, L3_gnn_a, L3_ffn_attention_mask, L3_ffn_wr, L3_ffn_br, L3_ffn_w1, L3_ffn_b1, L3_ffn_w2, L3_ffn_b2):
    import jax
    import jax.numpy as jnp

    def _L0_gnn_ref(x, edge_index, edge_weight, W, a_src, a_dst):
        import jax, jax.numpy as jnp
        import numpy as np
        N_NODES = 50000
        N_EDGES = 25000
        IN_F = 256
        OUT_F = 64
        HEADS = 4
        NEG_SLOPE = 0.2
        num_nodes = x.shape[0]
        h = jnp.einsum('ni,hio->hno', x, W)
        attn_src = jnp.einsum('hno,hod->hn', h, a_src)
        attn_dst = jnp.einsum('hno,hod->hn', h, a_dst)
        src_idx, dst_idx = (edge_index[0], edge_index[1])
        e = attn_src[:, src_idx] + attn_dst[:, dst_idx]
        e = jnp.where(e >= 0, e, NEG_SLOPE * e)
        e = e * edge_weight[None, :]
        e_exp = jnp.exp(e - jnp.max(e))
        denom = jax.ops.segment_sum(e_exp.T, dst_idx, num_segments=num_nodes).T
        alpha = e_exp / (denom[:, dst_idx] + 1e-10)
        msg = h[:, src_idx] * alpha[..., None]
        out = jax.vmap(lambda m: jax.ops.segment_sum(m, dst_idx, num_segments=num_nodes))(msg)
        return jnp.transpose(out, (1, 0, 2)).reshape(num_nodes, HEADS * OUT_F)

    def _L0_ffn_ref(x, router_w, router_b, W1, b1, W2, b2):
        import jax, jax.numpy as jnp
        import numpy as np
        B, K, D = (512, 16, 256)
        E = 32
        H = int(D * 0.25)
        xf = x.reshape(-1, D)
        logits = xf @ router_w.T + router_b
        idx = jnp.argmax(logits, axis=-1)
        w1t = jnp.take(W1, idx, axis=0)
        h = jnp.einsum('nd,ndh->nh', xf, w1t) + jnp.take(b1, idx, axis=0)
        h = jax.nn.relu(h)
        w2t = jnp.take(W2, idx, axis=0)
        out = jnp.einsum('nh,nhd->nd', h, w2t) + jnp.take(b2, idx, axis=0)
        out = jax.nn.relu(out)
        return out.reshape(x.shape)

    def _L1_gnn_ref(x, edge_index, edge_type, weights):
        import jax, jax.numpy as jnp
        import numpy as np
        N_EDGE_TYPE = 7
        N, C = x.shape
        row, col = (edge_index[0], edge_index[1])
        index = row * N_EDGE_TYPE + edge_type
        num_segments = N * N_EDGE_TYPE
        gathered = x[col]
        sums = jax.ops.segment_sum(gathered, index, num_segments=num_segments)
        cnt = jax.ops.segment_sum(jnp.ones((index.shape[0],), dtype=x.dtype), index, num_segments=num_segments)
        col_data = sums / jnp.maximum(cnt, 1.0)[:, None]
        out = col_data.reshape(N, N_EDGE_TYPE * C) @ weights
        return out

    def _L1_ffn_ref(x, sW1, sb1, sW2, sb2, sW3, sb3, eW1, eb1, eW2, eb2, eW3, eb3, gW, gb):
        import jax, jax.numpy as jnp
        import numpy as np
        B, A = (128, 8)
        IN, OUT = (256, 256)
        SH1, SH2 = (256, 128)
        EH1, EH2 = (128, 64)
        E, TOPK = (4, 2)

        def _shared_mlp(x, W1, b1, W2, b2, W3, b3):
            h = jax.nn.relu(x @ W1 + b1)
            h = jax.nn.relu(h @ W2 + b2)
            return h @ W3 + b3

        def _experts_mlp(x, eW1, eb1, eW2, eb2, eW3, eb3):
            h = jax.nn.relu(jnp.einsum('baf,efh->ebah', x, eW1) + eb1[:, None, None, :])
            h = jax.nn.relu(jnp.einsum('ebah,ehg->ebag', h, eW2) + eb2[:, None, None, :])
            o = jnp.einsum('ebag,ego->ebao', h, eW3) + eb3[:, None, None, :]
            return jnp.moveaxis(o, 0, -1)
        all_out = _experts_mlp(x, eW1, eb1, eW2, eb2, eW3, eb3)
        shared = _shared_mlp(x, sW1, sb1, sW2, sb2, sW3, sb3)
        gates = jax.nn.softmax(x @ gW + gb, axis=-1)
        topv, topi = jax.lax.top_k(gates, TOPK)
        topw = jax.nn.softmax(topv, axis=-1)
        sel = jnp.take_along_axis(all_out, topi[:, :, None, :], axis=-1)
        gated = jnp.sum(sel * topw[:, :, None, :], axis=-1)
        return shared + gated

    def _L2_gnn_ref(x, edge_index, W, b):
        import jax, jax.numpy as jnp
        import numpy as np
        N_NODES = 3125
        N_EDGES = 50000
        D_IN = 256
        D_OUT = 256
        h = jnp.einsum('nd,od->no', x, W) + b
        row, col = (edge_index[0], edge_index[1])
        msgs = h[col]
        out = jax.ops.segment_sum(msgs, row, num_segments=h.shape[0])
        return out

    def _L2_ffn_ref(input_embeddings, router_w, w1, b1, w2, b2):
        import jax, jax.numpy as jnp
        import numpy as np
        NUM_EXPERTS = 8
        TOP_K = 2
        B, S, D = (8, 256, 256)

        def _moe(tokens, router_w, w1, b1, w2, b2):
            N = tokens.shape[0]
            E = router_w.shape[0]
            logits = tokens.astype(jnp.float32) @ router_w.astype(jnp.float32).T
            probs = jax.nn.softmax(logits, axis=-1)
            rw, re = jax.lax.top_k(probs, TOP_K)
            if TOP_K > 1:
                rw = rw / jnp.maximum(rw.sum(-1, keepdims=True), 1e-12)
            rw = rw.astype(tokens.dtype)
            combine = jnp.zeros((N, E), tokens.dtype).at[jnp.arange(N)[:, None], re].set(rw)
            out = tokens
            for e in range(E):
                h = jax.nn.gelu(tokens @ w1[e] + b1[e], approximate=False)
                y = h @ w2[e] + b2[e]
                out = out + combine[:, e:e + 1] * y
            return out
        b, s, d = input_embeddings.shape
        tokens = input_embeddings.reshape(b * s, d)
        return _moe(tokens, router_w, w1, b1, w2, b2).reshape(b, s, d)

    def _L3_gnn_ref(x, edge_index, W1, b1, W2, b2, a):
        import jax, jax.numpy as jnp
        import numpy as np
        N_NODES = 3125
        F_DIM = 256
        NNZ = 50000

        def _prelu(x, a):
            return jnp.where(x >= 0, x, a * x)

        def _hconv(x, W, b, src, dst, n):
            xt = x @ W
            ones = jnp.ones(src.shape, xt.dtype)
            D = jax.ops.segment_sum(ones, src, num_segments=n)
            B = jax.ops.segment_sum(ones, dst, num_segments=n)
            Dinv = jnp.where(D > 0, 1.0 / D, 0.0)
            Binv = jnp.where(B > 0, 1.0 / B, 0.0)
            m = jax.ops.segment_sum(xt[src], dst, num_segments=n) * Binv[:, None]
            out = jax.ops.segment_sum(m[dst], src, num_segments=n) * Dinv[:, None]
            return out + b
        src, dst = (edge_index[0], edge_index[1])
        n = x.shape[0]
        h = _prelu(_hconv(x, W1, b1, src, dst, n), a)
        h = _hconv(h, W2, b2, src, dst, n) + x
        return _prelu(h, a)

    def _L3_ffn_ref(x, attention_mask, wr, br, w1, b1, w2, b2):
        import jax, jax.numpy as jnp
        import numpy as np
        B, S, D = (8, 128, 256)
        H = 4 * D
        CAPACITY = 0.5
        b, s, d = x.shape
        weights = (jnp.einsum('bsd,do->bso', x, wr) + br)[..., 0]
        k = max(1, int(CAPACITY * s))
        kk = k - 1 if k > 1 else 1
        _, idx = jax.lax.top_k(weights, k)
        sel_idx = idx[:, :kk]
        sel = jnp.take_along_axis(x, sel_idx[:, :, None], axis=1)
        h = jax.nn.gelu(jnp.einsum('bkd,dh->bkh', sel, w1) + b1)
        y = jnp.einsum('bkh,hd->bkd', h, w2) + b2
        w_sel = jnp.take_along_axis(weights, sel_idx, axis=1)
        y = y * w_sel[..., None]
        batch_idx = jnp.arange(b)[:, None]
        processed = jnp.zeros_like(x).at[batch_idx, sel_idx].set(y)
        return processed + x
    edge_index = jnp.stack([src, dst])
    x = x + _L0_gnn_ref(_layernorm(x, axis=-1), edge_index, edge_weight, L0_gnn_W, L0_gnn_a_src, L0_gnn_a_dst)
    x = x + _L0_ffn_ref(_layernorm(x, axis=-1)[None], L0_ffn_router_w, L0_ffn_router_b, L0_ffn_W1, L0_ffn_b1, L0_ffn_W2, L0_ffn_b2)[0]
    x = x + _L1_gnn_ref(_layernorm(x, axis=-1), edge_index, edge_type_7, L1_gnn_weights)
    x = x + _L1_ffn_ref(_layernorm(x, axis=-1)[None], L1_ffn_sW1, L1_ffn_sb1, L1_ffn_sW2, L1_ffn_sb2, L1_ffn_sW3, L1_ffn_sb3, L1_ffn_eW1, L1_ffn_eb1, L1_ffn_eW2, L1_ffn_eb2, L1_ffn_eW3, L1_ffn_eb3, L1_ffn_gW, L1_ffn_gb)[0]
    x = x + _L2_gnn_ref(_layernorm(x, axis=-1), edge_index, L2_gnn_W, L2_gnn_b)
    x = x + _L2_ffn_ref(_layernorm(x, axis=-1)[None], L2_ffn_router_w, L2_ffn_w1, L2_ffn_b1, L2_ffn_w2, L2_ffn_b2)[0]
    x = x + _L3_gnn_ref(_layernorm(x, axis=-1), edge_index, L3_gnn_W1, L3_gnn_b1, L3_gnn_W2, L3_gnn_b2, L3_gnn_a)
    x = x + _L3_ffn_ref(_layernorm(x, axis=-1)[None], L3_ffn_attention_mask, L3_ffn_wr, L3_ffn_br, L3_ffn_w1, L3_ffn_b1, L3_ffn_w2, L3_ffn_b2)[0]
    return x

_drawn_inputs = setup_inputs


def setup_inputs(seed=0):
    import zlib

    import numpy as np

    out = dict(_drawn_inputs(seed))
    spreads = {'L1_ffn_sb1': (0.0, 0.31),
     'L1_ffn_sb2': (0.0, 0.1),
     'L1_ffn_sb3': (0.0, 0.1),
     'L1_ffn_eb1': (0.0, 0.8),
     'L1_ffn_eb2': (0.0, 0.37),
     'L1_ffn_eb3': (0.0, 0.1),
     'L1_ffn_gb': (0.0, 0.586),
     'L2_ffn_b1': (0.0, 0.8),
     'L2_ffn_b2': (0.0, 0.716),
     'L3_gnn_b1': (0.0, 0.71),
     'L3_gnn_b2': (0.0, 0.8),
     'L3_ffn_b1': (0.0, 0.8),
     'L3_ffn_b2': (0.0, 0.8)}
    factors = {'L0_ffn_b1': 8.0, 'L0_ffn_b2': 3.479, 'L3_ffn_wr': 8.0, 'L3_ffn_w1': 8.0, 'L3_ffn_w2': 8.0}
    for name, (base, spread) in spreads.items():
        noise = np.random.default_rng([zlib.crc32(name.encode()), seed]).standard_normal(out[name].shape)
        drawn = base * np.exp(spread * noise) if base else spread * noise
        out[name] = jnp.asarray(drawn.astype(out[name].dtype))
    for name, factor in factors.items():
        out[name] = (out[name] * factor).astype(out[name].dtype)
    return out
```

```python
from contextlib import ExitStack

import numpy as np
import concourse.bass as bass
from concourse import mybir

F32 = mybir.dt.float32
I32 = mybir.dt.int32
U32 = mybir.dt.uint32
ALU = mybir.AluOpType
ACT = mybir.ActivationFunctionType
AX = mybir.AxisListType

P = 128
N = 3125
D = 256
NT = -(-N // P)
NP_ = NT * P
NTAIL = N - (NT - 1) * P
KC = D // P
E = 53125
EC = 416
EFULL = E // EC
ETAIL = E - EFULL * EC
HALF = 10
GROUP = 2 * HALF
TILES = -(-((E + NT * (P - 1)) // P) // GROUP) * GROUP
STEPS = TILES // GROUP
COLS = TILES + 16
NF = 8
F_OTHER, F_TYPED, F_LOCAL, F_WEIGHT, F_TYPE = range(5)
NTYPE = 7
HEADS = 4
HD = D // HEADS
TW = D + HEADS
PADKEY = NP_
LOWEST = -1.0e30
SCB = 16
SCL = EC // (2 * SCB)

C_ID, C_IOTA, C_TRI, C_ONES, C_TILE = 0, P, 2 * P, 3 * P, 4 * P
C_SEL0 = C_TILE + COLS
C_SEL1 = C_SEL0 + 16 * P
C_SEL2 = C_SEL1 + 2 * P
C_END = C_SEL2 + 16 * P


def ds(a, n):
    return bass.ds(a, n)


def peeled(engine, count, body):
    body(0)
    with engine.Fori(1, count) as i:
        body(i)


def by_parity(engine, body):
    with engine.Fori(0, NT // 2) as i:
        for h in range(2):
            body(i * 2 + h, h)
    if NT % 2:
        body(NT - 1, 0)


def wait(engine, semaphore, value):
    if not (isinstance(value, int) and value <= 0):
        engine.wait_ge(semaphore, value)


class Kit:

    def __init__(self, nc, ctx):
        self.nc, self.ctx, self.n = nc, ctx, 0
        self.stage_sems = []

    def sem(self, name):
        self.n += 1
        self.stage_sems.append(self.nc.alloc_semaphore(name=f"{name}_{self.n}"))
        return self.stage_sems[-1]

    def dma_sem(self, name):
        self.n += 1
        return self.ctx.enter_context(self.nc.semaphore(f"{name}_{self.n}"))

    def end_stage(self):
        self.nc.all_engine_barrier()
        self.nc.clear_and_free_semaphores(self.stage_sems)
        self.nc.all_engine_barrier()
        self.stage_sems = []

    def dram(self, name, shape, dt=F32):
        return self.nc.dram_tensor(name, shape, dt).ap()


def tensors(nc, ctx):
    mark = nc.next_id() if callable(nc.next_id) else nc.next_id

    def sb(name, shape, dt=F32):
        return ctx.enter_context(nc.sbuf_tensor(f"{name}_{mark}", shape, dt))

    def ps(name, shape, dt=F32):
        return ctx.enter_context(nc.psum_tensor(f"{name}_{mark}", shape, dt))
    return sb, ps


def load_state(k, A):
    loaded, zeroed = k.dma_sem("loaded"), k.sem("zeroed")
    with k.nc.Block() as block:
        @block.vector
        def _(dve):
            dve.memset(k.x[:, NT - 1:NT, :], 0.0)
            dve.memset(k.yT[:, :, NP_:], 0.0).then_inc(zeroed, 1)

        @block.sync
        def _(sp):
            sp.dma_start(k.const[:], A["consts"]).then_inc(loaded, 16)
            sp.dma_start(k.x[:, 0:NT - 1, :],
                         A["x"][0:(NT - 1) * P, :].rearrange("(t p) d -> p t d", p=P)).then_inc(loaded, 16)
            sp.wait_ge(zeroed, 1)
            sp.dma_start(k.x[0:NTAIL, NT - 1, :], A["x"][(NT - 1) * P:N, :]).then_inc(loaded, 16)
            sp.wait_ge(loaded, 48)


def sort_edges(k, A, key, other, slots, meta, btile, tag):
    nc = k.nc
    filled, tot, pref, placed = (k.sem(f"sort_{s}_{tag}") for s in ("filled", "totals", "prefix", "placed"))
    staged = [k.sem(f"staged{h}_{tag}") for h in range(2)]
    scattered = [k.dma_sem(f"scattered{h}_{tag}") for h in range(2)]
    loaded, blank, back = (k.dma_sem(f"sort_{s}_{tag}") for s in ("loaded", "blank", "back"))
    gate = k.sem(f"gate_{tag}")
    NB = NT + 1
    with ExitStack() as ctx:
        sb, ps = tensors(nc, ctx)
        raw = sb("raw", [P, 4, EC], I32)
        pay = sb("pay", [P, EC, NF], I32)
        bint = sb("bint", [P, EC], I32)
        bucket = sb("bucket", [P, EC])
        one = sb("one", [P, EC])
        mask = sb("mask", [P, EC])
        incl = sb("incl", [P, EC])
        within = sb("within", [P, EC])
        rowi = sb("rowi", [P, EC], I32)
        coli = sb("coli", [P, EC], I32)
        total = sb("total", [P, NB])
        cnti = sb("cnti", [P, NB], I32)
        ntile = sb("ntile", [P, NB])
        tincl = sb("tincl", [P, NB])
        start = sb("start", [P, NB])
        base = sb("base", [P, NB])
        bt = sb("bt", [P, COLS])
        stage = [sb(f"stage{h}", [P, SCB, NF], I32) for h in range(2)]
        sidx = [sb(f"sidx{h}", [P, SCB], I32) for h in range(2)]
        psx = ps("psx", [P, 2, NB])
        payf = pay[:].bitcast(F32)
        metai = meta[:]
        with nc.Block() as block:
            @block.sync
            def _(sp):
                sp.wait_ge(filled, 1)
                sp.dma_start(slots.rearrange("(p c) f -> p c f", p=P), metai).then_inc(blank, 16)
                sp.wait_ge(filled, 2)
                for i, a in enumerate((key, other, A["etype"], A["eweight"])):
                    sp.dma_start(raw[0:EFULL, i, :], a[0:EFULL * EC].rearrange("(p c) -> p c", c=EC)).then_inc(loaded, 16)
                    sp.dma_start(raw[EFULL:EFULL + 1, i, 0:ETAIL],
                                 a[EFULL * EC:E].rearrange("(p c) -> p c", p=1)).then_inc(loaded, 16)
                sp.wait_ge(scattered[0], 16 * SCB * SCL)
                sp.wait_ge(scattered[1], 16 * SCB * SCL)
                sp.dma_start(metai, slots.rearrange("(p c) f -> p c f", p=P)).then_inc(back, 16)
                sp.wait_ge(back, 16)

            @block.tensor
            def _(pe):
                pe.wait_ge(tot, 1)
                pe.matmul(psx[:, 0, :], k.tri, total[:], start=True, stop=True)
                pe.matmul(psx[:, 1, :], k.ones, total[:], start=True, stop=True).then_inc(pref, 1)

            @block.vector
            def _(dve):
                dve.memset(metai, 0)
                dve.drain()
                dve.memset(metai.bitcast(F32)[:, :, F_LOCAL:F_LOCAL + 1], -1.0)
                dve.memset(raw[:], 0)
                dve.memset(within[:], -1.0)
                dve.memset(one[:], 1.0)
                dve.memset(pay[:], 0)
                dve.memset(bt[:], 0.0)
                dve.drain().then_inc(filled, 1)
                dve.memset(raw[:, 0, :], PADKEY).then_inc(filled, 1)
                dve.wait_ge(loaded, 128)
                dve.tensor_scalar(bint[:], raw[:, 0, :], 7, None, ALU.arith_shift_right)
                dve.tensor_scalar(coli[:], raw[:, 0, :], P - 1, None, ALU.bitwise_and)
                dve.tensor_copy(pay[:, :, F_OTHER], raw[:, 1, :])
                dve.scalar_tensor_tensor(out=pay[:, :, F_TYPED], in0=raw[:, 1, :], scalar=float(NTYPE),
                                         in1=raw[:, 2, :], op0=ALU.mult, op1=ALU.add)
                dve.tensor_copy(payf[:, :, F_TYPE], raw[:, 2, :])
                dve.tensor_copy(pay[:, :, F_WEIGHT], raw[:, 3, :])
                dve.drain()
                dve.tensor_copy(bucket[:], bint[:])
                dve.drain()
                dve.tensor_scalar(mask[:], bucket[:], float(NT), float(-P), ALU.is_equal, ALU.mult)
                dve.drain()
                dve.tensor_tensor(payf[:, :, F_LOCAL], mask[:], coli[:], ALU.add)
                dve.drain()
                with dve.Fori(0, NB) as b:
                    dve.tensor_scalar(mask[:], bucket[:], k.iota[:, ds(b, 1)], None, ALU.is_equal)
                    dve.drain()
                    dve.tensor_tensor_scan(incl[:], one[:], mask[:], 0.0, ALU.mult, ALU.add)
                    dve.drain()
                    dve.tensor_copy(total[:, ds(b, 1)], incl[:, EC - 1:EC])
                    dve.tensor_tensor(mask[:], mask[:], incl[:], ALU.mult)
                    dve.drain()
                    dve.tensor_tensor(within[:], within[:], mask[:], ALU.add)
                    dve.drain()
                dve.drain().then_inc(tot, 1)
                dve.wait_ge(pref, 1)
                dve.tensor_scalar(cnti[:], psx[:, 1, :], float(P - 1), None, ALU.add)
                dve.drain()
                dve.tensor_scalar(cnti[:], cnti[:], 7, None, ALU.arith_shift_right)
                dve.drain()
                dve.tensor_scalar(ntile[:], cnti[:], 1.0, None, ALU.max)
                dve.drain()
                dve.tensor_tensor_scan(tincl[:], one[:, 0:NB], ntile[:], 0.0, ALU.mult, ALU.add)
                dve.drain()
                dve.tensor_tensor(start[:], tincl[:], ntile[:], ALU.subtract)
                dve.drain()
                dve.scalar_tensor_tensor(out=base[:], in0=start[:], scalar=float(P), in1=psx[:, 0, :],
                                         op0=ALU.mult, op1=ALU.add)
                dve.drain()
                with dve.Fori(0, NB) as b:
                    dve.tensor_scalar(mask[:], bucket[:], k.iota[:, ds(b, 1)], base[:, ds(b, 1)],
                                      ALU.is_equal, ALU.mult)
                    dve.drain()
                    dve.tensor_tensor(within[:], within[:], mask[:], ALU.add)
                    dve.drain()
                dve.tensor_copy(bint[:], within[:])
                dve.drain()
                dve.tensor_scalar(rowi[:], bint[:], P - 1, None, ALU.bitwise_and)
                dve.tensor_scalar(coli[:], bint[:], 7, None, ALU.arith_shift_right)
                dve.drain()
                dve.scalar_tensor_tensor(out=rowi[:], in0=rowi[:], scalar=float(COLS), in1=coli[:],
                                         op0=ALU.mult, op1=ALU.add)
                dve.drain()
                dve.wait_ge(blank, 16)
                dve.sem_inc(placed, 1)

                def stage_columns(i):
                    for h in range(2):
                        c = i * (2 * SCB) + h * SCB
                        wait(dve, scattered[h], i * (16 * SCB))
                        dve.tensor_copy(stage[h][:], pay[:, ds(c, SCB), :])
                        dve.tensor_copy(sidx[h][:], rowi[:, ds(c, SCB)])
                        dve.drain().then_inc(staged[h], 1)
                peeled(dve, SCL, stage_columns)
                with dve.Fori(1, NT) as b:
                    dve.scalar_tensor_tensor(out=bt[:], in0=k.tile_iota, scalar=start[:, ds(b, 1)], in1=bt[:],
                                             op0=ALU.is_ge, op1=ALU.add)
                    dve.drain()
                dve.tensor_copy(btile[:], bt[0:1, :])

            @block.gpsimd
            def _(pool):
                pool.wait_ge(placed, 1)
                with pool.Fori(0, SCL) as i:
                    for h in range(2):
                        pool.wait_ge(staged[h], i + 1)
                        pool.sem_inc(gate, 1)
                        for c in range(SCB):
                            pool.indirect_dma_start(
                                out=slots, out_offset=bass.IndirectOffsetOnAxis(ap=sidx[h][:, c:c + 1], axis=0),
                                in_=stage[h][:, c, :], in_offset=None).then_inc(scattered[h], 16)


def layer_norm(k):
    nc = k.nc
    norm, turned, taken = k.sem("ln_norm"), k.sem("ln_turned"), k.sem("ln_taken")
    var, root, moved = k.sem("ln_var"), k.sem("ln_root"), k.sem("ln_moved")
    with ExitStack() as ctx:
        sb, ps = tensors(nc, ctx)
        stats = sb("stats", [P, NT, 6])
        aggr = sb("aggr", [P, NT, 2])
        rstd = sb("rstd", [P, NT])
        pst = ps("pst", [P, 2, 4, P])
        tile = [sb(f"tile{h}", [P, 1, D]) for h in range(2)]
        with nc.Block() as block:
            @block.vector
            def _(dve):
                with dve.Fori(0, NT) as t:
                    dve.bn_stats(stats[:, ds(t, 1), :], k.x[:, ds(t, 1), :])
                dve.drain()
                dve.tensor_tensor(aggr[:, :, 0], stats[:, :, 1], stats[:, :, 4], ALU.add)
                dve.tensor_tensor(aggr[:, :, 1], stats[:, :, 1], stats[:, :, 4], ALU.subtract)
                dve.tensor_tensor(rstd[:], stats[:, :, 2], stats[:, :, 5], ALU.add)
                dve.drain()
                dve.tensor_scalar(aggr[:, :, 0], aggr[:, :, 0], 0.5, None, ALU.mult)
                dve.scalar_tensor_tensor(out=aggr[:, :, 1], in0=aggr[:, :, 1], scalar=0.25, in1=aggr[:, :, 1],
                                         op0=ALU.mult, op1=ALU.mult)
                dve.drain()
                dve.scalar_tensor_tensor(out=rstd[:], in0=rstd[:], scalar=1.0 / D, in1=aggr[:, :, 1],
                                         op0=ALU.mult, op1=ALU.add)
                dve.drain()
                dve.tensor_scalar(rstd[:], rstd[:], 1e-5, None, ALU.add).then_inc(var, 1)
                dve.wait_ge(root, 1)
                dve.reciprocal(rstd[:], rstd[:])
                dve.drain()

                def normalize(t, h):
                    dve.wait_ge(turned, t + 1)
                    dve.wait_ge(moved, t + 1)
                    dve.tensor_scalar(tile[h][:], k.x[:, ds(t, 1), :], aggr[:, ds(t, 1), 0:1],
                                      rstd[:, ds(t, 1)], ALU.subtract, ALU.mult).then_inc(norm, 1)
                by_parity(dve, normalize)

            @block.gpsimd
            def _(pool):
                pool.sem_inc(moved, 2)

                def move(t, h):
                    pool.wait_ge(norm, t + 1)
                    pool.tensor_copy(k.y[:, ds(t, 1), :], tile[h][:]).then_inc(moved, 1)
                by_parity(pool, move)

            @block.tensor
            def _(pe):
                turn_loop(k, pe, tile, pst, norm, turned, taken)

            @block.scalar
            def _(act):
                act.wait_ge(var, 1)
                act.activation(rstd[:], rstd[:], ACT.Sqrt).then_inc(root, 1)
                take_loop(k, act, pst, turned, taken)


def turn_loop(k, pe, src, pst, ready, turned, taken):
    pe.sem_inc(turned, 2)

    def turn(t, h):
        pe.wait_ge(ready, t + 1)
        pe.wait_ge(taken, t + 1)
        for c in range(KC):
            mm = pe.transpose(pst[:, h, c, :], src[h][:, 0, c * P:(c + 1) * P], k.ident)
        mm.then_inc(turned, 1)
    by_parity(pe, turn)


def take_loop(k, act, pst, turned, taken):
    act.sem_inc(taken, 2)

    def take(t, h):
        act.wait_ge(turned, t + 3)
        act.activation(k.yT[:, :, ds(t * P, P)], pst[:, h, 0:KC, :], ACT.Copy).then_inc(taken, 1)
    by_parity(act, take)


def stage_yT(k, act, yt, kept, moved):
    for t in range(2):
        act.activation(yt[t][:], k.yT[:, :, t * P:(t + 1) * P], ACT.Copy).then_inc(moved, 1)
    with act.Fori(1, NT // 2) as i:
        for h in range(2):
            act.wait_ge(kept, i * 2 + h - 1)
            act.activation(yt[h][:], k.yT[:, :, ds((i * 2 + h) * P, P)], ACT.Copy).then_inc(moved, 1)
    act.wait_ge(kept, NT - 2)
    act.activation(yt[0][:], k.yT[:, :, (NT - 1) * P:NT * P], ACT.Copy).then_inc(moved, 1)


def linear_to_table(k, weights, bias, table, width, attention=None, last_one=False):
    nc = k.nc
    loaded, stored = k.dma_sem("lin_loaded"), [k.dma_sem(f"lin_stored{h}") for h in range(2)]
    prod, kept = k.sem("lin_prod"), k.sem("lin_kept")
    moved = k.sem("lin_moved")
    nblk = -(-width // 512)
    bw = width // nblk
    tw = TW if (attention is not None or last_one) else width
    with ExitStack() as ctx:
        sb, ps = tensors(nc, ctx)
        w = sb("w", [P, KC, width])
        b = sb("b", [1, width]) if bias is not None else None
        row = [sb(f"row{h}", [P, tw]) for h in range(2)]
        if attention is not None:
            att = sb("att", [P, 2, D])
            prodt = sb("prodt", [P, 2, D])
        acc = [ps(f"acc{h}", [P, nblk, 512]) for h in range(2)]
        yt = [sb(f"yt{h}", [P, KC, P]) for h in range(2)]
        with nc.Block() as block:
            @block.scalar
            def _(act):
                stage_yT(k, act, yt, kept, moved)

            @block.sync
            def _(sp):
                sp.dma_start(w[:], weights).then_inc(loaded, 16)
                n = 16
                if bias is not None:
                    sp.dma_start(b[:], bias).then_inc(loaded, 16)
                    n += 16
                if attention is not None:
                    sp.dma_start(att[:], attention).then_inc(loaded, 16)
                    n += 16
                sp.wait_ge(loaded, n)
                with sp.Fori(0, NT // 2) as i:
                    for h in range(2):
                        sp.wait_ge(kept, i * 2 + h + 1)
                        sp.dma_start(table[ds((i * 2 + h) * P, P), :], row[h][:]).then_inc(stored[h], 16)
                sp.wait_ge(kept, NT)
                sp.dma_start(table[(NT - 1) * P:NT * P, :], row[0][:]).then_inc(stored[0], 16)
                sp.wait_ge(stored[0], 16 * (NT // 2 + 1))
                sp.wait_ge(stored[1], 16 * (NT // 2))

            @block.tensor
            def _(pe):
                pe.wait_ge(loaded, 16 * (1 + (bias is not None) + (attention is not None)))

                def product(t, h):
                    pe.wait_ge(moved, t + 1)
                    for j in range(nblk):
                        for c in range(KC):
                            mm = pe.matmul(acc[h][:, j, 0:bw], yt[h][:, c, :],
                                           w[:, c, j * bw:(j + 1) * bw], start=(c == 0),
                                           stop=(c == KC - 1 and bias is None))
                        if bias is not None:
                            mm = pe.matmul(acc[h][:, j, 0:bw], k.ones[0:1, :], b[:, j * bw:(j + 1) * bw],
                                           start=False, stop=True)
                    mm.then_inc(prod, 1)
                by_parity(pe, product)

            @block.vector
            def _(dve):
                if last_one:
                    for h in range(2):
                        dve.memset(row[h][:, D:TW], 1.0)

                def keep(t, h):
                    dve.wait_ge(prod, t + 1)
                    if attention is None:
                        dve.tensor_copy(row[h][:, 0:width].rearrange("p (j c) -> p j c", c=bw),
                                        acc[h][:, :, 0:bw]).then_inc(kept, 1)
                        return
                    dve.tensor_copy(row[h][:, 0:D], acc[h][:, 0, 0:D])
                    for s in range(2):
                        dve.tensor_tensor(prodt[:, s, :], acc[h][:, 0, 0:D], att[:, s, :], ALU.mult)
                    dve.drain()
                    dve.tensor_reduce(row[h][:, D:TW], prodt[:, 0, :].rearrange("p (a b) -> p a b", a=HEADS), AX.X, ALU.add)
                    dve.tensor_reduce(k.ad[:, ds(t, 1), :], prodt[:, 1, :].rearrange("p (a b) -> p a b", a=HEADS), AX.X, ALU.add)
                    dve.drain().then_inc(kept, 1)
                dve.wait_ge(loaded, 16 * (1 + (bias is not None) + (attention is not None)))
                keep(0, 0)
                keep(1, 1)
                with dve.Fori(1, NT // 2) as i:
                    for h in range(2):
                        dve.wait_ge(stored[h], i * 16)
                        keep(i * 2 + h, h)
                dve.wait_ge(stored[0], 16 * (NT // 2))
                keep(NT - 1, 0)


def onehots(k, dve, out, meta, first, weight=None):
    mf = meta[:].bitcast(F32)
    local = mf[:, ds(first, HALF), F_LOCAL:F_LOCAL + 1]
    if weight is None:
        return dve.tensor_tensor(out, k.iota.unsqueeze(1).broadcast_to([P, HALF, P]),
                                 local.broadcast_to([P, HALF, P]), ALU.is_equal)
    raise ValueError


def gather_loop(k, pool, idx, field, rows, table, rows_done, got, gate, staged):
    def step(i):
        for h in range(2):
            wait(pool, got[h], i * (16 * HALF))
            pool.tensor_copy(k.gidx[h][:], idx[:, ds(i * GROUP + h * HALF, HALF), field]).then_inc(staged, 1)
            pool.wait_ge(staged, i * 2 + h + 1)
            for j in range(HALF):
                n = h * HALF + j
                pool.wait_ge(rows_done, i * GROUP + n + 1)
                pool.sem_inc(gate, 1)
                pool.indirect_dma_start(
                    out=rows[:, n, :], out_offset=None, in_=table,
                    in_offset=bass.IndirectOffsetOnAxis(ap=k.gidx[h][:, j:j + 1], axis=0)).then_inc(got[h], 16)
    peeled(pool, STEPS, step)


def aggregate(k, meta, btile, field, table, weights, acc):
    nc = k.nc
    width = table.shape[1]
    hot, rdone, added, gate, staged, zero = (k.sem(f"agg_{s}") for s in ("onehots", "rows_done", "added", "gate", "staged", "zeroed"))
    got = [k.dma_sem(f"agg_got{h}") for h in range(2)]
    with ExitStack() as ctx:
        sb, ps = tensors(nc, ctx)
        rows = sb("rows", [P, GROUP, width])
        oh = [sb(f"oh{h}", [P, HALF, P]) for h in range(2)]
        k.gidx = [sb(f"gidx{h}", [P, HALF], I32) for h in range(2)]
        pacc = ps("pacc", [P, 4, 512])
        with nc.Block() as block:
            @block.gpsimd
            def _(pool):
                gather_loop(k, pool, meta, field, rows, table, rdone, got, gate, staged)

            @block.tensor
            def _(pe):
                pe.sem_inc(rdone, GROUP)
                with pe.Fori(0, STEPS) as i:
                    for h in range(2):
                        pe.wait_ge(hot, i * 2 + h + 1)
                        pe.wait_ge(got[h], (i + 1) * (16 * HALF))
                        for j in range(HALF):
                            n = h * HALF + j
                            pe.wait_ge(added, i * GROUP + n + 1)
                            pe.matmul(pacc[:, n % 4, 0:width], oh[h][:, j, :], rows[:, n, :],
                                      start=True, stop=True).then_inc(rdone, 1)

            @block.vector
            def _(dve):
                dve.memset(acc[:], 0.0)
                dve.sem_inc(added, 4)
                dve.drain()

                def hots(i, h, g):
                    first = onehots(k, dve, oh[h][:], meta, g * HALF)
                    if weights is not None:
                        dve.drain()
                        first = dve.tensor_tensor(oh[h][:], oh[h][:],
                                                  weights[:, ds(g * HALF, HALF)].unsqueeze(2).broadcast_to([P, HALF, P]),
                                                  ALU.mult)
                    first.then_inc(hot, 1)
                hots(0, 0, 0)
                with dve.Fori(0, STEPS) as i:
                    for h in range(2):
                        dve.wait_ge(rdone, i * GROUP + h * HALF + GROUP)
                        hots(i, 1 - h, i * 2 + h + 1)
                        for j in range(HALF):
                            n = h * HALF + j
                            b = dve.value_load(btile[0:1, ds(i * GROUP + n, 1)], min_val=0, max_val=NT - 1)
                            dve.wait_ge(rdone, i * GROUP + n + 1 + GROUP)
                            dve.wait_ge(added, i * GROUP + n + 4)
                            dve.tensor_tensor(acc[:, ds(b, 1), 0:width], acc[:, ds(b, 1), 0:width],
                                              pacc[:, n % 4:n % 4 + 1, 0:width], ALU.add).then_inc(added, 1)


def type_weights(k, meta, btile, wedge):
    nc = k.nc
    hot, cnt, added = k.sem("tw_hot"), k.sem("tw_cnt"), k.sem("tw_added")
    hot2, turn, copied, look, used = (k.sem(f"tw_{s}") for s in ("hot2", "turned", "copied", "looked", "used"))
    with ExitStack() as ctx:
        sb, ps = tensors(nc, ctx)
        oh = [sb(f"oh{h}", [P, HALF, P]) for h in range(2)]
        th = [sb(f"th{h}", [P, HALF, NTYPE]) for h in range(2)]
        ohT = sb("ohT", [P, HALF, P])
        inv = sb("inv", [P, NT, NTYPE])
        sel = sb("sel", [P, HALF, NTYPE])
        pc = ps("pc", [P, 2, 512])
        pT = ps("pT", [P, 3, 4, P])
        mf = meta[:].bitcast(F32)

        def hots(dve, h, g, sem):
            onehots(k, dve, oh[h][:], meta, g * HALF)
            dve.tensor_tensor(th[h][:], k.iota[:, 0:NTYPE].unsqueeze(1).broadcast_to([P, HALF, NTYPE]),
                              mf[:, ds(g * HALF, HALF), F_TYPE:F_TYPE + 1].broadcast_to([P, HALF, NTYPE]),
                              ALU.is_equal).then_inc(sem, 1)
        with nc.Block() as block:
            @block.tensor
            def _(pe):
                pe.sem_inc(cnt, 1)
                with pe.Fori(0, STEPS) as i:
                    for h in range(2):
                        pe.wait_ge(hot, i * 2 + h + 1)
                        pe.wait_ge(added, i * 2 + h + 1)
                        for j in range(HALF):
                            mm = pe.matmul(pc[:, h, j * NTYPE:(j + 1) * NTYPE], oh[h][:, j, :], th[h][:, j, :],
                                           start=True, stop=True)
                        mm.then_inc(cnt, 1)

            @block.vector
            def _(dve):
                dve.memset(inv[:], 0.0)
                dve.memset(wedge[:], 0.0)
                dve.sem_inc(added, 2)
                dve.drain()
                hots(dve, 0, 0, hot)
                with dve.Fori(0, STEPS) as i:
                    for h in range(2):
                        dve.wait_ge(cnt, i * 2 + h + 1)
                        hots(dve, 1 - h, i * 2 + h + 1, hot)
                        dve.wait_ge(cnt, i * 2 + h + 2)
                        for j in range(HALF):
                            b = dve.value_load(btile[0:1, ds(i * GROUP + h * HALF + j, 1)], min_val=0, max_val=NT - 1)
                            dve.tensor_tensor(inv[:, ds(b, 1), :], inv[:, ds(b, 1), :],
                                              pc[:, h:h + 1, j * NTYPE:(j + 1) * NTYPE], ALU.add)
                            dve.drain()
                        dve.sem_inc(added, 1)
                dve.tensor_scalar(inv[:], inv[:], 1.0, None, ALU.max)
                dve.drain()
                dve.reciprocal(inv[:], inv[:])
        with nc.Block() as block:
            @block.tensor
            def _(pe):
                pe.sem_inc(look, 1)
                with pe.Fori(0, STEPS) as i:
                    for h in range(2):
                        pe.wait_ge(hot2, i * 2 + h + 1)
                        for j in range(HALF):
                            mm = pe.transpose(pT[:, j // 4, j % 4, :], oh[h][:, j, :], k.ident)
                        mm.then_inc(turn, 1)
                        pe.wait_ge(copied, i * 2 + h + 1)
                        pe.wait_ge(used, i * 2 + h + 1)
                        for j in range(HALF):
                            b = pe.value_load(btile[0:1, ds(i * GROUP + h * HALF + j, 1)], min_val=0, max_val=NT - 1)
                            mm = pe.matmul(pc[:, h, j * NTYPE:(j + 1) * NTYPE], ohT[:, j, :], inv[:, ds(b, 1), :],
                                           start=True, stop=True)
                        mm.then_inc(look, 1)

            @block.scalar
            def _(act):
                with act.Fori(0, STEPS * 2) as g:
                    act.wait_ge(turn, g + 1)
                    act.wait_ge(look, g + 1)
                    for q in range(2):
                        act.activation(ohT[:, 4 * q:4 * q + 4, :], pT[:, q, :, :], ACT.Copy)
                    act.activation(ohT[:, 8:HALF, :], pT[:, 2, 0:HALF - 8, :], ACT.Copy)
                    act.drain().then_inc(copied, 1)

            @block.vector
            def _(dve):
                dve.sem_inc(used, 2)
                hots(dve, 0, 0, hot2)
                with dve.Fori(0, STEPS) as i:
                    for h in range(2):
                        dve.wait_ge(look, i * 2 + h + 1)
                        hots(dve, 1 - h, i * 2 + h + 1, hot2)
                        dve.wait_ge(look, i * 2 + h + 2)
                        dve.tensor_tensor(sel[:], pc[:, h, 0:HALF * NTYPE].rearrange("p (j c) -> p j c", c=NTYPE),
                                          th[h][:], ALU.mult)
                        dve.drain().then_inc(used, 1)
                        dve.tensor_reduce(wedge[:, ds((i * 2 + h) * HALF, HALF)], sel[:], AX.X, ALU.add)
                        dve.drain()


def attention_aggregate(k, meta, btile, table, acc, scale):
    nc = k.nc
    rdone, added, gate, staged = (k.sem(f"att_{s}") for s in ("rows_done", "added", "gate", "staged"))
    hot, turn, copied, look, eused = (k.sem(f"att_{s}") for s in ("hot", "turned", "copied", "looked", "eused"))
    top, topT, topr, topb, newtop, prob, msg = (k.sem(f"att_{s}") for s in ("top", "topT", "topr", "topb", "newtop", "prob", "msg"))
    got = [k.dma_sem(f"att_got{h}") for h in range(2)]
    with ExitStack() as ctx:
        sb, ps = tensors(nc, ctx)
        rows = sb("rows", [P, GROUP, TW])
        oh = [sb(f"oh{h}", [P, HALF, P]) for h in range(2)]
        ohT = sb("ohT", [P, HALF, P])
        k.gidx = [sb(f"gidx{h}", [P, HALF], I32) for h in range(2)]
        e = sb("e", [P, HALF, HEADS])
        pen = sb("pen", [P, HALF])
        mx = sb("mx", [P, 1])
        mrow = sb("mrow", [1, 1])
        ref = sb("ref", [P, 1])
        nref = sb("nref", [P, 1])
        drop = sb("drop", [P, 1])
        fac = sb("fac", [P, 1])
        pT = ps("pT", [P, 3, 4, P])
        pterm = [ps(f"pterm{h}", [P, 512]) for h in range(2)]
        ptop = ps("ptop", [P, 512])
        pacc = ps("pacc", [P, 2, 512])
        mf = meta[:].bitcast(F32)

        with nc.Block() as block:
            @block.gpsimd
            def _(pool):
                gather_loop(k, pool, meta, F_OTHER, rows, table, rdone, got, gate, staged)

            @block.tensor
            def _(pe):
                def destinations(i, h, g):
                    pe.wait_ge(hot, g + 1)
                    for j in range(HALF):
                        mm = pe.transpose(pT[:, j // 4, j % 4, :], oh[h][:, j, :], k.ident)
                    mm.then_inc(turn, 1)
                    pe.wait_ge(copied, g + 1)
                    pe.wait_ge(eused, g + 1)
                    for j in range(HALF):
                        b = pe.value_load(btile[0:1, ds(g * HALF + j, 1)], min_val=0, max_val=NT - 1)
                        mm = pe.matmul(pterm[h][:, j * HEADS:(j + 1) * HEADS], ohT[:, j, :],
                                       k.ad[:, ds(b, 1), :], start=True, stop=True)
                    mm.then_inc(look, 1)
                pe.sem_inc(rdone, GROUP)
                pe.sem_inc(look, 1)
                destinations(0, 0, 0)
                with pe.Fori(0, STEPS) as i:
                    for h in range(2):
                        g = i * 2 + h
                        destinations(i, 1 - h, g + 1)
                        pe.wait_ge(top, g + 1)
                        pe.transpose(ptop[0:1, 0:P], mx[:], k.ident).then_inc(topT, 1)
                        pe.wait_ge(topr, g + 1)
                        pe.matmul(ptop[:, 0:1], k.ones[0:1, :], mrow[:], start=True, stop=True).then_inc(topb, 1)
                        pe.wait_ge(msg, g + 1)
                        for j in range(HALF):
                            n = h * HALF + j
                            pe.wait_ge(added, i * GROUP + n + 1)
                            pe.matmul(pacc[:, n % 2, 0:TW], oh[h][:, j, :], rows[:, n, :],
                                      start=True, stop=True).then_inc(rdone, 1)

            @block.scalar
            def _(act):
                def copy_turned(g):
                    act.wait_ge(turn, g + 1)
                    act.wait_ge(look, g + 1)
                    for q in range(2):
                        act.activation(ohT[:, 4 * q:4 * q + 4, :], pT[:, q, :, :], ACT.Copy)
                    act.activation(ohT[:, 8:HALF, :], pT[:, 2, 0:HALF - 8, :], ACT.Copy)
                    act.drain().then_inc(copied, 1)
                copy_turned(0)
                with act.Fori(0, STEPS) as i:
                    for h in range(2):
                        g = i * 2 + h
                        copy_turned(g + 1)
                        act.wait_ge(newtop, g + 1)
                        act.activation(rows[:, h * HALF:(h + 1) * HALF, D:TW], e[:], ACT.Exp, bias=nref[:])
                        act.activation(fac[:], drop[:], ACT.Exp)
                        act.drain().then_inc(prob, 1)

            @block.vector
            def _(dve):
                def hots(h, g):
                    onehots(k, dve, oh[h][:], meta, g * HALF).then_inc(hot, 1)
                dve.memset(acc[:], 0.0)
                dve.memset(scale[:], 1.0)
                dve.memset(ref[:], LOWEST)
                dve.sem_inc(added, 2)
                dve.sem_inc(eused, 2)
                dve.drain()
                hots(0, 0)
                with dve.Fori(0, STEPS) as i:
                    for h in range(2):
                        g = i * 2 + h
                        dve.wait_ge(rdone, i * GROUP + h * HALF + GROUP)
                        hots(1 - h, g + 1)
                        dve.wait_ge(look, g + 2)
                        dve.wait_ge(got[h], (i + 1) * (16 * HALF))
                        sl = slice(h * HALF, (h + 1) * HALF)
                        dve.tensor_tensor(e[:], rows[:, sl, D:TW],
                                          pterm[h][:, 0:HALF * HEADS].rearrange("p (j c) -> p j c", c=HEADS), ALU.add)
                        dve.tensor_scalar(pen[:], mf[:, ds(g * HALF, HALF), F_LOCAL], 0.0, -LOWEST, ALU.min, ALU.mult)
                        dve.drain().then_inc(eused, 1)
                        dve.scalar_tensor_tensor(out=e[:], in0=e[:], scalar=0.2, in1=e[:], op0=ALU.mult, op1=ALU.max)
                        dve.drain()
                        dve.tensor_tensor(e[:], e[:], mf[:, ds(g * HALF, HALF), F_WEIGHT:F_WEIGHT + 1]
                                          .broadcast_to([P, HALF, HEADS]), ALU.mult)
                        dve.drain()
                        dve.tensor_tensor(e[:], e[:], pen[:].unsqueeze(2).broadcast_to([P, HALF, HEADS]), ALU.add)
                        dve.drain()
                        dve.tensor_reduce(mx[:], e[:], AX.XY, ALU.max).then_inc(top, 1)
                        dve.wait_ge(topT, g + 1)
                        dve.tensor_reduce(mrow[:], ptop[0:1, 0:P], AX.X, ALU.max).then_inc(topr, 1)
                        dve.wait_ge(topb, g + 1)
                        dve.tensor_tensor(nref[:], ref[:], ptop[:, 0:1], ALU.max)
                        dve.drain()
                        dve.tensor_tensor(drop[:], ref[:], nref[:], ALU.subtract)
                        dve.drain()
                        dve.tensor_copy(ref[:], nref[:])
                        dve.drain()
                        dve.tensor_scalar(nref[:], ref[:], -1.0, None, ALU.mult)
                        dve.drain().then_inc(newtop, 1)
                        dve.wait_ge(prob, g + 1)
                        dve.tensor_scalar(scale[:], scale[:], fac[:], None, ALU.mult)
                        dve.tensor_tensor(rows[:, sl, 0:D].rearrange("p j (a b) -> p j a b", a=HEADS),
                                          rows[:, sl, 0:D].rearrange("p j (a b) -> p j a b", a=HEADS),
                                          rows[:, sl, D:TW].unsqueeze(3).broadcast_to([P, HALF, HEADS, HD]), ALU.mult)
                        dve.drain().then_inc(msg, 1)
                        for j in range(HALF):
                            n = h * HALF + j
                            b = dve.value_load(btile[0:1, ds(i * GROUP + n, 1)], min_val=0, max_val=NT - 1)
                            dve.wait_ge(rdone, i * GROUP + n + 1 + GROUP)
                            dve.wait_ge(added, i * GROUP + n + 2)
                            dve.scalar_tensor_tensor(out=acc[:, ds(b, 1), :], in0=acc[:, ds(b, 1), :],
                                                     scalar=scale[:, ds(b, 1)], in1=pacc[:, n % 2:n % 2 + 1, 0:TW],
                                                     op0=ALU.mult, op1=ALU.add)
                            dve.drain()
                            dve.tensor_copy(scale[:, ds(b, 1)], k.ones[:, 0:1])
                            dve.drain().then_inc(added, 1)


def attention_finish(k, acc, scale):
    with ExitStack() as ctx:
        sb, _ = tensors(k.nc, ctx)
        rden = sb("rden", [P, NT, HEADS])
        with k.nc.Block() as block:
            @block.vector
            def _(dve):
                dve.tensor_tensor(acc[:], acc[:], scale[:].unsqueeze(2).broadcast_to([P, NT, TW]), ALU.mult)
                dve.drain()
                dve.tensor_scalar(rden[:], acc[:, :, D:TW], 1e-10, None, ALU.add)
                dve.drain()
                dve.reciprocal(rden[:], rden[:])
                dve.drain()
                with dve.Fori(0, NT) as t:
                    dve.tensor_tensor(acc[:, ds(t, 1), 0:D].rearrange("p t (a b) -> p (t a) b", a=HEADS),
                                      acc[:, ds(t, 1), 0:D].rearrange("p t (a b) -> p (t a) b", a=HEADS),
                                      rden[:, ds(t, 1), :].rearrange("p t a -> p (t a)").unsqueeze(2)
                                      .broadcast_to([P, HEADS, HD]), ALU.mult)
                dve.drain()
                dve.tensor_tensor(k.x[:], k.x[:], acc[:, :, 0:D], ALU.add)


def logits(k, lg, width, weights, bias):
    nc = k.nc
    loaded = k.dma_sem("lg_loaded")
    prod, kept, moved = (k.sem(f"lg_{s}") for s in ("prod", "kept", "moved"))
    with ExitStack() as ctx:
        sb, ps = tensors(nc, ctx)
        w = sb("lw", [P, KC, width])
        b = sb("lb", [1, width]) if bias is not None else None
        pl = ps("pl", [P, 2, 512])
        nload = 16 * (1 + (bias is not None))
        yt = [sb(f"yt{h}", [P, KC, P]) for h in range(2)]
        with nc.Block() as block:
            @block.scalar
            def _(act):
                stage_yT(k, act, yt, kept, moved)

            @block.sync
            def _(sp):
                sp.dma_start(w[:], weights).then_inc(loaded, 16)
                if bias is not None:
                    sp.dma_start(b[:], bias).then_inc(loaded, 16)

            @block.tensor
            def _(pe):
                pe.wait_ge(loaded, nload)

                def product(t, h):
                    pe.wait_ge(moved, t + 1)
                    for c in range(KC):
                        mm = pe.matmul(pl[:, h, 0:width], yt[h][:, c, :], w[:, c, :],
                                       start=(c == 0), stop=(c == KC - 1 and bias is None))
                    if bias is not None:
                        mm = pe.matmul(pl[:, h, 0:width], k.ones[0:1, :], b[:], start=False, stop=True)
                    mm.then_inc(prod, 1)
                by_parity(pe, product)

            @block.vector
            def _(dve):
                dve.memset(lg[:], LOWEST)
                dve.drain()

                def keep(t, h):
                    dve.wait_ge(prod, t + 1)
                    dve.tensor_copy(lg[:, ds(t, 1), 0:width], pl[:, h:h + 1, 0:width]).then_inc(kept, 1)
                by_parity(dve, keep)


def gates(k, width, experts, kind):
    nc = k.nc
    with ExitStack() as ctx:
        sb, ps = tensors(nc, ctx)
        EP = experts
        lg = sb("lg", [P, NT, EP])
        logits(k, lg, experts, *width)
        top = sb("top", [P, NT, 2])
        second = sb("second", [P, NT, EP])
        w = sb("w", [P, NT, P])
        tmp = sb("tmp", [P, NT, EP])
        one = sb("one", [P, NT, 2])
        tile = [sb(f"tile{h}", [P, P]) for h in range(2)]
        pt = ps("pt", [P, 2, 512])
        shift, powered, diff, powd, ready, turned, taken = (
            k.sem(f"gate_{s}") for s in ("shift", "powered", "diff", "powd", "ready", "turned", "taken"))
        with nc.Block() as block:
            @block.vector
            def _(dve):
                def both(a, n):
                    return a.broadcast_to([P, NT, n])
                dve.memset(w[:], 0.0)
                if kind != "top1":
                    dve.tensor_reduce(one[:, :, 0:1], lg[:], AX.X, ALU.max)
                    dve.drain()
                    dve.tensor_tensor(lg[:], lg[:], both(one[:, :, 0:1], EP), ALU.subtract)
                    dve.drain().then_inc(shift, 1)
                    dve.wait_ge(powered, 1)
                    dve.tensor_reduce(one[:, :, 0:1], lg[:], AX.X, ALU.add)
                    dve.drain()
                    dve.reciprocal(one[:, :, 1:2], one[:, :, 0:1])
                    dve.drain()
                    dve.tensor_tensor(lg[:], lg[:], both(one[:, :, 1:2], EP), ALU.mult)
                dve.drain()
                iota = k.iota[:, 0:experts].unsqueeze(1).broadcast_to([P, NT, experts])

                def first_largest(n, values, out):
                    dve.tensor_reduce(top[:, :, n:n + 1], values, AX.X, ALU.max)
                    dve.drain()
                    dve.tensor_tensor(tmp[:], values, both(top[:, :, n:n + 1], EP), ALU.is_equal)
                    dve.drain()
                    dve.tensor_scalar(tmp[:], tmp[:], -float(P), None, ALU.mult)
                    dve.drain()
                    dve.tensor_tensor(tmp[:], tmp[:], iota, ALU.add)
                    dve.drain()
                    dve.tensor_reduce(one[:, :, 0:1], tmp[:], AX.X, ALU.min)
                    dve.drain()
                    dve.tensor_tensor(out, tmp[:], both(one[:, :, 0:1], EP), ALU.is_equal)
                    dve.drain()
                first_largest(0, lg[:], w[:, :, 0:experts])
                if kind != "top1":
                    dve.scalar_tensor_tensor(out=lg[:], in0=w[:, :, 0:experts], scalar=-2.0, in1=lg[:],
                                             op0=ALU.mult, op1=ALU.add)
                    dve.drain()
                    first_largest(1, lg[:], second[:])
                if kind == "soft2":
                    dve.tensor_tensor(one[:, :, 1:2], top[:, :, 1:2], top[:, :, 0:1], ALU.subtract)
                    dve.drain().then_inc(diff, 1)
                    dve.wait_ge(powd, 1)
                    dve.tensor_scalar(one[:, :, 0:1], one[:, :, 1:2], 1.0, None, ALU.add)
                    dve.drain()
                    dve.reciprocal(one[:, :, 0:1], one[:, :, 0:1])
                    dve.drain()
                    dve.tensor_tensor(one[:, :, 1:2], one[:, :, 1:2], one[:, :, 0:1], ALU.mult)
                elif kind == "share2":
                    dve.tensor_tensor(one[:, :, 0:1], top[:, :, 0:1], top[:, :, 1:2], ALU.add)
                    dve.drain()
                    dve.tensor_scalar(one[:, :, 0:1], one[:, :, 0:1], 1e-12, None, ALU.max)
                    dve.drain()
                    dve.reciprocal(one[:, :, 0:1], one[:, :, 0:1])
                    dve.drain()
                    dve.tensor_tensor(one[:, :, 1:2], top[:, :, 1:2], one[:, :, 0:1], ALU.mult)
                    dve.tensor_tensor(one[:, :, 0:1], top[:, :, 0:1], one[:, :, 0:1], ALU.mult)
                dve.drain()
                if kind != "top1":
                    dve.tensor_tensor(w[:, :, 0:experts], w[:, :, 0:experts], both(one[:, :, 0:1], experts), ALU.mult)
                    dve.tensor_tensor(second[:], second[:], both(one[:, :, 1:2], experts), ALU.mult)
                    dve.drain()
                    dve.tensor_tensor(w[:, :, 0:experts], w[:, :, 0:experts], second[:], ALU.add)
                    dve.drain()

                def stage(t, h):
                    dve.wait_ge(turned, t + 1)
                    dve.tensor_copy(tile[h][:].unsqueeze(1), w[:, ds(t, 1), :]).then_inc(ready, 1)
                by_parity(dve, stage)

            @block.scalar
            def _(act):
                if kind != "top1":
                    act.wait_ge(shift, 1)
                    act.activation(lg[:], lg[:], ACT.Exp).then_inc(powered, 1)
                if kind == "soft2":
                    act.wait_ge(diff, 1)
                    act.activation(one[:, :, 1:2], one[:, :, 1:2], ACT.Exp).then_inc(powd, 1)
                act.sem_inc(taken, 2)

                def take(t, h):
                    act.wait_ge(turned, t + 3)
                    act.activation(k.gates[0:experts, ds(t * P, P)], pt[0:experts, h, 0:P], ACT.Copy).then_inc(taken, 1)
                by_parity(act, take)

            @block.tensor
            def _(pe):
                pe.sem_inc(turned, 2)

                def turn(t, h):
                    pe.wait_ge(ready, t + 1)
                    pe.wait_ge(taken, t + 1)
                    pe.transpose(pt[:, h, 0:P], tile[h][:], k.ident).then_inc(turned, 1)
                by_parity(pe, turn)


def feed_forward(k, chunks, w1d, b1d, func, experts, sel, w2d, b2d, finish, rank=None):
    nc = k.nc
    G = 4
    ng = chunks // G
    gstaged = k.sem("ff_gates")
    loaded = k.dma_sem("ff_loaded")
    hid, act_, gated, osum, fin = (k.sem(f"ff_{s}") for s in ("hidden", "active", "gated", "summed", "finished"))
    with ExitStack() as ctx:
        sb, ps = tensors(nc, ctx)
        w1 = sb("w1", [P, KC, chunks * P])
        b1 = sb("b1", [P, chunks])
        w2 = sb("w2", [P, chunks, D])
        b2 = sb("b2", [max(experts, 1), D])
        gt = sb("gt", [max(experts, 1), P])
        h = [sb(f"h{i}", [P, G, P]) for i in range(2)]
        hm = [sb(f"hm{i}", [P, G, P]) for i in range(2)] if sel is not None else h
        ph = [ps(f"ph{i}", [P, G, P]) for i in range(2)]
        pm = [ps(f"pm{i}", [P, G, P]) for i in range(2)] if sel is not None else None
        po = ps("po", [P, 512])
        used = gated if sel is not None else act_
        with nc.Block() as block:
            @block.sync
            def _(sp):
                for a, b in ((w1, w1d), (b1, b1d), (w2, w2d), (b2, b2d)):
                    sp.dma_start(a[:], b).then_inc(loaded, 16)

            @block.tensor
            def _(pe):
                def hidden(t, g, s):
                    pe.wait_ge(act_, s + 1)
                    if sel is not None:
                        pe.wait_ge(gated, s + 1)
                    for j in range(G):
                        n = g * G + j
                        for c in range(KC):
                            mm = pe.matmul(ph[g % 2][:, j, :], w1[:, c, n * P:(n + 1) * P], k.yT[:, c, ds(t * P, P)],
                                           start=(c == 0), stop=(c == KC - 1))
                    if sel is not None:
                        for j in range(G):
                            n = g * G + j
                            mm = pe.matmul(pm[g % 2][:, j, :], sel[:, n * P:(n + 1) * P],
                                           k.gates[0:experts, ds(t * P, P)], start=True, stop=True)
                    mm.then_inc(hid, 1)
                pe.sem_inc(osum, 2)
                pe.wait_ge(loaded, 64)
                hidden(0, 0, 0)
                with pe.Fori(0, NT) as t:
                    for g in range(ng):
                        s = t * ng + g
                        hidden(t + (g + 1) // ng, (g + 1) % ng, s + 1)
                        pe.wait_ge(used, s + 3)
                        if g == 0:
                            pe.wait_ge(fin, t + 1)
                        for j in range(G):
                            mm = pe.matmul(po[:, 0:D], hm[g % 2][:, j, :], w2[:, g * G + j, :],
                                           start=(g == 0 and j == 0), stop=False)
                        if g < ng - 1:
                            mm.then_inc(osum, 1)
                    lhs = gt[:] if experts > 1 else k.ones[0:1, :]
                    if experts > 1:
                        pe.wait_ge(gstaged, t + 1)
                    mm = pe.matmul(po[:, 0:D], lhs, b2[:], start=False, stop=True).then_inc(osum, 1)

            @block.scalar
            def _(act):
                act.sem_inc(act_, 2)
                if rank is not None:
                    act.sem_inc(fin, 1)
                act.wait_ge(loaded, 64)
                with act.Fori(0, NT) as t:
                    for g in range(ng):
                        s = t * ng + g
                        act.wait_ge(hid, s + 1)
                        act.wait_ge(gated if sel is not None else osum, s + 1)
                        for j in range(G):
                            mm = act.activation(h[g % 2][:, j, :], ph[g % 2][:, j, :], func,
                                                bias=b1[:, g * G + j:g * G + j + 1])
                        mm.then_inc(act_, 1)
                    if rank is not None:
                        act.wait_ge(osum, t * ng + ng + 2)
                        act.activation(k.z[:, ds(t, 1), 0:D], po[:, 0:D].unsqueeze(1), ACT.Copy).then_inc(fin, 1)

            @block.vector
            def _(dve):
                if rank is not None:
                    rank(dve)
                    return
                dve.sem_inc(gated, 2)
                dve.sem_inc(fin, 1)
                with dve.Fori(0, NT) as t:
                    dve.tensor_copy(gt[:], k.gates[0:experts, ds(t * P, P)]).then_inc(gstaged, 1)
                    for g in range(ng):
                        s = t * ng + g
                        dve.wait_ge(act_, s + 3)
                        dve.wait_ge(osum, s + 1)
                        dve.tensor_tensor(hm[g % 2][:], h[g % 2][:], pm[g % 2][:], ALU.mult).then_inc(gated, 1)
                    dve.wait_ge(osum, t * ng + ng + 2)
                    finish(dve, t, po[:, 0:D].unsqueeze(1))
                    dve.drain().then_inc(fin, 1)


def shared_and_experts(k, A):
    nc = k.nc
    loaded = k.dma_sem("moe1_loaded")
    l1, a1, l2, a2, gt, osum, fin = (k.sem(f"moe1_{s}") for s in (
        "first", "act1", "second", "act2", "gated", "out", "fin"))
    NX = 4
    gstaged = k.sem("moe1_gates")
    with ExitStack() as ctx:
        sb, ps = tensors(nc, ctx)
        w1 = sb("w1", [P, KC, 6 * P])
        w2 = sb("w2", [P, 6, P])
        w3 = sb("w3", [P, 3, D])
        b1 = sb("b1", [P, 6])
        b2 = sb("b2", [P, 3])
        b3 = sb("b3", [NX, D])
        sb3 = sb("sb3", [1, D])
        gtile = sb("gtile", [NX, P])
        h1 = [sb(f"h1{i}", [P, 6, P]) for i in range(2)]
        h2 = [sb(f"h2{i}", [P, 3, P]) for i in range(2)]
        p1 = ps("p1", [P, 2, 4, P])
        p2 = ps("p2", [P, 4, P])
        pm = ps("pm", [P, 4, P])
        po = ps("po", [P, 512])
        with nc.Block() as block:
            @block.sync
            def _(sp):
                for a, n in ((w1, "m1_w1"), (w2, "m1_w2"), (w3, "m1_w3"), (b1, "m1_b1"), (b2, "m1_b2"),
                             (b3, "m1_b3"), (sb3, "m1_sb3")):
                    sp.dma_start(a[:], A[n]).then_inc(loaded, 16)

            @block.tensor
            def _(pe):
                def first(t):
                    pe.wait_ge(a1, t + 1)
                    for n in range(6):
                        for c in range(KC):
                            mm = pe.matmul(p1[:, n // 4, n % 4, :], w1[:, c, n * P:(n + 1) * P],
                                           k.yT[:, c, ds(t * P, P)], start=(c == 0), stop=(c == KC - 1))
                    mm.then_inc(l1, 1)
                pe.sem_inc(osum, 1)
                pe.wait_ge(loaded, 16 * 7)
                first(0)
                with pe.Fori(0, NT) as t:
                    pe.wait_ge(a1, t + 2)
                    pe.wait_ge(gt, t + 1)
                    for n, of in ((0, 0), (1, 0), (2, 1), (3, 1), (4, 2), (5, 2)):
                        mm = pe.matmul(p2[:, of, :], w2[:, n, :], h1[0][:, n, :], start=(n % 2 == 0), stop=(n % 2 == 1))
                    for n in range(2):
                        mm = pe.matmul(pm[:, n, :], k.sel1[:, n * P:(n + 1) * P], k.gates[0:NX, ds(t * P, P)],
                                       start=True, stop=True)
                    mm.then_inc(l2, 1)
                    first(t + 1)
                    pe.wait_ge(gt, t + 2)
                    pe.wait_ge(fin, t + 1)
                    for n in range(3):
                        pe.matmul(po[:, 0:D], h2[1][:, n, :], w3[:, n, :], start=(n == 0), stop=False)
                    pe.wait_ge(gstaged, t + 1)
                    pe.matmul(po[:, 0:D], gtile[:], b3[:], start=False, stop=False)
                    pe.matmul(po[:, 0:D], k.ones[0:1, :], sb3[:], start=False, stop=True).then_inc(osum, 1)

            @block.scalar
            def _(act):
                act.sem_inc(a1, 1)
                act.wait_ge(loaded, 16 * 7)
                with act.Fori(0, NT) as t:
                    act.wait_ge(l1, t + 1)
                    act.wait_ge(l2, t + 1)
                    for n in range(6):
                        mm = act.activation(h1[0][:, n, :], p1[:, n // 4, n % 4, :], ACT.Relu, bias=b1[:, n:n + 1])
                    mm.then_inc(a1, 1)
                    act.wait_ge(l2, t + 2)
                    act.wait_ge(gt, t + 1)
                    for n in range(3):
                        mm = act.activation(h2[0][:, n, :], p2[:, n, :], ACT.Relu, bias=b2[:, n:n + 1])
                    mm.then_inc(a2, 1)

            @block.vector
            def _(dve):
                dve.sem_inc(gt, 1)
                dve.sem_inc(fin, 1)
                dve.sem_inc(l2, 1)
                with dve.Fori(0, NT) as t:
                    dve.wait_ge(a2, t + 1)
                    dve.wait_ge(osum, t + 1)
                    dve.tensor_copy(gtile[:], k.gates[0:NX, ds(t * P, P)]).then_inc(gstaged, 1)
                    dve.tensor_copy(h2[1][:, 0, :], h2[0][:, 0, :])
                    dve.tensor_tensor(h2[1][:, 1:3, :], h2[0][:, 1:3, :], pm[:, 0:2, :], ALU.mult)
                    dve.drain().then_inc(gt, 1)
                    dve.wait_ge(osum, t + 2)
                    dve.tensor_tensor(k.x[:, ds(t, 1), :], k.x[:, ds(t, 1), :], po[:, 0:D].unsqueeze(1), ALU.add)
                    dve.drain().then_inc(fin, 1)


def add_sums(k, acc):
    with k.nc.Block() as block:
        @block.vector
        def _(dve):
            dve.tensor_tensor(k.x[:], k.x[:], acc[:, :, 0:D], ALU.add)


def inverse_counts(dve, rc, acc):
    dve.tensor_scalar(rc, acc[:, :, D:D + 1], 1.0, None, ALU.max)
    dve.drain()
    dve.reciprocal(rc, rc)
    dve.drain()


def means_to_table(k, acc, table):
    stored, ready = k.dma_sem("means_stored"), k.sem("means_ready")
    with ExitStack() as ctx:
        sb, _ = tensors(k.nc, ctx)
        rc = sb("rc", [P, NT, 1])
        with k.nc.Block() as block:
            @block.vector
            def _(dve):
                inverse_counts(dve, rc[:], acc)
                dve.tensor_tensor(acc[:, :, 0:D], acc[:, :, 0:D], rc[:].broadcast_to([P, NT, D]), ALU.mult)
                dve.memset(acc[:, :, D:TW], 1.0)
                dve.drain().then_inc(ready, 1)

            @block.sync
            def _(sp):
                sp.wait_ge(ready, 1)
                sp.dma_start(table.rearrange("(t p) w -> p t w", p=P), acc[:]).then_inc(stored, 16)
                sp.wait_ge(stored, 16)


def hyper_activation(k, A, acc, bias_name, last):
    nc = k.nc
    loaded = k.dma_sem("ha_loaded")
    ready, turned, taken = (k.sem(f"ha_{s}") for s in ("ready", "turned", "taken"))
    with ExitStack() as ctx:
        sb, ps = tensors(nc, ctx)
        rc = sb("rc", [P, NT, 1])
        bias = sb("bias", [P, D])
        slope = sb("slope", [P, 1])
        low = sb("low", [P, NT, D])
        pst = ps("pst", [P, 2, 4, P])
        tile = [sb(f"tile{h}", [P, 1, D]) for h in range(2)]
        with nc.Block() as block:
            @block.sync
            def _(sp):
                sp.dma_start(bias[:], A[bias_name]).then_inc(loaded, 16)
                sp.dma_start(slope[:], A["g3_a"]).then_inc(loaded, 16)

            @block.vector
            def _(dve):
                inverse_counts(dve, rc[:], acc)
                dve.wait_ge(loaded, 32)
                a = acc[:, :, 0:D]
                dve.tensor_tensor(a, a, rc[:].broadcast_to([P, NT, D]), ALU.mult)
                dve.drain()
                dve.tensor_tensor(a, a, bias[:].unsqueeze(1).broadcast_to([P, NT, D]), ALU.add)
                dve.drain()
                if last:
                    dve.tensor_tensor(a, a, k.y[:], ALU.add)
                    dve.drain()
                dve.tensor_scalar(low[:], a, 0.0, slope[:], ALU.min, ALU.mult)
                dve.tensor_scalar(a, a, 0.0, None, ALU.max)
                dve.drain()
                dve.tensor_tensor(a, a, low[:], ALU.add)
                dve.drain()
                if last:
                    dve.tensor_tensor(k.x[:], k.x[:], a, ALU.add)
                else:
                    def stage(t, h):
                        dve.wait_ge(turned, t + 1)
                        dve.tensor_copy(tile[h][:], acc[:, ds(t, 1), 0:D]).then_inc(ready, 1)
                    by_parity(dve, stage)
            if not last:
                @block.tensor
                def _(pe):
                    turn_loop(k, pe, tile, pst, ready, turned, taken)

                @block.scalar
                def _(act):
                    take_loop(k, act, pst, turned, taken)


def chosen_tokens(k, A, wt, wrow_d):
    nc = k.nc
    logits(k, wt, 1, A["f3_wr"], A["f3_br"])
    turned, copied, stored = k.sem("rank_turned"), k.sem("rank_copied"), k.dma_sem("rank_stored")
    with ExitStack() as ctx:
        sb, ps = tensors(nc, ctx)
        pad = sb("pad", [P, P])
        rowt = sb("rowt", [NT, P])
        pt = ps("pt", [P, P])
        with nc.Block() as block:
            @block.vector
            def _(dve):
                dve.memset(pad[:], 0.0)
                dve.drain()
                dve.tensor_copy(pad[:, 0:NT], wt[:, :, 0])
                dve.drain().then_inc(copied, 1)
                dve.wait_ge(turned, 1)
                dve.tensor_copy(rowt[:], pt[0:NT, :]).then_inc(copied, 1)

            @block.tensor
            def _(pe):
                pe.wait_ge(copied, 1)
                pe.transpose(pt[:], pad[:], k.ident).then_inc(turned, 1)

            @block.sync
            def _(sp):
                sp.wait_ge(copied, 2)
                sp.dma_start(wrow_d, rowt[:]).then_inc(stored, 16)
                sp.wait_ge(stored, 16)


CHOSEN = max(1, N // 2) - 1


def build(nc, A, out):
    with ExitStack() as ctx:
        k = Kit(nc, ctx)
        sb, _ = tensors(nc, ctx)
        k.const = sb("const", [P, C_END])
        k.x = sb("x", [P, NT, D])
        k.y = sb("y", [P, NT, D])
        k.yT = sb("yT", [P, KC, NP_ + P])
        graph = ctx.enter_context(ExitStack())
        gsb, _ = tensors(nc, graph)
        meta_d = gsb("meta_dst", [P, COLS, NF], I32)
        meta_s = gsb("meta_src", [P, COLS, NF], I32)
        bt_d = gsb("bt_dst", [1, COLS], I32)
        bt_s = gsb("bt_src", [1, COLS], I32)
        k.ad = gsb("ad", [P, NT, HEADS])
        wedge = gsb("wedge", [P, COLS])
        c = k.const
        k.ident, k.iota, k.tri, k.ones = (c[:, o:o + P] for o in (C_ID, C_IOTA, C_TRI, C_ONES))
        k.tile_iota = c[:, C_TILE:C_TILE + COLS]
        sel0, k.sel1, sel2 = c[0:32, C_SEL0:C_SEL1], c[0:4, C_SEL1:C_SEL2], c[0:8, C_SEL2:C_END]
        slots_d, slots_s = k.dram("slots_dst", [P * COLS, NF], I32), k.dram("slots_src", [P * COLS, NF], I32)
        table = k.dram("table", [NP_, TW])
        table7 = k.dram("table7", [NP_, NTYPE * D])
        wrow_d = k.dram("wrow", [NT, P])

        load_state(k, A)
        k.end_stage()
        sort_edges(k, A, A["src"], A["dst"], slots_s, meta_s, bt_s, "src")
        k.end_stage()
        sort_edges(k, A, A["dst"], A["src"], slots_d, meta_d, bt_d, "dst")
        k.end_stage()
        type_weights(k, meta_s, bt_s, wedge)
        k.end_stage()

        layer_norm(k)
        k.end_stage()
        linear_to_table(k, A["g0_w"], None, table, D, attention=A["g0_a"])
        k.end_stage()
        with ExitStack() as part:
            psb, _ = tensors(nc, part)
            acc, scale = psb("acc", [P, NT, TW]), psb("scale", [P, NT])
            attention_aggregate(k, meta_d, bt_d, table, acc, scale)
            k.end_stage()
            attention_finish(k, acc, scale)
            k.end_stage()
        with ExitStack() as part:
            psb, _ = tensors(nc, part)
            k.gates = psb("gates", [32, NP_ + P])
            with nc.Block() as block:
                @block.vector
                def _(dve):
                    dve.memset(k.gates[:], 0.0)

            layer_norm(k)
            k.end_stage()
            gates(k, (A["f0_rw"], A["f0_rb"]), 32, "top1")
            k.end_stage()

            def finish0(dve, t, po):
                dve.scalar_tensor_tensor(out=k.x[:, ds(t, 1), :], in0=po, scalar=0.0, in1=k.x[:, ds(t, 1), :],
                                         op0=ALU.max, op1=ALU.add)
            feed_forward(k, 16, A["f0_w1"], A["f0_b1"], ACT.Relu, 32, sel0, A["f0_w2"], A["f0_b2"], finish0)
            k.end_stage()

        layer_norm(k)
        k.end_stage()
        linear_to_table(k, A["g1_w"], None, table7, NTYPE * D)
        k.end_stage()
        with ExitStack() as part:
            psb, _ = tensors(nc, part)
            acc = psb("acc", [P, NT, TW])
            aggregate(k, meta_s, bt_s, F_TYPED, table7.rearrange("n (t d) -> (n t) d", t=NTYPE), wedge, acc)
            k.end_stage()
            add_sums(k, acc)
            k.end_stage()
        with ExitStack() as part:
            psb, _ = tensors(nc, part)
            k.gates = psb("gates", [32, NP_ + P])
            with nc.Block() as block:
                @block.vector
                def _(dve):
                    dve.memset(k.gates[:], 0.0)
            layer_norm(k)
            k.end_stage()
            gates(k, (A["m1_gw"], A["m1_gb"]), 4, "soft2")
            k.end_stage()
            shared_and_experts(k, A)
            k.end_stage()

        layer_norm(k)
        k.end_stage()
        linear_to_table(k, A["g2_w"], A["g2_b"], table, D, last_one=True)
        k.end_stage()
        with ExitStack() as part:
            psb, _ = tensors(nc, part)
            acc = psb("acc", [P, NT, TW])
            aggregate(k, meta_s, bt_s, F_OTHER, table, None, acc)
            k.end_stage()
            add_sums(k, acc)
            k.end_stage()
        with ExitStack() as part:
            psb, _ = tensors(nc, part)
            k.gates = psb("gates", [32, NP_ + P])
            with nc.Block() as block:
                @block.vector
                def _(dve):
                    dve.memset(k.gates[:], 0.0)
            layer_norm(k)
            k.end_stage()
            gates(k, (A["f2_rw"], None), 8, "share2")
            k.end_stage()

            def finish2(dve, t, po):
                dve.tensor_tensor(k.y[:, ds(t, 1), :], k.y[:, ds(t, 1), :], po, ALU.add)
                dve.drain()
                dve.tensor_tensor(k.x[:, ds(t, 1), :], k.x[:, ds(t, 1), :], k.y[:, ds(t, 1), :], ALU.add)
            feed_forward(k, 16, A["f2_w1"], A["f2_b1"], ACT.Gelu, 8, sel2, A["f2_w2"], A["f2_b2"], finish2)
            k.end_stage()

        layer_norm(k)
        k.end_stage()
        with ExitStack() as part:
            psb, _ = tensors(nc, part)
            acc = psb("acc", [P, NT, TW])
            for w, b, last in (("g3_w1", "g3_b1", False), ("g3_w2", "g3_b2", True)):
                linear_to_table(k, A[w], None, table, D, last_one=True)
                k.end_stage()
                aggregate(k, meta_d, bt_d, F_OTHER, table, None, acc)
                k.end_stage()
                means_to_table(k, acc, table)
                k.end_stage()
                aggregate(k, meta_s, bt_s, F_OTHER, table, None, acc)
                k.end_stage()
                hyper_activation(k, A, acc, b, last)
                k.end_stage()

        graph.close()

        layer_norm(k)
        k.end_stage()
        with ExitStack() as part:
            psb, _ = tensors(nc, part)
            wt = psb("wt", [P, NT, 1])
            k.z = psb("z", [P, NT, D])
            chosen_tokens(k, A, wt, wrow_d)
            k.end_stage()
            wall = psb("wall", [P, N])
            after = psb("after", [P, 2 * NP_], mybir.dt.bfloat16)
            mask = psb("mask", [P, N], mybir.dt.bfloat16)
            above = psb("above", [P, NT, 2])
            got = k.dma_sem("rank_got")
            with nc.Block() as block:
                @block.sync
                def _(sp):
                    sp.dma_start(wall[:], wrow_d.rearrange("t p -> (t p)").unsqueeze(0)[:, 0:N].broadcast_to([P, N])).then_inc(got, 16)
                    sp.dma_start(after[:], A["before"]).then_inc(got, 16)

            def rank(dve):
                dve.wait_ge(got, 32)
                with dve.Fori(0, NT) as t:
                    dve.tensor_scalar(mask[:], wall[:], wt[:, ds(t, 1), :].rearrange("p t o -> p (t o)"), 0.0,
                                      ALU.is_gt, ALU.add, accum_out=above[:, ds(t, 1), 0:1].rearrange("p t o -> p (t o)"))
                    dve.drain()
                    dve.scalar_tensor_tensor(out=mask[:], in0=wall[:], scalar=wt[:, ds(t, 1), :].rearrange("p t o -> p (t o)"),
                                             in1=after[:, ds(NP_ - t * P, N)], op0=ALU.is_equal, op1=ALU.mult,
                                             accum_out=above[:, ds(t, 1), 1:2].rearrange("p t o -> p (t o)"))
                    dve.drain()
                dve.tensor_tensor(above[:, :, 0:1], above[:, :, 0:1], above[:, :, 1:2], ALU.add)
                dve.drain()
                dve.tensor_scalar(above[:, :, 0:1], above[:, :, 0:1], float(CHOSEN), None, ALU.is_lt)
                dve.drain()
                dve.tensor_tensor(wt[:], wt[:], above[:, :, 0:1], ALU.mult)
            feed_forward(k, 8, A["f3_w1"], A["f3_b1"], ACT.Gelu_apprx_tanh, 1, None, A["f3_w2"], A["f3_b2"], None, rank=rank)
            k.end_stage()
            with nc.Block() as block:
                @block.vector
                def _(dve):
                    dve.tensor_tensor(k.z[:], k.z[:], wt[:].broadcast_to([P, NT, D]), ALU.mult)
                    dve.tensor_tensor(k.x[:], k.x[:], k.y[:], ALU.add)
                    dve.drain()
                    dve.tensor_tensor(k.x[:], k.x[:], k.z[:], ALU.add)
        dump(k, out)


def dump(k, out):
    stored = k.dma_sem("stored")
    with k.nc.Block() as block:
        @block.sync
        def _(sp):
            sp.dma_start(out[0:(NT - 1) * P, :].rearrange("(t p) d -> p t d", p=P), k.x[:, 0:NT - 1, :]).then_inc(stored, 16)
            sp.dma_start(out[(NT - 1) * P:N, :], k.x[0:NTAIL, NT - 1, :]).then_inc(stored, 16)
            sp.wait_ge(stored, 32)


def constants():
    c = np.zeros((P, C_END), np.float32)
    c[:, C_ID:C_ID + P] = np.eye(P)
    c[:, C_IOTA:C_IOTA + P] = np.arange(P)
    c[:, C_TRI:C_TRI + P] = np.triu(np.ones((P, P)), 1)
    c[:, C_ONES:C_ONES + P] = 1.0
    c[:, C_TILE:C_TILE + COLS] = np.arange(COLS)
    r = np.arange(16 * P)
    for e in range(32):
        c[e, C_SEL0:C_SEL1] = r // 64 == e
    for e in range(4):
        c[e, C_SEL1:C_SEL2] = r[:2 * P] // 64 == e
    for e in range(8):
        c[e, C_SEL2:C_END] = r // D == e
    return c


def kernel(**inputs):
    import concourse.bacc as _bacc
    import ml_dtypes
    from concourse.bass_utils import run_bass_kernel_spmd as _run

    g = {n: np.asarray(v) for n, v in inputs.items()}

    def rows(w):
        return w.reshape(-1, P, w.shape[-1]).transpose(1, 0, 2)

    def column(b):
        return b.reshape(-1, P).T

    def spread(b):
        return np.broadcast_to(b.reshape(1, -1), (P, b.size))

    ew2 = np.zeros((P, 6, P), np.float32)
    ew2[:, 0:2] = rows(g["L1_ffn_sW2"])
    for e in range(4):
        ew2[:, 2 + e, 64 * (e % 2):64 * (e % 2) + 64] = g["L1_ffn_eW2"][e]
    arrays = {
        "consts": constants(),
        "before": (np.arange(2 * NP_)[None, :] - NP_ < np.arange(P)[:, None]).astype(ml_dtypes.bfloat16),
        "x": g["x"], "src": g["src"], "dst": g["dst"], "etype": g["edge_type_7"],
        "eweight": g["edge_weight"].view(np.int32),
        "g0_w": rows(g["L0_gnn_W"].transpose(1, 0, 2).reshape(D, D)),
        "g0_a": np.stack([spread(g["L0_gnn_a_src"]), spread(g["L0_gnn_a_dst"])], 1),
        "f0_rw": rows(g["L0_ffn_router_w"].T), "f0_rb": g["L0_ffn_router_b"][None],
        "f0_w1": rows(g["L0_ffn_W1"].transpose(1, 0, 2).reshape(D, -1)), "f0_b1": column(g["L0_ffn_b1"]),
        "f0_w2": rows(g["L0_ffn_W2"].reshape(-1, D)), "f0_b2": g["L0_ffn_b2"],
        "g1_w": rows(g["L1_gnn_weights"].reshape(NTYPE, D, D).transpose(1, 0, 2).reshape(D, -1)),
        "m1_w1": rows(np.concatenate([g["L1_ffn_sW1"], g["L1_ffn_eW1"].transpose(1, 0, 2).reshape(D, -1)], 1)),
        "m1_b1": column(np.concatenate([g["L1_ffn_sb1"], g["L1_ffn_eb1"].reshape(-1)])),
        "m1_w2": ew2, "m1_b2": column(np.concatenate([g["L1_ffn_sb2"], g["L1_ffn_eb2"].reshape(-1)])),
        "m1_w3": rows(np.concatenate([g["L1_ffn_sW3"], g["L1_ffn_eW3"].reshape(-1, D)], 0)),
        "m1_b3": g["L1_ffn_eb3"], "m1_sb3": g["L1_ffn_sb3"][None],
        "m1_gw": rows(g["L1_ffn_gW"]), "m1_gb": g["L1_ffn_gb"][None],
        "g2_w": rows(g["L2_gnn_W"].T), "g2_b": g["L2_gnn_b"][None],
        "f2_rw": rows(g["L2_ffn_router_w"].T),
        "f2_w1": rows(g["L2_ffn_w1"].transpose(1, 0, 2).reshape(D, -1)), "f2_b1": column(g["L2_ffn_b1"]),
        "f2_w2": rows(g["L2_ffn_w2"].reshape(-1, D)), "f2_b2": g["L2_ffn_b2"],
        "g3_w1": rows(g["L3_gnn_W1"]), "g3_w2": rows(g["L3_gnn_W2"]),
        "g3_b1": spread(g["L3_gnn_b1"]), "g3_b2": spread(g["L3_gnn_b2"]), "g3_a": spread(g["L3_gnn_a"]),
        "f3_wr": rows(g["L3_ffn_wr"]), "f3_br": g["L3_ffn_br"][None],
        "f3_w1": rows(g["L3_ffn_w1"]), "f3_b1": column(g["L3_ffn_b1"]),
        "f3_w2": rows(g["L3_ffn_w2"]), "f3_b2": g["L3_ffn_b2"][None],
    }
    nc = _bacc.Bacc("TRN2", target_bir_lowering=False, num_devices=1)
    args = {}
    for name, a in arrays.items():
        arrays[name] = a = np.ascontiguousarray(a)
        args[name] = nc.dram_tensor(f"in_{name}", a.shape, mybir.dt.from_np(a.dtype), kind="ExternalInput").ap()
    out = nc.dram_tensor("out", (N, D), F32, kind="ExternalOutput").ap()
    build(nc, args, out)
    r = _run(nc, [{f"in_{n}": a for n, a in arrays.items()}], core_ids=[0])
    return r.results[0]["out"]
```

```python
from contextlib import ExitStack

import numpy as np
import concourse.bass as bass
from concourse import mybir

F32 = mybir.dt.float32
I32 = mybir.dt.int32
BF16 = mybir.dt.bfloat16
ALU = mybir.AluOpType
ACT = mybir.ActivationFunctionType
AX = mybir.AxisListType

P = 128
N = 3125
D = 256
NT = -(-N // P)
NP_ = NT * P
NTAIL = N - (NT - 1) * P
KC = D // P
E = 53125
EC = 416
EFULL = E // EC
ETAIL = E - EFULL * EC
HALF = 10
GROUP = 2 * HALF
TILES = -(-((E + NT * (P - 1)) // P) // GROUP) * GROUP
STEPS = TILES // GROUP
COLS = TILES + 16
NF = 8
F_OTHER, F_TYPED, F_LOCAL, F_WEIGHT, F_TYPE = range(5)
NTYPE = 7
HEADS = 4
HD = D // HEADS
TW = D + HEADS
PADKEY = NP_
LOWEST = -1.0e30
SCB = 16
SCL = EC // (2 * SCB)

C_ID, C_IOTA, C_TRI, C_ONES, C_TILE = 0, P, 3 * P, 4 * P, 5 * P
C_END = C_TILE + COLS


def ds(a, n):
    return bass.ds(a, n)


def peeled(engine, count, body):
    body(0)
    with engine.Fori(1, count) as i:
        body(i)


def by_parity(engine, body):
    with engine.Fori(0, NT // 2) as i:
        for h in range(2):
            body(i * 2 + h, h)
    if NT % 2:
        body(NT - 1, 0)


def wait(engine, semaphore, value):
    if not (isinstance(value, int) and value <= 0):
        engine.wait_ge(semaphore, value)


class Kit:

    def __init__(self, nc, ctx):
        self.nc, self.ctx, self.n = nc, ctx, 0
        self.stage_sems = []

    def sem(self, name):
        self.n += 1
        self.stage_sems.append(self.nc.alloc_semaphore(name=f"{name}_{self.n}"))
        return self.stage_sems[-1]

    def dma_sem(self, name):
        self.n += 1
        return self.ctx.enter_context(self.nc.semaphore(f"{name}_{self.n}"))

    def end_stage(self):
        self.nc.all_engine_barrier()
        self.nc.clear_and_free_semaphores(self.stage_sems)
        self.nc.all_engine_barrier()
        self.stage_sems = []

    def dram(self, name, shape, dt=F32):
        return self.nc.dram_tensor(name, shape, dt).ap()


def run(k, *parts):
    with k.nc.Block() as block:
        for name, register in (("sync", block.sync), ("gpsimd", block.gpsimd), ("tensor", block.tensor),
                               ("scalar", block.scalar), ("vector", block.vector)):
            programs = [p[name] for p in parts if name in p]
            if programs:
                def program(engine, programs=programs):
                    for n, f in enumerate(programs):
                        if n:
                            engine.drain()
                        f(engine)
                register(program)
    k.end_stage()


def tensors(nc, ctx):
    mark = nc.next_id() if callable(nc.next_id) else nc.next_id

    def sb(name, shape, dt=F32):
        return ctx.enter_context(nc.sbuf_tensor(f"{name}_{mark}", shape, dt))

    def ps(name, shape, dt=F32):
        return ctx.enter_context(nc.psum_tensor(f"{name}_{mark}", shape, dt))
    return sb, ps


def load_state(k, A):
    loaded, zeroed = k.dma_sem("loaded"), k.sem("zeroed")
    with k.nc.Block() as block:
        @block.vector
        def _(dve):
            dve.memset(k.x[:, NT - 1:NT, :], 0.0)
            dve.memset(k.yT[:, :, NP_:], 0.0).then_inc(zeroed, 1)

        @block.sync
        def _(sp):
            sp.dma_start(k.const[:], A["consts"]).then_inc(loaded, 16)
            sp.dma_start(k.x[:, 0:NT - 1, :],
                         A["x"][0:(NT - 1) * P, :].rearrange("(t p) d -> p t d", p=P)).then_inc(loaded, 16)
            sp.wait_ge(zeroed, 1)
            sp.dma_start(k.x[0:NTAIL, NT - 1, :], A["x"][(NT - 1) * P:N, :]).then_inc(loaded, 16)
            sp.wait_ge(loaded, 48)


class Sorting:

    def __init__(self, k, ctx, tag, slots, meta, btile, start):
        nc = k.nc
        self.tag, self.slots, self.meta, self.btile, self.start = tag, slots, meta, btile, start
        self.loaded, self.blank, self.back = (k.dma_sem(f"{s}_{tag}") for s in ("loaded", "blank", "back"))
        self.scattered = [k.dma_sem(f"scattered{h}_{tag}") for h in range(2)]
        sb, ps = tensors(nc, ctx)
        self.pay = sb("pay", [P, EC, NF], I32)
        self.row = sb("row", [P, EC], I32)
        self.local = sb("local", [P, EC])
        self.stage = [sb(f"stage{h}", [P, SCB, NF], I32) for h in range(2)]
        self.sidx = [sb(f"sidx{h}", [P, SCB], I32) for h in range(2)]

    def renew(self, k):
        self.filled, self.totals, self.prefix, self.staged, self.gate = (
            k.sem(f"{s}_{self.tag}") for s in ("filled", "totals", "prefix", "staged", "gate"))


def rank_edges(k, ctx, A, S, key, other, scratch):
    NB = NT + 1
    sb, ps = tensors(k.nc, ctx)
    raw, bint, coli, bucket, one, mask, incl, within = scratch
    total, ntile, tincl, base = (sb(n, [P, NB]) for n in ("total", "ntile", "tincl", "base"))
    cnti = sb("cnti", [P, NB], I32)
    bt = sb("bt", [P, COLS])
    psx = ps("psx", [P, 2, NB])
    pay = S.pay
    payf = pay[:].bitcast(F32)
    meta = S.meta[:]

    def sync(sp):
        sp.wait_ge(S.filled, 1)
        sp.dma_start(S.slots.rearrange("(p c) f -> p c f", p=P), meta).then_inc(S.blank, 16)
        for i, a in enumerate((key, other, A["etype"], A["eweight"])):
            sp.dma_start(raw[0:EFULL, i, :], a[0:EFULL * EC].rearrange("(p c) -> p c", c=EC)).then_inc(S.loaded, 16)
            sp.dma_start(raw[EFULL:EFULL + 1, i, 0:ETAIL],
                         a[EFULL * EC:E].rearrange("(p c) -> p c", p=1)).then_inc(S.loaded, 16)

    def tensor(pe):
        pe.wait_ge(S.totals, 1)
        pe.matmul(psx[:, 0, :], k.tri, total[:], start=True, stop=True)
        pe.matmul(psx[:, 1, :], k.ones, total[:], start=True, stop=True).then_inc(S.prefix, 1)

    def vector(dve):
        dve.memset(raw[:, 1:4, :], 0)
        dve.memset(raw[:, 0, :], PADKEY)
        dve.memset(meta, 0)
        dve.drain()
        dve.memset(meta.bitcast(F32)[:, :, F_LOCAL:F_LOCAL + 1], -1.0)
        dve.drain().then_inc(S.filled, 1)
        dve.memset(within[:], -1.0)
        dve.memset(one[:], 1.0)
        dve.memset(pay[:], 0)
        dve.memset(bt[:], 0.0)
        dve.drain()
        dve.wait_ge(S.loaded, 128)
        dve.tensor_scalar(bint[:], raw[:, 0, :], 7, None, ALU.arith_shift_right)
        dve.tensor_scalar(coli[:], raw[:, 0, :], P - 1, None, ALU.bitwise_and)
        dve.tensor_copy(pay[:, :, F_OTHER], raw[:, 1, :])
        dve.scalar_tensor_tensor(out=pay[:, :, F_TYPED], in0=raw[:, 1, :], scalar=float(NTYPE),
                                 in1=raw[:, 2, :], op0=ALU.mult, op1=ALU.add)
        dve.tensor_copy(payf[:, :, F_TYPE], raw[:, 2, :])
        dve.tensor_copy(pay[:, :, F_WEIGHT], raw[:, 3, :])
        dve.drain()
        dve.tensor_copy(bucket[:], bint[:])
        dve.drain()
        dve.tensor_scalar(mask[:], bucket[:], float(NT), float(-P), ALU.is_equal, ALU.mult)
        dve.drain()
        dve.tensor_tensor(S.local[:], mask[:], coli[:], ALU.add)
        dve.drain()
        dve.tensor_copy(payf[:, :, F_LOCAL], S.local[:])
        with dve.Fori(0, NB) as b:
            dve.tensor_scalar(mask[:], bucket[:], k.iota[:, ds(b, 1)], None, ALU.is_equal)
            dve.drain()
            dve.tensor_tensor_scan(incl[:], one[:], mask[:], 0.0, ALU.mult, ALU.add)
            dve.drain()
            dve.tensor_copy(total[:, ds(b, 1)], incl[:, EC - 1:EC])
            dve.tensor_tensor(mask[:], mask[:], incl[:], ALU.mult)
            dve.drain()
            dve.tensor_tensor(within[:], within[:], mask[:], ALU.add)
            dve.drain()
        dve.drain().then_inc(S.totals, 1)
        dve.wait_ge(S.prefix, 1)
        dve.tensor_scalar(cnti[:], psx[:, 1, :], float(P - 1), None, ALU.add)
        dve.drain()
        dve.tensor_scalar(cnti[:], cnti[:], 7, None, ALU.arith_shift_right)
        dve.drain()
        dve.tensor_scalar(ntile[:], cnti[:], 1.0, None, ALU.max)
        dve.drain()
        dve.tensor_tensor_scan(tincl[:], one[:, 0:NB], ntile[:], 0.0, ALU.mult, ALU.add)
        dve.drain()
        dve.tensor_tensor(S.start[:], tincl[:], ntile[:], ALU.subtract)
        dve.drain()
        dve.scalar_tensor_tensor(out=base[:], in0=S.start[:], scalar=float(P), in1=psx[:, 0, :],
                                 op0=ALU.mult, op1=ALU.add)
        dve.drain()
        with dve.Fori(0, NB) as b:
            dve.tensor_scalar(mask[:], bucket[:], k.iota[:, ds(b, 1)], base[:, ds(b, 1)],
                              ALU.is_equal, ALU.mult)
            dve.drain()
            dve.tensor_tensor(within[:], within[:], mask[:], ALU.add)
            dve.drain()
        dve.tensor_copy(bint[:], within[:])
        dve.drain()
        dve.tensor_scalar(S.row[:], bint[:], P - 1, None, ALU.bitwise_and)
        dve.tensor_scalar(coli[:], bint[:], 7, None, ALU.arith_shift_right)
        dve.drain()
        dve.scalar_tensor_tensor(out=S.row[:], in0=S.row[:], scalar=float(COLS), in1=coli[:],
                                 op0=ALU.mult, op1=ALU.add)
        with dve.Fori(1, NT) as b:
            dve.scalar_tensor_tensor(out=bt[:], in0=k.tile_iota, scalar=S.start[:, ds(b, 1)], in1=bt[:],
                                     op0=ALU.is_ge, op1=ALU.add)
            dve.drain()
        dve.tensor_copy(S.btile[:], bt[0:1, :])
    return {"sync": sync, "tensor": tensor, "vector": vector}


def scatter_edges(k, S):
    def gpsimd(pool):
        pool.wait_ge(S.blank, 16)

        def step(i):
            for h in range(2):
                c = i * (2 * SCB) + h * SCB
                wait(pool, S.scattered[h], i * (16 * SCB))
                pool.tensor_copy(S.stage[h][:], S.pay[:, ds(c, SCB), :])
                pool.tensor_copy(S.sidx[h][:], S.row[:, ds(c, SCB)]).then_inc(S.staged, 1)
                pool.wait_ge(S.staged, i * 2 + h + 1)
                pool.sem_inc(S.gate, 1)
                for c in range(SCB):
                    pool.indirect_dma_start(
                        out=S.slots, out_offset=bass.IndirectOffsetOnAxis(ap=S.sidx[h][:, c:c + 1], axis=0),
                        in_=S.stage[h][:, c, :], in_offset=None).then_inc(S.scattered[h], 16)
        peeled(pool, SCL, step)

    def sync(sp):
        sp.wait_ge(S.blank, 16)
        for h in range(2):
            sp.wait_ge(S.scattered[h], 16 * SCB * SCL)
        sp.dma_start(S.meta[:], S.slots.rearrange("(p c) f -> p c f", p=P)).then_inc(S.back, 16)
        sp.wait_ge(S.back, 16)
    return {"gpsimd": gpsimd, "sync": sync}


def count_types(k, ctx, S, raw, inv):
    sb, ps = tensors(k.nc, ctx)
    W = NT * NTYPE
    B = 8
    typed = sb("typed", [P, EC])
    bint = sb("tbint", [P, EC], I32)
    iob = sb("iob", [P, 2 * P], BF16)
    oh = [sb(f"coh{h}", [P, B, P], BF16) for h in range(2)]
    th = [sb(f"cth{h}", [P, B, W], BF16) for h in range(2)]
    zero = sb("zero", [P, P], BF16)
    pc = ps("pcount", [P, 512])
    hot, used = k.sem("count_hot"), k.sem("count_used")

    def tensor(pe):
        pe.wait_ge(hot, 1)
        pe.matmul(pc[:, 0:W], zero[:], th[0][:, 0, :], start=True, stop=False).then_inc(used, 2)
        with pe.Fori(0, EC // (2 * B)) as i:
            for h in range(2):
                pe.wait_ge(hot, i * 2 + h + 2)
                for j in range(B):
                    mm = pe.matmul(pc[:, 0:W], oh[h][:, j, :], th[h][:, j, :], start=False, stop=False)
                mm.then_inc(used, 1)
        pe.matmul(pc[:, 0:W], zero[:], th[0][:, 0, :], start=False, stop=True).then_inc(used, 1)

    def vector(dve):
        dve.tensor_scalar(bint[:], raw[:, 0, :], 7, None, ALU.arith_shift_right)
        dve.memset(zero[:], 0.0)
        dve.memset(th[0][:], 0.0)
        dve.tensor_copy(iob[:], k.iota256)
        dve.drain().then_inc(hot, 1)
        dve.scalar_tensor_tensor(out=typed[:], in0=bint[:], scalar=float(NTYPE), in1=raw[:, 2, :],
                                 op0=ALU.mult, op1=ALU.add)
        dve.drain()
        with dve.Fori(0, EC // (2 * B)) as i:
            for h in range(2):
                dve.wait_ge(used, i * 2 + h + 1)
                for j in range(B):
                    c = i * (2 * B) + h * B + j
                    dve.tensor_scalar(oh[h][:, j, :], iob[:, 0:P], S.local[:, ds(c, 1)], None, ALU.is_equal)
                    mm = dve.tensor_scalar(th[h][:, j, :], iob[:, 0:W], typed[:, ds(c, 1)], None, ALU.is_equal)
                mm.then_inc(hot, 1)
        dve.wait_ge(used, EC // B + 3)
        dve.tensor_scalar(inv[:].rearrange("p t c -> p (t c)"), pc[:, 0:W], 1.0, None, ALU.max)
        dve.drain()
        dve.reciprocal(inv[:], inv[:])
    return {"tensor": tensor, "vector": vector}


def layer_norm(k, ctx, keep=True):
    nc = k.nc
    norm, turned, taken = k.sem("ln_norm"), k.sem("ln_turned"), k.sem("ln_taken")
    var, root, moved = k.sem("ln_var"), k.sem("ln_root"), k.sem("ln_moved")
    sb, ps = tensors(nc, ctx)
    stats = sb("stats", [P, NT, 6])
    aggr = sb("aggr", [P, NT, 2])
    rstd = sb("rstd", [P, NT])
    pst = ps("pst", [P, 2, 4, P])
    tile = [sb(f"tile{h}", [P, 1, D]) for h in range(2)]

    def vector(dve):
        with dve.Fori(0, NT) as t:
            dve.bn_stats(stats[:, ds(t, 1), :], k.x[:, ds(t, 1), :])
        dve.drain()
        dve.tensor_tensor(aggr[:, :, 0], stats[:, :, 1], stats[:, :, 4], ALU.add)
        dve.tensor_tensor(aggr[:, :, 1], stats[:, :, 1], stats[:, :, 4], ALU.subtract)
        dve.tensor_tensor(rstd[:], stats[:, :, 2], stats[:, :, 5], ALU.add)
        dve.drain()
        dve.tensor_scalar(aggr[:, :, 0], aggr[:, :, 0], 0.5, None, ALU.mult)
        dve.scalar_tensor_tensor(out=aggr[:, :, 1], in0=aggr[:, :, 1], scalar=0.25, in1=aggr[:, :, 1],
                                 op0=ALU.mult, op1=ALU.mult)
        dve.drain()
        dve.scalar_tensor_tensor(out=rstd[:], in0=rstd[:], scalar=1.0 / D, in1=aggr[:, :, 1],
                                 op0=ALU.mult, op1=ALU.add)
        dve.drain()
        dve.tensor_scalar(rstd[:], rstd[:], 1e-5, None, ALU.add).then_inc(var, 1)
        dve.wait_ge(root, 1)
        dve.reciprocal(rstd[:], rstd[:])
        dve.drain()

        def normalize(t, h):
            dve.wait_ge(turned, t + 1)
            if keep:
                dve.wait_ge(moved, t + 1)
            dve.tensor_scalar(tile[h][:], k.x[:, ds(t, 1), :], aggr[:, ds(t, 1), 0:1],
                              rstd[:, ds(t, 1)], ALU.subtract, ALU.mult).then_inc(norm, 1)
        by_parity(dve, normalize)

    def gpsimd(pool):
        pool.sem_inc(moved, 2)

        def move(t, h):
            pool.wait_ge(norm, t + 1)
            pool.tensor_copy(k.y[:, ds(t, 1), :], tile[h][:]).then_inc(moved, 1)
        by_parity(pool, move)

    def tensor(pe):
        turn_loop(k, pe, tile, pst, norm, turned, taken)

    def scalar(act):
        act.wait_ge(var, 1)
        act.activation(rstd[:], rstd[:], ACT.Sqrt).then_inc(root, 1)
        take_loop(k, act, pst, turned, taken)
    return {"vector": vector, "tensor": tensor, "scalar": scalar} | ({"gpsimd": gpsimd} if keep else {})


def turn_loop(k, pe, src, pst, ready, turned, taken):
    pe.sem_inc(turned, 2)

    def turn(t, h):
        pe.wait_ge(ready, t + 1)
        pe.wait_ge(taken, t + 1)
        for c in range(KC):
            mm = pe.transpose(pst[:, h, c, :], src[h][:, 0, c * P:(c + 1) * P], k.ident)
        mm.then_inc(turned, 1)
    by_parity(pe, turn)


def take_loop(k, act, pst, turned, taken):
    act.sem_inc(taken, 2)

    def take(t, h):
        act.wait_ge(turned, t + 3)
        act.activation(k.yT[:, :, ds(t * P, P)], pst[:, h, 0:KC, :], ACT.Copy).then_inc(taken, 1)
    by_parity(act, take)


def stage_yT(k, act, yt, kept, moved):
    for t in range(2):
        act.activation(yt[t][:], k.yT[:, :, t * P:(t + 1) * P], ACT.Copy).then_inc(moved, 1)
    with act.Fori(1, NT // 2) as i:
        for h in range(2):
            act.wait_ge(kept, i * 2 + h - 1)
            act.activation(yt[h][:], k.yT[:, :, ds((i * 2 + h) * P, P)], ACT.Copy).then_inc(moved, 1)
    act.wait_ge(kept, NT - 2)
    act.activation(yt[0][:], k.yT[:, :, (NT - 1) * P:NT * P], ACT.Copy).then_inc(moved, 1)


def linear_to_table(k, ctx, weights, bias, table, width, attention=None, last_one=False):
    nc = k.nc
    loaded, stored = k.dma_sem("lin_loaded"), [k.dma_sem(f"lin_stored{h}") for h in range(2)]
    prod, kept = k.sem("lin_prod"), k.sem("lin_kept")
    moved = k.sem("lin_moved")
    nblk = -(-width // 512)
    bw = width // nblk
    tw = TW if (attention is not None or last_one) else width
    sb, ps = tensors(nc, ctx)
    w = sb("w", [P, KC, width])
    b = sb("b", [1, width]) if bias is not None else None
    row = [sb(f"row{h}", [P, tw]) for h in range(2)]
    if attention is not None:
        att = sb("att", [P, 2, D])
        prodt = sb("prodt", [P, 2, D])
    acc = [ps(f"acc{h}", [P, nblk, 512]) for h in range(2)]
    yt = [sb(f"yt{h}", [P, KC, P]) for h in range(2)]
    def scalar(act):
        stage_yT(k, act, yt, kept, moved)

    def sync(sp):
        sp.dma_start(w[:], weights).then_inc(loaded, 16)
        n = 16
        if bias is not None:
            sp.dma_start(b[:], bias).then_inc(loaded, 16)
            n += 16
        if attention is not None:
            sp.dma_start(att[:], attention).then_inc(loaded, 16)
            n += 16
        sp.wait_ge(loaded, n)
        with sp.Fori(0, NT // 2) as i:
            for h in range(2):
                sp.wait_ge(kept, i * 2 + h + 1)
                sp.dma_start(table[ds((i * 2 + h) * P, P), :], row[h][:]).then_inc(stored[h], 16)
        sp.wait_ge(kept, NT)
        sp.dma_start(table[(NT - 1) * P:NT * P, :], row[0][:]).then_inc(stored[0], 16)
        sp.wait_ge(stored[0], 16 * (NT // 2 + 1))
        sp.wait_ge(stored[1], 16 * (NT // 2))

    def tensor(pe):
        pe.wait_ge(loaded, 16 * (1 + (bias is not None) + (attention is not None)))

        def product(t, h):
            pe.wait_ge(moved, t + 1)
            for j in range(nblk):
                for c in range(KC):
                    mm = pe.matmul(acc[h][:, j, 0:bw], yt[h][:, c, :],
                                   w[:, c, j * bw:(j + 1) * bw], start=(c == 0),
                                   stop=(c == KC - 1 and bias is None))
                if bias is not None:
                    mm = pe.matmul(acc[h][:, j, 0:bw], k.ones[0:1, :], b[:, j * bw:(j + 1) * bw],
                                   start=False, stop=True)
            mm.then_inc(prod, 1)
        by_parity(pe, product)

    def vector(dve):
        if last_one:
            for h in range(2):
                dve.memset(row[h][:, D:TW], 1.0)

        def keep(t, h):
            dve.wait_ge(prod, t + 1)
            if attention is None:
                dve.tensor_copy(row[h][:, 0:width].rearrange("p (j c) -> p j c", c=bw),
                                acc[h][:, :, 0:bw]).then_inc(kept, 1)
                return
            dve.tensor_copy(row[h][:, 0:D], acc[h][:, 0, 0:D])
            for s in range(2):
                dve.tensor_tensor(prodt[:, s, :], acc[h][:, 0, 0:D], att[:, s, :], ALU.mult)
            dve.drain()
            dve.tensor_reduce(row[h][:, D:TW], prodt[:, 0, :].rearrange("p (a b) -> p a b", a=HEADS), AX.X, ALU.add)
            dve.tensor_reduce(k.ad[:, ds(t, 1), :], prodt[:, 1, :].rearrange("p (a b) -> p a b", a=HEADS), AX.X, ALU.add)
            dve.drain().then_inc(kept, 1)
        dve.wait_ge(loaded, 16 * (1 + (bias is not None) + (attention is not None)))
        keep(0, 0)
        keep(1, 1)
        with dve.Fori(1, NT // 2) as i:
            for h in range(2):
                dve.wait_ge(stored[h], i * 16)
                keep(i * 2 + h, h)
        dve.wait_ge(stored[0], 16 * (NT // 2))
        keep(NT - 1, 0)
    return {"scalar": scalar, "sync": sync, "tensor": tensor, "vector": vector}


def onehots(k, dve, out, meta, first, weight=None):
    mf = meta[:].bitcast(F32)
    local = mf[:, ds(first, HALF), F_LOCAL:F_LOCAL + 1]
    if weight is None:
        return dve.tensor_tensor(out, k.iota.unsqueeze(1).broadcast_to([P, HALF, P]),
                                 local.broadcast_to([P, HALF, P]), ALU.is_equal)
    raise ValueError


def distances(k, act, out, meta, first):
    mf = meta[:].bitcast(F32)
    for j in range(HALF):
        act.activation(out[:, j, :], k.iota, ACT.Abs, scale=-1.0, bias=mf[:, ds(first + j, 1), F_LOCAL])


def node_tiles(k, engine, btile, first, count):
    return k.nc.values_load_multi_w_load_instructions(
        btile[0:1, ds(first, count)], engines=(engine,), min_val=0, max_val=NT - 1,
        skip_runtime_bounds_check_because="a node tile is a count of NT - 1 comparisons that hold")[1]


def gather_loop(k, pool, idx, field, rows, table, rows_done, got, gate, staged):
    def step(i):
        for h in range(2):
            wait(pool, got[h], i * (16 * HALF))
            pool.tensor_copy(k.gidx[h][:], idx[:, ds(i * GROUP + h * HALF, HALF), field]).then_inc(staged, 1)
            pool.wait_ge(staged, i * 2 + h + 1)
            for j in range(HALF):
                n = h * HALF + j
                pool.wait_ge(rows_done, i * GROUP + n + 1)
                pool.sem_inc(gate, 1)
                pool.indirect_dma_start(
                    out=rows[:, n, :], out_offset=None, in_=table,
                    in_offset=bass.IndirectOffsetOnAxis(ap=k.gidx[h][:, j:j + 1], axis=0)).then_inc(got[h], 16)
    peeled(pool, STEPS, step)


def aggregate(k, meta, btile, field, table, weights, acc):
    nc = k.nc
    width = table.shape[1]
    hot, rdone, added, gate, staged, zero = (k.sem(f"agg_{s}") for s in ("onehots", "rows_done", "added", "gate", "staged", "zeroed"))
    got = [k.dma_sem(f"agg_got{h}") for h in range(2)]
    with ExitStack() as ctx:
        sb, ps = tensors(nc, ctx)
        rows = sb("rows", [P, GROUP, width])
        oh = [sb(f"oh{h}", [P, HALF, P]) for h in range(2)]
        away = sb("away", [P, HALF, P])
        if weights is not None:
            minus = sb("minus", [P, COLS])
        k.gidx = [sb(f"gidx{h}", [P, HALF], I32) for h in range(2)]
        pacc = ps("pacc", [P, 4, 512])
        with nc.Block() as block:
            @block.gpsimd
            def _(pool):
                gather_loop(k, pool, meta, field, rows, table, rdone, got, gate, staged)

            @block.tensor
            def _(pe):
                pe.sem_inc(rdone, GROUP)
                with pe.Fori(0, STEPS) as i:
                    for h in range(2):
                        pe.wait_ge(hot, i * 2 + h + 1)
                        pe.wait_ge(got[h], (i + 1) * (16 * HALF))
                        for j in range(HALF):
                            n = h * HALF + j
                            pe.wait_ge(added, i * GROUP + n + 1)
                            pe.matmul(pacc[:, n % 4, 0:width], oh[h][:, j, :], rows[:, n, :],
                                      start=True, stop=True).then_inc(rdone, 1)

            @block.scalar
            def _(act):
                if weights is not None:
                    act.activation(minus[:], weights[:], ACT.Copy, scale=-1.0)
                with act.Fori(0, STEPS) as i:
                    for h in range(2):
                        g = i * 2 + h
                        act.drain()
                        distances(k, act, away, meta, g * HALF)
                        act.drain()
                        act.wait_ge(rdone, g * HALF + HALF)
                        if weights is None:
                            mm = act.activation(oh[h][:], away[:], ACT.Relu, scale=-1.0, bias=1.0)
                        else:
                            for j in range(HALF):
                                mm = act.activation(oh[h][:, j, :], away[:, j, :], ACT.Relu,
                                                    scale=minus[:, ds(g * HALF + j, 1)],
                                                    bias=weights[:, ds(g * HALF + j, 1)])
                        mm.then_inc(hot, 1)

            @block.vector
            def _(dve):
                dve.memset(acc[:], 0.0)
                dve.sem_inc(added, 4)
                dve.drain()
                with dve.Fori(0, STEPS) as i:
                    for h in range(2):
                        bs = node_tiles(k, mybir.EngineType.DVE, btile, i * GROUP + h * HALF, HALF)
                        for j in range(HALF):
                            n = h * HALF + j
                            dve.wait_ge(rdone, i * GROUP + n + 1 + GROUP)
                            dve.wait_ge(added, i * GROUP + n + 4)
                            dve.tensor_tensor(acc[:, ds(bs[j], 1), 0:width], acc[:, ds(bs[j], 1), 0:width],
                                              pacc[:, n % 4:n % 4 + 1, 0:width], ALU.add).then_inc(added, 1)


def look_up_weights(k, ctx, meta, btile, inv, wedge):
    sb, ps = tensors(k.nc, ctx)
    hot, turn, copied, look, used = (k.sem(f"look_{s}") for s in ("hot", "turned", "copied", "looked", "used"))
    oh = [sb(f"loh{h}", [P, HALF, P]) for h in range(2)]
    th = [sb(f"lth{h}", [P, HALF, NTYPE]) for h in range(2)]
    ohT = [sb(f"lohT{h}", [P, HALF, P]) for h in range(2)]
    sel = sb("sel", [P, HALF, NTYPE])
    pc = [ps(f"plook{h}", [P, 512]) for h in range(2)]
    pT = [ps(f"plT{h}", [P, 3, 4, P]) for h in range(2)]
    mf = meta[:].bitcast(F32)

    def tensor(pe):
        def turn_group(h, g):
            pe.wait_ge(hot, g + 1)
            pe.wait_ge(copied, g + 1)
            for j in range(HALF):
                mm = pe.transpose(pT[h][:, j // 4, j % 4, :], oh[h][:, j, :], k.ident)
            mm.then_inc(turn, 1)

        def body(i, last):
            for h in range(2):
                g = i * 2 + h
                if not (last and h == 1):
                    turn_group(1 - h, g + 1)
                pe.wait_ge(copied, g + 3)
                pe.wait_ge(used, g + 1)
                for j in range(HALF):
                    b = pe.value_load(btile[0:1, ds(g * HALF + j, 1)], min_val=0, max_val=NT - 1)
                    mm = pe.matmul(pc[h][:, j * NTYPE:(j + 1) * NTYPE], ohT[h][:, j, :], inv[:, ds(b, 1), :],
                                   start=True, stop=True)
                mm.then_inc(look, 1)
        pe.sem_inc(look, 2)
        turn_group(0, 0)
        with pe.Fori(0, STEPS - 1) as i:
            body(i, False)
        body(STEPS - 1, True)

    def scalar(act):
        act.sem_inc(copied, 2)
        with act.Fori(0, STEPS) as i:
            for h in range(2):
                g = i * 2 + h
                act.wait_ge(turn, g + 1)
                act.wait_ge(look, g + 1)
                copy_turned(act, ohT[h], pT[h])
                act.drain().then_inc(copied, 1)

    def vector(dve):
        def hots(h, g):
            onehots(k, dve, oh[h][:], meta, g * HALF)
            dve.tensor_tensor(th[h][:], k.iota[:, 0:NTYPE].unsqueeze(1).broadcast_to([P, HALF, NTYPE]),
                              mf[:, ds(g * HALF, HALF), F_TYPE:F_TYPE + 1].broadcast_to([P, HALF, NTYPE]),
                              ALU.is_equal).then_inc(hot, 1)

        def body(i, last):
            for h in range(2):
                g = i * 2 + h
                dve.wait_ge(look, g + 3)
                dve.tensor_tensor(sel[:], pc[h][:, 0:HALF * NTYPE].rearrange("p (j c) -> p j c", c=NTYPE),
                                  th[h][:], ALU.mult)
                dve.drain().then_inc(used, 1)
                dve.tensor_reduce(wedge[:, ds(g * HALF, HALF)], sel[:], AX.X, ALU.add)
                if not last:
                    hots(h, g + 2)
                dve.drain()
        dve.memset(wedge[:], 0.0)
        dve.drain()
        dve.sem_inc(used, 2)
        hots(0, 0)
        hots(1, 1)
        with dve.Fori(0, STEPS - 1) as i:
            body(i, False)
        body(STEPS - 1, True)
    return {"tensor": tensor, "scalar": scalar, "vector": vector}


def copy_turned(act, out, banks):
    for q in range(2):
        act.activation(out[:, 4 * q:4 * q + 4, :], banks[:, q, :, :], ACT.Copy)
    act.activation(out[:, 8:HALF, :], banks[:, 2, 0:HALF - 8, :], ACT.Copy)


def attention_aggregate(k, meta, btile, start, table, acc):
    nc = k.nc
    rdone, added, gate, staged = (k.sem(f"att_{s}") for s in ("rows_done", "added", "gate", "staged"))
    coded, hot, turn, copied, look, eused = (
        k.sem(f"att_{s}") for s in ("coded", "hot", "turned", "copied", "looked", "eused"))
    top, topT, topr, topb, newtop, prob, msg = (
        k.sem(f"att_{s}") for s in ("top", "topT", "topr", "topb", "newtop", "prob", "msg"))
    split, last_top, factors = k.sem("att_split"), k.sem("att_last_top"), k.sem("att_factors")
    got = [k.dma_sem(f"att_got{h}") for h in range(2)]
    GROUPS = STEPS * 2
    PARTS = 3
    TERMS = PARTS * HEADS
    with ExitStack() as ctx:
        sb, ps = tensors(nc, ctx)
        rows = sb("rows", [P, GROUP, TW])
        oh = [sb(f"oh{h}", [P, HALF, P]) for h in range(2)]
        away = sb("away", [P, HALF, P], BF16)
        code = [sb(f"code{h}", [P, HALF, P], BF16) for h in range(2)]
        codeT = sb("codeT", [P, HALF, P], BF16)
        idb = sb("idb", [P, P], BF16)
        adb = sb("adb", [P, NT, TERMS], BF16)
        rest = sb("rest", [P, NT, HEADS])
        k.gidx = [sb(f"gidx{h}", [P, HALF], I32) for h in range(2)]
        term = sb("term", [P, HALF, HEADS])
        e = sb("e", [P, HALF, HEADS])
        pen = sb("pen", [P, HALF])
        mx = sb("mx", [P, 1])
        mrow = sb("mrow", [1, 1])
        ref = [sb(f"ref{h}", [P, 1]) for h in range(2)]
        nref = sb("nref", [P, 1])
        drop = sb("drop", [P, 1])
        fac = [sb(f"fac{h}", [P, 1]) for h in range(2)]
        tops = sb("tops", [P, GROUPS])
        before = sb("before", [P, GROUPS])
        scale = sb("scale", [P, NT])
        rden = sb("rden", [P, NT, HEADS])
        pT = ps("pT", [P, 2, 8, P], BF16)
        pterm = [ps(f"pterm{h}", [P, 512]) for h in range(2)]
        ptop = ps("ptop", [P, 512])
        pacc = ps("pacc", [P, 2, 512])
        mf = meta[:].bitcast(F32)

        def gpsimd(pool):
            gather_loop(k, pool, meta, F_OTHER, rows, table, rdone, got, gate, staged)

        def tensor(pe):
            def turn_group(h, g):
                pe.wait_ge(coded, g + 1)
                pe.wait_ge(copied, g + 1)
                for j in range(HALF):
                    mm = pe.transpose(pT[:, j // 8, j % 8, :], code[h][:, j, :], idb[:])
                mm.then_inc(turn, 1)

            def destinations(h, g):
                bs = node_tiles(k, mybir.EngineType.PE, btile, g * HALF, HALF)
                pe.wait_ge(copied, g + 2)
                pe.wait_ge(eused, g + 1)
                for j in range(HALF):
                    mm = pe.matmul(pterm[h][:, j * TERMS:(j + 1) * TERMS], codeT[:, j, :],
                                   adb[:, ds(bs[j], 1), :], start=True, stop=True)
                mm.then_inc(look, 1)

            def partition_tops(g):
                pe.wait_ge(top, g + 1)
                pe.transpose(ptop[0:1, 0:P], mx[:], k.ident).then_inc(topT, 1)

            def spread_top(g):
                pe.wait_ge(topr, g + 1)
                pe.matmul(ptop[:, 0:1], k.ones[0:1, :], mrow[:], start=True, stop=True).then_inc(topb, 1)

            def body(i, last):
                for h in range(2):
                    g = i * 2 + h
                    second = not (last and h == 1)
                    third = not last
                    for j in range(HALF):
                        n = h * HALF + j
                        if j == 0:
                            pe.wait_ge(hot, g + 1)
                            pe.wait_ge(msg, g + 1)
                        pe.wait_ge(added, i * GROUP + n + 1)
                        pe.matmul(pacc[:, n % 2, 0:TW], oh[h][:, j, :], rows[:, n, :],
                                  start=True, stop=True).then_inc(rdone, 1)
                        if third and j == 0:
                            turn_group(h, g + 2)
                        if second and j == 3:
                            partition_tops(g + 1)
                        if second and j == 5:
                            spread_top(g + 1)
                        if third and j == 7:
                            destinations(h, g + 2)
            pe.sem_inc(rdone, GROUP)
            pe.sem_inc(look, 1)
            turn_group(0, 0)
            pe.wait_ge(split, 1)
            destinations(0, 0)
            turn_group(1, 1)
            destinations(1, 1)
            partition_tops(0)
            spread_top(0)
            with pe.Fori(0, STEPS - 1) as i:
                body(i, False)
            body(STEPS - 1, True)

        def scalar(act):
            def encode(h, g):
                distances(k, act, away, meta, g * HALF)
                act.drain()
                act.activation(code[h][:], away[:], ACT.Relu, scale=-1.0, bias=1.0)
                act.drain().then_inc(coded, 1)

            def widen(h):
                act.activation(oh[h][:], code[h][:], ACT.Copy).then_inc(hot, 1)

            def copy_group(g):
                act.wait_ge(turn, g + 1)
                act.wait_ge(look, g + 1)
                act.activation(codeT[:, 0:8, :], pT[:, 0, :, :], ACT.Copy)
                act.activation(codeT[:, 8:HALF, :], pT[:, 1, 0:HALF - 8, :], ACT.Copy)
                act.drain().then_inc(copied, 1)

            def powers(h, g):
                act.wait_ge(newtop, g + 1)
                act.activation(rows[:, h * HALF:(h + 1) * HALF, D:TW], e[:], ACT.Exp, bias=nref[:])
                act.activation(fac[h][:], drop[:], ACT.Exp)
                act.drain().then_inc(prob, 1)

            def body(i, last):
                for h in range(2):
                    g = i * 2 + h
                    if not last:
                        copy_group(g + 2)
                    if not (last and h == 1):
                        if not last:
                            encode(1 - h, g + 3)
                        powers(1 - h, g + 1)
                    if not last:
                        act.wait_ge(rdone, i * GROUP + (h + 1) * HALF + GROUP)
                        widen(h)
            act.activation(idb[:], k.ident, ACT.Copy)
            act.sem_inc(copied, 1)
            encode(0, 0)
            widen(0)
            copy_group(0)
            encode(1, 1)
            widen(1)
            copy_group(1)
            encode(0, 2)
            powers(0, 0)
            with act.Fori(0, STEPS - 1) as i:
                body(i, False)
            body(STEPS - 1, True)
            act.wait_ge(last_top, 1)
            act.activation(scale[:], scale[:], ACT.Exp).then_inc(factors, 1)

        def vector(dve):
            def scores(i, h, g):
                dve.tensor_scalar(pen[:], mf[:, ds(g * HALF, HALF), F_LOCAL], 0.0, -LOWEST, ALU.min, ALU.mult)
                dve.wait_ge(look, g + 2)
                dve.tensor_reduce(term[:], pterm[h][:, 0:HALF * TERMS].rearrange("p (j s c) -> p j c s", s=PARTS, c=HEADS),
                                  AX.X, ALU.add)
                dve.drain().then_inc(eused, 1)
                dve.wait_ge(got[h], (i + 1) * (16 * HALF))
                dve.tensor_tensor(e[:], rows[:, h * HALF:(h + 1) * HALF, D:TW], term[:], ALU.add)
                dve.drain()
                dve.scalar_tensor_tensor(out=e[:], in0=e[:], scalar=0.2, in1=e[:], op0=ALU.mult, op1=ALU.max)
                dve.drain()
                dve.tensor_tensor(e[:], e[:], mf[:, ds(g * HALF, HALF), F_WEIGHT:F_WEIGHT + 1]
                                  .broadcast_to([P, HALF, HEADS]), ALU.mult)
                dve.drain()
                dve.tensor_tensor(e[:], e[:], pen[:].unsqueeze(2).broadcast_to([P, HALF, HEADS]), ALU.add)
                dve.drain()
                dve.tensor_reduce(mx[:], e[:], AX.XY, ALU.max).then_inc(top, 1)

            def group_top(g):
                dve.wait_ge(topT, g + 1)
                dve.tensor_reduce(mrow[:], ptop[0:1, 0:P], AX.X, ALU.max).then_inc(topr, 1)

            def new_top(h, g):
                dve.wait_ge(topb, g + 1)
                dve.tensor_tensor(ref[h][:], ref[1 - h][:], ptop[:, 0:1], ALU.max)
                dve.drain()
                dve.tensor_tensor(drop[:], ref[1 - h][:], ref[h][:], ALU.subtract)
                dve.tensor_copy(tops[:, ds(g, 1)], ref[h][:])
                dve.tensor_scalar(nref[:], ref[h][:], -1.0, None, ALU.mult)
                dve.drain().then_inc(newtop, 1)

            def messages(h, g):
                dve.wait_ge(prob, g + 1)
                part = rows[:, h * HALF:(h + 1) * HALF, :]
                dve.tensor_tensor(part[:, :, 0:D].rearrange("p j (a b) -> p j a b", a=HEADS),
                                  part[:, :, 0:D].rearrange("p j (a b) -> p j a b", a=HEADS),
                                  part[:, :, D:TW].unsqueeze(3).broadcast_to([P, HALF, HEADS, HD]),
                                  ALU.mult).then_inc(msg, 1)

            def add(i, h, j, b):
                n = h * HALF + j
                dve.wait_ge(rdone, i * GROUP + n + 1 + GROUP)
                dve.wait_ge(added, i * GROUP + n + 2)
                into, sums = acc[:, ds(b, 1), :], pacc[:, n % 2:n % 2 + 1, 0:TW]
                if j == 0:
                    dve.scalar_tensor_tensor(out=into, in0=into, scalar=fac[h][:], in1=sums,
                                             op0=ALU.mult, op1=ALU.add).then_inc(added, 1)
                else:
                    dve.tensor_tensor(into, into, sums, ALU.add).then_inc(added, 1)

            def body(i, last):
                for h in range(2):
                    g = i * 2 + h
                    ahead = not (last and h == 1)
                    bs = node_tiles(k, mybir.EngineType.DVE, btile, i * GROUP + h * HALF, HALF)
                    for j in range(HALF):
                        add(i, h, j, bs[j])
                        if ahead and j == 2:
                            scores(i + h, 1 - h, g + 1)
                        if ahead and j == 4:
                            group_top(g + 1)
                        if ahead and j == 6:
                            new_top(1 - h, g + 1)
                        if ahead and j == 8:
                            messages(1 - h, g + 1)
            dve.tensor_copy(rest[:], k.ad[:])
            dve.memset(acc[:], 0.0)
            for s in range(PARTS):
                part = adb[:, :, s * HEADS:(s + 1) * HEADS]
                dve.drain()
                dve.tensor_copy(part, rest[:])
                dve.drain()
                if s < PARTS - 1:
                    dve.tensor_tensor(rest[:], rest[:], part, ALU.subtract)
            dve.memset(ref[1][:], LOWEST)
            dve.sem_inc(added, 2)
            dve.sem_inc(eused, 2)
            dve.drain().then_inc(split, 1)
            scores(0, 0, 0)
            group_top(0)
            new_top(0, 0)
            messages(0, 0)
            with dve.Fori(0, STEPS - 1) as i:
                body(i, False)
            body(STEPS - 1, True)
            dve.drain()
            with dve.Fori(0, NT) as t:
                dve.tensor_scalar(before[:], k.tile_iota[:, 0:TILES:HALF], start[:, ds(t + 1, 1)], 1.0,
                                  ALU.is_lt, ALU.subtract)
                dve.drain()
                dve.scalar_tensor_tensor(out=before[:], in0=before[:], scalar=3.0e38, in1=tops[:],
                                         op0=ALU.mult, op1=ALU.add)
                dve.drain()
                dve.tensor_reduce(scale[:, ds(t, 1)], before[:], AX.X, ALU.max)
                dve.drain()
            dve.tensor_scalar(scale[:], scale[:], tops[:, GROUPS - 1:GROUPS], None, ALU.subtract).then_inc(last_top, 1)
            dve.wait_ge(factors, 1)
            dve.tensor_tensor(rden[:], acc[:, :, D:TW], scale[:].unsqueeze(2).broadcast_to([P, NT, HEADS]), ALU.mult)
            dve.drain()
            dve.tensor_scalar(rden[:], rden[:], 1e-10, None, ALU.add)
            dve.drain()
            dve.reciprocal(rden[:], rden[:])
            dve.drain()
            dve.tensor_tensor(rden[:], rden[:], scale[:].unsqueeze(2).broadcast_to([P, NT, HEADS]), ALU.mult)
            dve.drain()
            with dve.Fori(0, NT) as t:
                dve.tensor_tensor(acc[:, ds(t, 1), 0:D].rearrange("p t (a b) -> p (t a) b", a=HEADS),
                                  acc[:, ds(t, 1), 0:D].rearrange("p t (a b) -> p (t a) b", a=HEADS),
                                  rden[:, ds(t, 1), :].rearrange("p t a -> p (t a)").unsqueeze(2)
                                  .broadcast_to([P, HEADS, HD]), ALU.mult)
            dve.drain()
            dve.tensor_tensor(k.x[:], k.x[:], acc[:, :, 0:D], ALU.add)
        run(k, {"gpsimd": gpsimd, "tensor": tensor, "scalar": scalar, "vector": vector})


def logits(k, lg, width, weights, bias):
    nc = k.nc
    loaded = k.dma_sem("lg_loaded")
    prod, kept, moved = (k.sem(f"lg_{s}") for s in ("prod", "kept", "moved"))
    with ExitStack() as ctx:
        sb, ps = tensors(nc, ctx)
        w = sb("lw", [P, KC, width])
        b = sb("lb", [1, width]) if bias is not None else None
        pl = ps("pl", [P, 2, 512])
        nload = 16 * (1 + (bias is not None))
        yt = [sb(f"yt{h}", [P, KC, P]) for h in range(2)]
        with nc.Block() as block:
            @block.scalar
            def _(act):
                stage_yT(k, act, yt, kept, moved)

            @block.sync
            def _(sp):
                sp.dma_start(w[:], weights).then_inc(loaded, 16)
                if bias is not None:
                    sp.dma_start(b[:], bias).then_inc(loaded, 16)

            @block.tensor
            def _(pe):
                pe.wait_ge(loaded, nload)

                def product(t, h):
                    pe.wait_ge(moved, t + 1)
                    for c in range(KC):
                        mm = pe.matmul(pl[:, h, 0:width], yt[h][:, c, :], w[:, c, :],
                                       start=(c == 0), stop=(c == KC - 1 and bias is None))
                    if bias is not None:
                        mm = pe.matmul(pl[:, h, 0:width], k.ones[0:1, :], b[:], start=False, stop=True)
                    mm.then_inc(prod, 1)
                by_parity(pe, product)

            @block.vector
            def _(dve):
                dve.memset(lg[:], LOWEST)
                dve.drain()

                def keep(t, h):
                    dve.wait_ge(prod, t + 1)
                    dve.tensor_copy(lg[:, ds(t, 1), 0:width], pl[:, h:h + 1, 0:width]).then_inc(kept, 1)
                by_parity(dve, keep)


def gates(k, width, experts, kind):
    nc = k.nc
    with ExitStack() as ctx:
        sb, ps = tensors(nc, ctx)
        EP = experts
        lg = sb("lg", [P, NT, EP])
        logits(k, lg, experts, *width)
        top = sb("top", [P, NT, 2])
        second = sb("second", [P, NT, EP])
        w = sb("w", [P, NT, P])
        tmp = sb("tmp", [P, NT, EP])
        one = sb("one", [P, NT, 2])
        tile = [sb(f"tile{h}", [P, P]) for h in range(2)]
        pt = ps("pt", [P, 2, 512])
        shift, powered, diff, powd, ready, turned, taken = (
            k.sem(f"gate_{s}") for s in ("shift", "powered", "diff", "powd", "ready", "turned", "taken"))
        with nc.Block() as block:
            @block.vector
            def _(dve):
                def both(a, n):
                    return a.broadcast_to([P, NT, n])
                dve.memset(w[:], 0.0)
                if kind != "top1":
                    dve.tensor_reduce(one[:, :, 0:1], lg[:], AX.X, ALU.max)
                    dve.drain()
                    dve.tensor_tensor(lg[:], lg[:], both(one[:, :, 0:1], EP), ALU.subtract)
                    dve.drain().then_inc(shift, 1)
                    dve.wait_ge(powered, 1)
                    dve.tensor_reduce(one[:, :, 0:1], lg[:], AX.X, ALU.add)
                    dve.drain()
                    dve.reciprocal(one[:, :, 1:2], one[:, :, 0:1])
                    dve.drain()
                    dve.tensor_tensor(lg[:], lg[:], both(one[:, :, 1:2], EP), ALU.mult)
                dve.drain()
                iota = k.iota[:, 0:experts].unsqueeze(1).broadcast_to([P, NT, experts])

                def first_largest(n, values, out):
                    dve.tensor_reduce(top[:, :, n:n + 1], values, AX.X, ALU.max)
                    dve.drain()
                    dve.tensor_tensor(tmp[:], values, both(top[:, :, n:n + 1], EP), ALU.is_equal)
                    dve.drain()
                    dve.tensor_scalar(tmp[:], tmp[:], -float(P), None, ALU.mult)
                    dve.drain()
                    dve.tensor_tensor(tmp[:], tmp[:], iota, ALU.add)
                    dve.drain()
                    dve.tensor_reduce(one[:, :, 0:1], tmp[:], AX.X, ALU.min)
                    dve.drain()
                    dve.tensor_tensor(out, tmp[:], both(one[:, :, 0:1], EP), ALU.is_equal)
                    dve.drain()
                first_largest(0, lg[:], w[:, :, 0:experts])
                if kind != "top1":
                    dve.scalar_tensor_tensor(out=lg[:], in0=w[:, :, 0:experts], scalar=-2.0, in1=lg[:],
                                             op0=ALU.mult, op1=ALU.add)
                    dve.drain()
                    first_largest(1, lg[:], second[:])
                if kind == "soft2":
                    dve.tensor_tensor(one[:, :, 1:2], top[:, :, 1:2], top[:, :, 0:1], ALU.subtract)
                    dve.drain().then_inc(diff, 1)
                    dve.wait_ge(powd, 1)
                    dve.tensor_scalar(one[:, :, 0:1], one[:, :, 1:2], 1.0, None, ALU.add)
                    dve.drain()
                    dve.reciprocal(one[:, :, 0:1], one[:, :, 0:1])
                    dve.drain()
                    dve.tensor_tensor(one[:, :, 1:2], one[:, :, 1:2], one[:, :, 0:1], ALU.mult)
                elif kind == "share2":
                    dve.tensor_tensor(one[:, :, 0:1], top[:, :, 0:1], top[:, :, 1:2], ALU.add)
                    dve.drain()
                    dve.tensor_scalar(one[:, :, 0:1], one[:, :, 0:1], 1e-12, None, ALU.max)
                    dve.drain()
                    dve.reciprocal(one[:, :, 0:1], one[:, :, 0:1])
                    dve.drain()
                    dve.tensor_tensor(one[:, :, 1:2], top[:, :, 1:2], one[:, :, 0:1], ALU.mult)
                    dve.tensor_tensor(one[:, :, 0:1], top[:, :, 0:1], one[:, :, 0:1], ALU.mult)
                dve.drain()
                if kind != "top1":
                    dve.tensor_tensor(w[:, :, 0:experts], w[:, :, 0:experts], both(one[:, :, 0:1], experts), ALU.mult)
                    dve.tensor_tensor(second[:], second[:], both(one[:, :, 1:2], experts), ALU.mult)
                    dve.drain()
                    dve.tensor_tensor(w[:, :, 0:experts], w[:, :, 0:experts], second[:], ALU.add)
                    dve.drain()

                def stage(t, h):
                    dve.wait_ge(turned, t + 1)
                    dve.tensor_copy(tile[h][:].unsqueeze(1), w[:, ds(t, 1), :]).then_inc(ready, 1)
                by_parity(dve, stage)

            @block.scalar
            def _(act):
                if kind != "top1":
                    act.wait_ge(shift, 1)
                    act.activation(lg[:], lg[:], ACT.Exp).then_inc(powered, 1)
                if kind == "soft2":
                    act.wait_ge(diff, 1)
                    act.activation(one[:, :, 1:2], one[:, :, 1:2], ACT.Exp).then_inc(powd, 1)
                act.sem_inc(taken, 2)

                def take(t, h):
                    act.wait_ge(turned, t + 3)
                    act.activation(k.gates[0:experts, ds(t * P, P)], pt[0:experts, h, 0:P], ACT.Copy).then_inc(taken, 1)
                by_parity(act, take)

            @block.tensor
            def _(pe):
                pe.sem_inc(turned, 2)

                def turn(t, h):
                    pe.wait_ge(ready, t + 1)
                    pe.wait_ge(taken, t + 1)
                    pe.transpose(pt[:, h, 0:P], tile[h][:], k.ident).then_inc(turned, 1)
                by_parity(pe, turn)


def feed_forward(k, chunks, w1d, b1d, func, experts, seld, w2d, b2d, finish, rank=None):
    nc = k.nc
    G = 4
    ng = chunks // G
    loads = 4 if seld is None else 5
    gstaged = k.sem("ff_gates")
    loaded = k.dma_sem("ff_loaded")
    hid, act_, gated, osum, fin = (k.sem(f"ff_{s}") for s in ("hidden", "active", "gated", "summed", "finished"))
    with ExitStack() as ctx:
        sb, ps = tensors(nc, ctx)
        w1 = sb("w1", [P, KC, chunks * P])
        b1 = sb("b1", [P, chunks])
        w2 = sb("w2", [P, chunks, D])
        b2 = sb("b2", [max(experts, 1), D])
        gt = sb("gt", [max(experts, 1), P])
        sel = sb("sel", [experts, chunks * P]) if seld is not None else None
        h = [sb(f"h{i}", [P, G, P]) for i in range(2)]
        hm = [sb(f"hm{i}", [P, G, P]) for i in range(2)] if sel is not None else h
        ph = [ps(f"ph{i}", [P, G, P]) for i in range(2)]
        pm = [ps(f"pm{i}", [P, G, P]) for i in range(2)] if sel is not None else None
        po = ps("po", [P, 512])
        used = gated if sel is not None else act_
        with nc.Block() as block:
            @block.sync
            def _(sp):
                for a, b in ((w1, w1d), (b1, b1d), (w2, w2d), (b2, b2d), (sel, seld))[0:loads]:
                    sp.dma_start(a[:], b).then_inc(loaded, 16)

            @block.tensor
            def _(pe):
                def hidden(t, g, s):
                    pe.wait_ge(act_, s + 1)
                    if sel is not None:
                        pe.wait_ge(gated, s + 1)
                    for j in range(G):
                        n = g * G + j
                        for c in range(KC):
                            mm = pe.matmul(ph[g % 2][:, j, :], w1[:, c, n * P:(n + 1) * P], k.yT[:, c, ds(t * P, P)],
                                           start=(c == 0), stop=(c == KC - 1))
                    if sel is not None:
                        for j in range(G):
                            n = g * G + j
                            mm = pe.matmul(pm[g % 2][:, j, :], sel[:, n * P:(n + 1) * P],
                                           k.gates[0:experts, ds(t * P, P)], start=True, stop=True)
                    mm.then_inc(hid, 1)
                pe.sem_inc(osum, 2)
                pe.wait_ge(loaded, 16 * loads)
                hidden(0, 0, 0)
                with pe.Fori(0, NT) as t:
                    for g in range(ng):
                        s = t * ng + g
                        hidden(t + (g + 1) // ng, (g + 1) % ng, s + 1)
                        pe.wait_ge(used, s + 3)
                        if g == 0:
                            pe.wait_ge(fin, t + 1)
                        for j in range(G):
                            mm = pe.matmul(po[:, 0:D], hm[g % 2][:, j, :], w2[:, g * G + j, :],
                                           start=(g == 0 and j == 0), stop=False)
                        if g < ng - 1:
                            mm.then_inc(osum, 1)
                    lhs = gt[:] if experts > 1 else k.ones[0:1, :]
                    if experts > 1:
                        pe.wait_ge(gstaged, t + 1)
                    mm = pe.matmul(po[:, 0:D], lhs, b2[:], start=False, stop=True).then_inc(osum, 1)

            @block.scalar
            def _(act):
                act.sem_inc(act_, 2)
                if rank is not None:
                    act.sem_inc(fin, 1)
                act.wait_ge(loaded, 16 * loads)
                with act.Fori(0, NT) as t:
                    for g in range(ng):
                        s = t * ng + g
                        act.wait_ge(hid, s + 1)
                        act.wait_ge(gated if sel is not None else osum, s + 1)
                        for j in range(G):
                            mm = act.activation(h[g % 2][:, j, :], ph[g % 2][:, j, :], func,
                                                bias=b1[:, g * G + j:g * G + j + 1])
                        mm.then_inc(act_, 1)
                    if rank is not None:
                        act.wait_ge(osum, t * ng + ng + 2)
                        act.activation(k.z[:, ds(t, 1), 0:D], po[:, 0:D].unsqueeze(1), ACT.Copy).then_inc(fin, 1)

            @block.vector
            def _(dve):
                if rank is not None:
                    rank(dve)
                    return
                dve.sem_inc(gated, 2)
                dve.sem_inc(fin, 1)
                with dve.Fori(0, NT) as t:
                    dve.tensor_copy(gt[:], k.gates[0:experts, ds(t * P, P)]).then_inc(gstaged, 1)
                    for g in range(ng):
                        s = t * ng + g
                        dve.wait_ge(act_, s + 3)
                        dve.wait_ge(osum, s + 1)
                        dve.tensor_tensor(hm[g % 2][:], h[g % 2][:], pm[g % 2][:], ALU.mult).then_inc(gated, 1)
                    dve.wait_ge(osum, t * ng + ng + 2)
                    finish(dve, t, po[:, 0:D].unsqueeze(1))
                    dve.drain().then_inc(fin, 1)


def shared_and_experts(k, A):
    nc = k.nc
    loaded = k.dma_sem("moe1_loaded")
    l1, a1, l2, a2, gt, osum, fin = (k.sem(f"moe1_{s}") for s in (
        "first", "act1", "second", "act2", "gated", "out", "fin"))
    NX = 4
    gstaged = k.sem("moe1_gates")
    with ExitStack() as ctx:
        sb, ps = tensors(nc, ctx)
        w1 = sb("w1", [P, KC, 6 * P])
        w2 = sb("w2", [P, 6, P])
        w3 = sb("w3", [P, 3, D])
        b1 = sb("b1", [P, 6])
        b2 = sb("b2", [P, 3])
        b3 = sb("b3", [NX, D])
        sb3 = sb("sb3", [1, D])
        sel = sb("sel", [NX, 2 * P])
        gtile = sb("gtile", [NX, P])
        h1 = [sb(f"h1{i}", [P, 6, P]) for i in range(2)]
        h2 = [sb(f"h2{i}", [P, 3, P]) for i in range(2)]
        p1 = ps("p1", [P, 2, 4, P])
        p2 = ps("p2", [P, 4, P])
        pm = ps("pm", [P, 4, P])
        po = ps("po", [P, 512])
        with nc.Block() as block:
            @block.sync
            def _(sp):
                for a, n in ((w1, "m1_w1"), (w2, "m1_w2"), (w3, "m1_w3"), (b1, "m1_b1"), (b2, "m1_b2"),
                             (b3, "m1_b3"), (sb3, "m1_sb3"), (sel, "sel1")):
                    sp.dma_start(a[:], A[n]).then_inc(loaded, 16)

            @block.tensor
            def _(pe):
                def first(t):
                    pe.wait_ge(a1, t + 1)
                    for n in range(6):
                        for c in range(KC):
                            mm = pe.matmul(p1[:, n // 4, n % 4, :], w1[:, c, n * P:(n + 1) * P],
                                           k.yT[:, c, ds(t * P, P)], start=(c == 0), stop=(c == KC - 1))
                    mm.then_inc(l1, 1)
                pe.sem_inc(osum, 1)
                pe.wait_ge(loaded, 16 * 8)
                first(0)
                with pe.Fori(0, NT) as t:
                    pe.wait_ge(a1, t + 2)
                    pe.wait_ge(gt, t + 1)
                    for n, of in ((0, 0), (1, 0), (2, 1), (3, 1), (4, 2), (5, 2)):
                        mm = pe.matmul(p2[:, of, :], w2[:, n, :], h1[0][:, n, :], start=(n % 2 == 0), stop=(n % 2 == 1))
                    for n in range(2):
                        mm = pe.matmul(pm[:, n, :], sel[:, n * P:(n + 1) * P], k.gates[0:NX, ds(t * P, P)],
                                       start=True, stop=True)
                    mm.then_inc(l2, 1)
                    first(t + 1)
                    pe.wait_ge(gt, t + 2)
                    pe.wait_ge(fin, t + 1)
                    for n in range(3):
                        pe.matmul(po[:, 0:D], h2[1][:, n, :], w3[:, n, :], start=(n == 0), stop=False)
                    pe.wait_ge(gstaged, t + 1)
                    pe.matmul(po[:, 0:D], gtile[:], b3[:], start=False, stop=False)
                    pe.matmul(po[:, 0:D], k.ones[0:1, :], sb3[:], start=False, stop=True).then_inc(osum, 1)

            @block.scalar
            def _(act):
                act.sem_inc(a1, 1)
                act.wait_ge(loaded, 16 * 8)
                with act.Fori(0, NT) as t:
                    act.wait_ge(l1, t + 1)
                    act.wait_ge(l2, t + 1)
                    for n in range(6):
                        mm = act.activation(h1[0][:, n, :], p1[:, n // 4, n % 4, :], ACT.Relu, bias=b1[:, n:n + 1])
                    mm.then_inc(a1, 1)
                    act.wait_ge(l2, t + 2)
                    act.wait_ge(gt, t + 1)
                    for n in range(3):
                        mm = act.activation(h2[0][:, n, :], p2[:, n, :], ACT.Relu, bias=b2[:, n:n + 1])
                    mm.then_inc(a2, 1)

            @block.vector
            def _(dve):
                dve.sem_inc(gt, 1)
                dve.sem_inc(fin, 1)
                dve.sem_inc(l2, 1)
                with dve.Fori(0, NT) as t:
                    dve.wait_ge(a2, t + 1)
                    dve.wait_ge(osum, t + 1)
                    dve.tensor_copy(gtile[:], k.gates[0:NX, ds(t * P, P)]).then_inc(gstaged, 1)
                    dve.tensor_copy(h2[1][:, 0, :], h2[0][:, 0, :])
                    dve.tensor_tensor(h2[1][:, 1:3, :], h2[0][:, 1:3, :], pm[:, 0:2, :], ALU.mult)
                    dve.drain().then_inc(gt, 1)
                    dve.wait_ge(osum, t + 2)
                    dve.tensor_tensor(k.x[:, ds(t, 1), :], k.x[:, ds(t, 1), :], po[:, 0:D].unsqueeze(1), ALU.add)
                    dve.drain().then_inc(fin, 1)


def add_sums(k, acc):
    with k.nc.Block() as block:
        @block.vector
        def _(dve):
            dve.tensor_tensor(k.x[:], k.x[:], acc[:, :, 0:D], ALU.add)


def inverse_counts(dve, rc, acc):
    dve.tensor_scalar(rc, acc[:, :, D:D + 1], 1.0, None, ALU.max)
    dve.drain()
    dve.reciprocal(rc, rc)
    dve.drain()


def means_to_table(k, acc, table):
    stored, ready = k.dma_sem("means_stored"), k.sem("means_ready")
    with ExitStack() as ctx:
        sb, _ = tensors(k.nc, ctx)
        rc = sb("rc", [P, NT, 1])
        with k.nc.Block() as block:
            @block.vector
            def _(dve):
                inverse_counts(dve, rc[:], acc)
                dve.tensor_tensor(acc[:, :, 0:D], acc[:, :, 0:D], rc[:].broadcast_to([P, NT, D]), ALU.mult)
                dve.memset(acc[:, :, D:TW], 1.0)
                dve.drain().then_inc(ready, 1)

            @block.sync
            def _(sp):
                sp.wait_ge(ready, 1)
                sp.dma_start(table.rearrange("(t p) w -> p t w", p=P), acc[:]).then_inc(stored, 16)
                sp.wait_ge(stored, 16)


def hyper_activation(k, A, acc, bias_name, last):
    nc = k.nc
    loaded = k.dma_sem("ha_loaded")
    ready, turned, taken = (k.sem(f"ha_{s}") for s in ("ready", "turned", "taken"))
    with ExitStack() as ctx:
        sb, ps = tensors(nc, ctx)
        rc = sb("rc", [P, NT, 1])
        bias = sb("bias", [P, D])
        slope = sb("slope", [P, 1])
        low = sb("low", [P, NT, D])
        pst = ps("pst", [P, 2, 4, P])
        tile = [sb(f"tile{h}", [P, 1, D]) for h in range(2)]
        with nc.Block() as block:
            @block.sync
            def _(sp):
                sp.dma_start(bias[:], A[bias_name]).then_inc(loaded, 16)
                sp.dma_start(slope[:], A["g3_a"]).then_inc(loaded, 16)

            @block.vector
            def _(dve):
                inverse_counts(dve, rc[:], acc)
                dve.wait_ge(loaded, 32)
                a = acc[:, :, 0:D]
                dve.tensor_tensor(a, a, rc[:].broadcast_to([P, NT, D]), ALU.mult)
                dve.drain()
                dve.tensor_tensor(a, a, bias[:].unsqueeze(1).broadcast_to([P, NT, D]), ALU.add)
                dve.drain()
                if last:
                    dve.tensor_tensor(a, a, k.y[:], ALU.add)
                    dve.drain()
                dve.tensor_scalar(low[:], a, 0.0, slope[:], ALU.min, ALU.mult)
                dve.tensor_scalar(a, a, 0.0, None, ALU.max)
                dve.drain()
                dve.tensor_tensor(a, a, low[:], ALU.add)
                dve.drain()
                if last:
                    dve.tensor_tensor(k.x[:], k.x[:], a, ALU.add)
                else:
                    def stage(t, h):
                        dve.wait_ge(turned, t + 1)
                        dve.tensor_copy(tile[h][:], acc[:, ds(t, 1), 0:D]).then_inc(ready, 1)
                    by_parity(dve, stage)
            if not last:
                @block.tensor
                def _(pe):
                    turn_loop(k, pe, tile, pst, ready, turned, taken)

                @block.scalar
                def _(act):
                    take_loop(k, act, pst, turned, taken)


def chosen_tokens(k, A, wt, wrow_d):
    nc = k.nc
    logits(k, wt, 1, A["f3_wr"], A["f3_br"])
    turned, copied, stored = k.sem("rank_turned"), k.sem("rank_copied"), k.dma_sem("rank_stored")
    with ExitStack() as ctx:
        sb, ps = tensors(nc, ctx)
        pad = sb("pad", [P, P])
        rowt = sb("rowt", [NT, P])
        pt = ps("pt", [P, P])
        with nc.Block() as block:
            @block.vector
            def _(dve):
                dve.memset(pad[:], 0.0)
                dve.drain()
                dve.tensor_copy(pad[:, 0:NT], wt[:, :, 0])
                dve.drain().then_inc(copied, 1)
                dve.wait_ge(turned, 1)
                dve.tensor_copy(rowt[:], pt[0:NT, :]).then_inc(copied, 1)

            @block.tensor
            def _(pe):
                pe.wait_ge(copied, 1)
                pe.transpose(pt[:], pad[:], k.ident).then_inc(turned, 1)

            @block.sync
            def _(sp):
                sp.wait_ge(copied, 2)
                sp.dma_start(wrow_d, rowt[:]).then_inc(stored, 16)
                sp.wait_ge(stored, 16)


CHOSEN = max(1, N // 2) - 1


def build(nc, A, out):
    with ExitStack() as ctx:
        k = Kit(nc, ctx)
        sb, _ = tensors(nc, ctx)
        k.const = sb("const", [P, C_END])
        k.x = sb("x", [P, NT, D])
        k.y = sb("y", [P, NT, D])
        k.yT = sb("yT", [P, KC, NP_ + P])
        graph = ctx.enter_context(ExitStack())
        gsb, _ = tensors(nc, graph)
        meta_d = gsb("meta_dst", [P, COLS, NF], I32)
        meta_s = gsb("meta_src", [P, COLS, NF], I32)
        bt_d = gsb("bt_dst", [1, COLS], I32)
        bt_s = gsb("bt_src", [1, COLS], I32)
        k.ad = gsb("ad", [P, NT, HEADS])
        wedge = gsb("wedge", [P, COLS])
        c = k.const
        k.ident, k.iota, k.tri, k.ones = (c[:, o:o + P] for o in (C_ID, C_IOTA, C_TRI, C_ONES))
        k.iota256 = c[:, C_IOTA:C_IOTA + 2 * P]
        k.tile_iota = c[:, C_TILE:C_TILE + COLS]
        slots_d, slots_s = k.dram("slots_dst", [P * COLS, NF], I32), k.dram("slots_src", [P * COLS, NF], I32)
        table = k.dram("table", [NP_, TW])
        table7 = k.dram("table7", [NP_, NTYPE * D])
        wrow_d = k.dram("wrow", [NT, P])

        start_s, start_d = gsb("start_src", [P, NT + 1]), gsb("start_dst", [P, NT + 1])
        inv = gsb("inv", [P, NT, NTYPE])

        load_state(k, A)
        k.end_stage()
        with ExitStack() as part:
            psb, _ = tensors(nc, part)
            scratch = (psb("raw", [P, 4, EC], I32), psb("bint", [P, EC], I32), psb("coli", [P, EC], I32),
                       psb("bucket", [P, EC]), psb("one", [P, EC]), psb("mask", [P, EC]), psb("incl", [P, EC]),
                       psb("within", [P, EC]))
            by_dst = Sorting(k, part, "dst", slots_d, meta_d, bt_d, start_d)
            with ExitStack() as inner:
                by_src = Sorting(k, inner, "src", slots_s, meta_s, bt_s, start_s)
                by_src.renew(k)
                with ExitStack() as c1:
                    run(k, rank_edges(k, c1, A, by_src, A["src"], A["dst"], scratch))
                by_src.renew(k)
                by_dst.renew(k)
                with ExitStack() as c2:
                    run(k, count_types(k, c2, by_src, scratch[0], inv),
                        rank_edges(k, c2, A, by_dst, A["dst"], A["src"], scratch),
                        layer_norm(k, c2, keep=False),
                        linear_to_table(k, c2, A["g0_w"], None, table, D, attention=A["g0_a"]),
                        scatter_edges(k, by_src))
            by_dst.renew(k)
            with ExitStack() as c3:
                run(k, look_up_weights(k, c3, meta_s, bt_s, inv, wedge), scatter_edges(k, by_dst))

        with ExitStack() as part:
            psb, _ = tensors(nc, part)
            attention_aggregate(k, meta_d, bt_d, start_d, table, psb("acc", [P, NT, TW]))
        with ExitStack() as part:
            psb, _ = tensors(nc, part)
            k.gates = psb("gates", [32, NP_ + P])
            with nc.Block() as block:
                @block.vector
                def _(dve):
                    dve.memset(k.gates[:], 0.0)

            with ExitStack() as c:
                run(k, layer_norm(k, c))
            gates(k, (A["f0_rw"], A["f0_rb"]), 32, "top1")
            k.end_stage()

            def finish0(dve, t, po):
                dve.scalar_tensor_tensor(out=k.x[:, ds(t, 1), :], in0=po, scalar=0.0, in1=k.x[:, ds(t, 1), :],
                                         op0=ALU.max, op1=ALU.add)
            feed_forward(k, 16, A["f0_w1"], A["f0_b1"], ACT.Relu, 32, A["sel0"], A["f0_w2"], A["f0_b2"], finish0)
            k.end_stage()

        with ExitStack() as c:
            run(k, layer_norm(k, c, keep=False))
        with ExitStack() as c:
            run(k, linear_to_table(k, c, A["g1_w"], None, table7, NTYPE * D))
        with ExitStack() as part:
            psb, _ = tensors(nc, part)
            acc = psb("acc", [P, NT, TW])
            aggregate(k, meta_s, bt_s, F_TYPED, table7.rearrange("n (t d) -> (n t) d", t=NTYPE), wedge, acc)
            k.end_stage()
            add_sums(k, acc)
            k.end_stage()
        with ExitStack() as part:
            psb, _ = tensors(nc, part)
            k.gates = psb("gates", [32, NP_ + P])
            with nc.Block() as block:
                @block.vector
                def _(dve):
                    dve.memset(k.gates[:], 0.0)
            with ExitStack() as c:
                run(k, layer_norm(k, c))
            gates(k, (A["m1_gw"], A["m1_gb"]), 4, "soft2")
            k.end_stage()
            shared_and_experts(k, A)
            k.end_stage()

        with ExitStack() as c:
            run(k, layer_norm(k, c, keep=False), linear_to_table(k, c, A["g2_w"], A["g2_b"], table, D, last_one=True))
        with ExitStack() as part:
            psb, _ = tensors(nc, part)
            acc = psb("acc", [P, NT, TW])
            aggregate(k, meta_s, bt_s, F_OTHER, table, None, acc)
            k.end_stage()
            add_sums(k, acc)
            k.end_stage()
        with ExitStack() as part:
            psb, _ = tensors(nc, part)
            k.gates = psb("gates", [32, NP_ + P])
            with nc.Block() as block:
                @block.vector
                def _(dve):
                    dve.memset(k.gates[:], 0.0)
            with ExitStack() as c:
                run(k, layer_norm(k, c))
            gates(k, (A["f2_rw"], None), 8, "share2")
            k.end_stage()

            def finish2(dve, t, po):
                dve.tensor_tensor(k.y[:, ds(t, 1), :], k.y[:, ds(t, 1), :], po, ALU.add)
                dve.drain()
                dve.tensor_tensor(k.x[:, ds(t, 1), :], k.x[:, ds(t, 1), :], k.y[:, ds(t, 1), :], ALU.add)
            feed_forward(k, 16, A["f2_w1"], A["f2_b1"], ACT.Gelu, 8, A["sel2"], A["f2_w2"], A["f2_b2"], finish2)
            k.end_stage()

        with ExitStack() as c:
            run(k, layer_norm(k, c))
        with ExitStack() as part:
            psb, _ = tensors(nc, part)
            acc = psb("acc", [P, NT, TW])
            for w, b, last in (("g3_w1", "g3_b1", False), ("g3_w2", "g3_b2", True)):
                with ExitStack() as c:
                    run(k, linear_to_table(k, c, A[w], None, table, D, last_one=True))
                aggregate(k, meta_d, bt_d, F_OTHER, table, None, acc)
                k.end_stage()
                means_to_table(k, acc, table)
                k.end_stage()
                aggregate(k, meta_s, bt_s, F_OTHER, table, None, acc)
                k.end_stage()
                hyper_activation(k, A, acc, b, last)
                k.end_stage()

        graph.close()

        with ExitStack() as c:
            run(k, layer_norm(k, c))
        with ExitStack() as part:
            psb, _ = tensors(nc, part)
            wt = psb("wt", [P, NT, 1])
            k.z = psb("z", [P, NT, D])
            chosen_tokens(k, A, wt, wrow_d)
            k.end_stage()
            wall = psb("wall", [P, N])
            after = psb("after", [P, 2 * NP_], mybir.dt.bfloat16)
            mask = psb("mask", [P, N], mybir.dt.bfloat16)
            above = psb("above", [P, NT, 2])
            got = k.dma_sem("rank_got")
            with nc.Block() as block:
                @block.sync
                def _(sp):
                    sp.dma_start(wall[:], wrow_d.rearrange("t p -> (t p)").unsqueeze(0)[:, 0:N].broadcast_to([P, N])).then_inc(got, 16)
                    sp.dma_start(after[:], A["before"]).then_inc(got, 16)

            def rank(dve):
                dve.wait_ge(got, 32)
                with dve.Fori(0, NT) as t:
                    dve.tensor_scalar(mask[:], wall[:], wt[:, ds(t, 1), :].rearrange("p t o -> p (t o)"), 0.0,
                                      ALU.is_gt, ALU.add, accum_out=above[:, ds(t, 1), 0:1].rearrange("p t o -> p (t o)"))
                    dve.drain()
                    dve.scalar_tensor_tensor(out=mask[:], in0=wall[:], scalar=wt[:, ds(t, 1), :].rearrange("p t o -> p (t o)"),
                                             in1=after[:, ds(NP_ - t * P, N)], op0=ALU.is_equal, op1=ALU.mult,
                                             accum_out=above[:, ds(t, 1), 1:2].rearrange("p t o -> p (t o)"))
                    dve.drain()
                dve.tensor_tensor(above[:, :, 0:1], above[:, :, 0:1], above[:, :, 1:2], ALU.add)
                dve.drain()
                dve.tensor_scalar(above[:, :, 0:1], above[:, :, 0:1], float(CHOSEN), None, ALU.is_lt)
                dve.drain()
                dve.tensor_tensor(wt[:], wt[:], above[:, :, 0:1], ALU.mult)
            feed_forward(k, 8, A["f3_w1"], A["f3_b1"], ACT.Gelu_apprx_tanh, 1, None, A["f3_w2"], A["f3_b2"], None, rank=rank)
            k.end_stage()
            with nc.Block() as block:
                @block.vector
                def _(dve):
                    dve.tensor_tensor(k.z[:], k.z[:], wt[:].broadcast_to([P, NT, D]), ALU.mult)
                    dve.tensor_tensor(k.x[:], k.x[:], k.y[:], ALU.add)
                    dve.drain()
                    dve.tensor_tensor(k.x[:], k.x[:], k.z[:], ALU.add)
        dump(k, out)


def dump(k, out):
    stored = k.dma_sem("stored")
    with k.nc.Block() as block:
        @block.sync
        def _(sp):
            sp.dma_start(out[0:(NT - 1) * P, :].rearrange("(t p) d -> p t d", p=P), k.x[:, 0:NT - 1, :]).then_inc(stored, 16)
            sp.dma_start(out[(NT - 1) * P:N, :], k.x[0:NTAIL, NT - 1, :]).then_inc(stored, 16)
            sp.wait_ge(stored, 32)


def constants():
    c = np.zeros((P, C_END), np.float32)
    c[:, C_ID:C_ID + P] = np.eye(P)
    c[:, C_IOTA:C_IOTA + 2 * P] = np.arange(2 * P)
    c[:, C_TRI:C_TRI + P] = np.triu(np.ones((P, P)), 1)
    c[:, C_ONES:C_ONES + P] = 1.0
    c[:, C_TILE:C_TILE + COLS] = np.arange(COLS)
    return c


def selector(experts, width):
    return (np.arange(experts * width)[None, :] // width == np.arange(experts)[:, None]).astype(np.float32)


def kernel(**inputs):
    import concourse.bacc as _bacc
    import ml_dtypes
    from concourse.bass_utils import run_bass_kernel_spmd as _run

    g = {n: np.asarray(v) for n, v in inputs.items()}

    def rows(w):
        return w.reshape(-1, P, w.shape[-1]).transpose(1, 0, 2)

    def column(b):
        return b.reshape(-1, P).T

    def spread(b):
        return np.broadcast_to(b.reshape(1, -1), (P, b.size))

    ew2 = np.zeros((P, 6, P), np.float32)
    ew2[:, 0:2] = rows(g["L1_ffn_sW2"])
    for e in range(4):
        ew2[:, 2 + e, 64 * (e % 2):64 * (e % 2) + 64] = g["L1_ffn_eW2"][e]
    arrays = {
        "consts": constants(),
        "before": (np.arange(2 * NP_)[None, :] - NP_ < np.arange(P)[:, None]).astype(ml_dtypes.bfloat16),
        "sel0": selector(32, 64), "sel1": selector(4, 64), "sel2": selector(8, D),
        "x": g["x"], "src": g["src"], "dst": g["dst"], "etype": g["edge_type_7"],
        "eweight": g["edge_weight"].view(np.int32),
        "g0_w": rows(g["L0_gnn_W"].transpose(1, 0, 2).reshape(D, D)),
        "g0_a": np.stack([spread(g["L0_gnn_a_src"]), spread(g["L0_gnn_a_dst"])], 1),
        "f0_rw": rows(g["L0_ffn_router_w"].T), "f0_rb": g["L0_ffn_router_b"][None],
        "f0_w1": rows(g["L0_ffn_W1"].transpose(1, 0, 2).reshape(D, -1)), "f0_b1": column(g["L0_ffn_b1"]),
        "f0_w2": rows(g["L0_ffn_W2"].reshape(-1, D)), "f0_b2": g["L0_ffn_b2"],
        "g1_w": rows(g["L1_gnn_weights"].reshape(NTYPE, D, D).transpose(1, 0, 2).reshape(D, -1)),
        "m1_w1": rows(np.concatenate([g["L1_ffn_sW1"], g["L1_ffn_eW1"].transpose(1, 0, 2).reshape(D, -1)], 1)),
        "m1_b1": column(np.concatenate([g["L1_ffn_sb1"], g["L1_ffn_eb1"].reshape(-1)])),
        "m1_w2": ew2, "m1_b2": column(np.concatenate([g["L1_ffn_sb2"], g["L1_ffn_eb2"].reshape(-1)])),
        "m1_w3": rows(np.concatenate([g["L1_ffn_sW3"], g["L1_ffn_eW3"].reshape(-1, D)], 0)),
        "m1_b3": g["L1_ffn_eb3"], "m1_sb3": g["L1_ffn_sb3"][None],
        "m1_gw": rows(g["L1_ffn_gW"]), "m1_gb": g["L1_ffn_gb"][None],
        "g2_w": rows(g["L2_gnn_W"].T), "g2_b": g["L2_gnn_b"][None],
        "f2_rw": rows(g["L2_ffn_router_w"].T),
        "f2_w1": rows(g["L2_ffn_w1"].transpose(1, 0, 2).reshape(D, -1)), "f2_b1": column(g["L2_ffn_b1"]),
        "f2_w2": rows(g["L2_ffn_w2"].reshape(-1, D)), "f2_b2": g["L2_ffn_b2"],
        "g3_w1": rows(g["L3_gnn_W1"]), "g3_w2": rows(g["L3_gnn_W2"]),
        "g3_b1": spread(g["L3_gnn_b1"]), "g3_b2": spread(g["L3_gnn_b2"]), "g3_a": spread(g["L3_gnn_a"]),
        "f3_wr": rows(g["L3_ffn_wr"]), "f3_br": g["L3_ffn_br"][None],
        "f3_w1": rows(g["L3_ffn_w1"]), "f3_b1": column(g["L3_ffn_b1"]),
        "f3_w2": rows(g["L3_ffn_w2"]), "f3_b2": g["L3_ffn_b2"][None],
    }
    nc = _bacc.Bacc("TRN2", target_bir_lowering=False, num_devices=1)
    args = {}
    for name, a in arrays.items():
        arrays[name] = a = np.ascontiguousarray(a)
        args[name] = nc.dram_tensor(f"in_{name}", a.shape, mybir.dt.from_np(a.dtype), kind="ExternalInput").ap()
    out = nc.dram_tensor("out", (N, D), F32, kind="ExternalOutput").ap()
    build(nc, args, out)
    r = _run(nc, [{f"in_{n}": a for n, a in arrays.items()}], core_ids=[0])
    return r.results[0]["out"]
```

```python
from contextlib import ExitStack

import numpy as np
import concourse.bass as bass
from concourse import mybir

F32 = mybir.dt.float32
I32 = mybir.dt.int32
BF16 = mybir.dt.bfloat16
ALU = mybir.AluOpType
ACT = mybir.ActivationFunctionType
AX = mybir.AxisListType

P = 128
N = 3125
D = 256
NT = -(-N // P)
NP_ = NT * P
NTAIL = N - (NT - 1) * P
KC = D // P
E = 53125
EC = 416
EFULL = E // EC
ETAIL = E - EFULL * EC
HALF = 10
GROUP = 2 * HALF
TILES = -(-((E + NT * (P - 1)) // P) // GROUP) * GROUP
STEPS = TILES // GROUP
COLS = TILES + GROUP
NF = 8
F_OTHER, F_TYPED, F_LOCAL, F_WEIGHT, F_TYPE = range(5)
NTYPE = 7
HEADS = 4
HD = D // HEADS
TW = D + HEADS
PADKEY = NP_
LOWEST = -1.0e30
UNROLL = 4
SCB = 52
SCL = EC // (2 * SCB)

C_ID, C_IOTA, C_TRI, C_ONES, C_TILE = 0, P, 3 * P, 4 * P, 5 * P
C_END = C_TILE + COLS


def ds(a, n):
    return bass.ds(a, n)


def peeled(engine, count, body):
    body(0)
    with engine.Fori(1, count) as i:
        body(i)


def by_parity(engine, body):
    with engine.Fori(0, NT // UNROLL) as i:
        for j in range(UNROLL):
            body(i * UNROLL + j, j % 2)
    for t in range(NT // UNROLL * UNROLL, NT):
        body(t, t % 2)


def by_turns(engine, body):
    body(0, 0)
    with engine.Fori(0, NT // 2) as i:
        for q in (1, 2):
            body(i * 2 + q, q % 2)


def wait(engine, semaphore, value):
    if not (isinstance(value, int) and value <= 0):
        engine.wait_ge(semaphore, value)


class Kit:

    def __init__(self, nc, ctx):
        self.nc, self.ctx, self.n = nc, ctx, 0
        self.stage_sems = []

    def sem(self, name):
        self.n += 1
        self.stage_sems.append(self.nc.alloc_semaphore(name=f"{name}_{self.n}"))
        return self.stage_sems[-1]

    def dma_sem(self, name):
        self.n += 1
        return self.ctx.enter_context(self.nc.semaphore(f"{name}_{self.n}"))

    def end_stage(self):
        self.nc.all_engine_barrier()
        self.nc.clear_and_free_semaphores(self.stage_sems)
        self.nc.all_engine_barrier()
        self.stage_sems = []

    def dram(self, name, shape, dt=F32):
        return self.nc.dram_tensor(name, shape, dt).ap()


def run(k, *parts):
    with k.nc.Block() as block:
        for name, register in (("sync", block.sync), ("gpsimd", block.gpsimd), ("tensor", block.tensor),
                               ("scalar", block.scalar), ("vector", block.vector)):
            programs = [p[name] for p in parts if name in p]
            if programs:
                def program(engine, programs=programs):
                    for n, f in enumerate(programs):
                        if n:
                            engine.drain()
                        f(engine)
                register(program)
    k.end_stage()


def tensors(nc, ctx):
    mark = nc.next_id() if callable(nc.next_id) else nc.next_id

    def sb(name, shape, dt=F32):
        return ctx.enter_context(nc.sbuf_tensor(f"{name}_{mark}", shape, dt))

    def ps(name, shape, dt=F32):
        return ctx.enter_context(nc.psum_tensor(f"{name}_{mark}", shape, dt))
    return sb, ps


def load_state(k, A):
    k.const_loaded = k.dma_sem("const_loaded")
    loaded, zeroed = k.dma_sem("x_loaded"), k.sem("zeroed")

    def constants(sp):
        sp.dma_start(k.const[:], A["consts"]).then_inc(k.const_loaded, 16)

    def zero(dve):
        dve.memset(k.x[:, NT - 1:NT, :], 0.0)
        dve.memset(k.yT[:, :, NP_:], 0.0).then_inc(zeroed, 1)

    def state(sp):
        sp.dma_start(k.x[:, 0:NT - 1, :],
                     A["x"][0:(NT - 1) * P, :].rearrange("(t p) d -> p t d", p=P)).then_inc(loaded, 16)
        sp.wait_ge(zeroed, 1)
        sp.dma_start(k.x[0:NTAIL, NT - 1, :], A["x"][(NT - 1) * P:N, :]).then_inc(loaded, 16)
        sp.wait_ge(loaded, 32)
    return {"sync": constants, "vector": zero}, {"sync": state}


class Sorting:

    def __init__(self, k, ctx, tag, slots, meta, btile, start):
        nc = k.nc
        self.tag, self.slots, self.meta, self.btile, self.start = tag, slots, meta, btile, start
        self.loaded, self.blank, self.back = (k.dma_sem(f"{s}_{tag}") for s in ("loaded", "blank", "back"))
        self.scattered = [k.dma_sem(f"scattered{h}_{tag}") for h in range(2)]
        sb, ps = tensors(nc, ctx)
        self.pay = sb("pay", [P, EC, NF], I32)
        self.row = sb("row", [P, EC], I32)
        self.local = sb("local", [P, EC])
        self.stage = [sb(f"stage{h}", [P, SCB, NF], I32) for h in range(2)]
        self.sidx = [sb(f"sidx{h}", [P, SCB], I32) for h in range(2)]

    def renew(self, k):
        self.filled, self.totals, self.prefix, self.staged, self.gate = (
            k.sem(f"{s}_{self.tag}") for s in ("filled", "totals", "prefix", "staged", "gate"))


def rank_edges(k, ctx, A, S, key, other, scratch):
    NB = NT + 1
    sb, ps = tensors(k.nc, ctx)
    raw, bint, coli, bucket, one, mask, incl, within = scratch[0:8]
    masks, incls = (mask, scratch[8]), (incl, scratch[9])
    total, ntile, tincl, base = (sb(n, [P, NB]) for n in ("total", "ntile", "tincl", "base"))
    cnti = sb("cnti", [P, NB], I32)
    psx = ps("psx", [P, 2, NB])
    pay = S.pay
    payf = pay[:].bitcast(F32)
    meta = S.meta[:]

    def sync(sp):
        sp.wait_ge(S.filled, 1)
        sp.dma_start(S.slots.rearrange("(p c) f -> p c f", p=P), meta).then_inc(S.blank, 16)
        for i, a in enumerate((key, other, A["etype"], A["eweight"])):
            sp.dma_start(raw[0:EFULL, i, :], a[0:EFULL * EC].rearrange("(p c) -> p c", c=EC)).then_inc(S.loaded, 16)
            sp.dma_start(raw[EFULL:EFULL + 1, i, 0:ETAIL],
                         a[EFULL * EC:E].rearrange("(p c) -> p c", p=1)).then_inc(S.loaded, 16)

    def tensor(pe):
        pe.wait_ge(S.totals, 1)
        pe.matmul(psx[:, 0, :], k.tri, total[:], start=True, stop=True)
        pe.matmul(psx[:, 1, :], k.ones, total[:], start=True, stop=True).then_inc(S.prefix, 1)

    def vector(dve):
        dve.memset(raw[:, 1:4, :], 0)
        dve.memset(raw[:, 0, :], PADKEY)
        dve.memset(meta, 0)
        dve.drain()
        dve.memset(meta.bitcast(F32)[:, :, F_LOCAL:F_LOCAL + 1], -1.0)
        dve.drain().then_inc(S.filled, 1)
        dve.memset(within[:], -1.0)
        dve.memset(one[:], 1.0)
        dve.memset(pay[:], 0)
        dve.drain()
        dve.wait_ge(S.loaded, 128)
        dve.wait_ge(k.const_loaded, 16)
        dve.tensor_scalar(bint[:], raw[:, 0, :], 7, None, ALU.arith_shift_right)
        dve.tensor_scalar(coli[:], raw[:, 0, :], P - 1, None, ALU.bitwise_and)
        dve.tensor_copy(pay[:, :, F_OTHER], raw[:, 1, :])
        dve.scalar_tensor_tensor(out=pay[:, :, F_TYPED], in0=raw[:, 1, :], scalar=float(NTYPE),
                                 in1=raw[:, 2, :], op0=ALU.mult, op1=ALU.add)
        dve.tensor_copy(payf[:, :, F_TYPE], raw[:, 2, :])
        dve.tensor_copy(pay[:, :, F_WEIGHT], raw[:, 3, :])
        dve.drain()
        dve.tensor_copy(bucket[:], bint[:])
        dve.drain()
        dve.tensor_scalar(mask[:], bucket[:], float(NT), float(-P), ALU.is_equal, ALU.mult)
        dve.drain()
        dve.tensor_tensor(S.local[:], mask[:], coli[:], ALU.add)
        dve.drain()
        dve.tensor_copy(payf[:, :, F_LOCAL], S.local[:])
        with dve.Fori(0, NB // 2) as i:
            for h in range(2):
                dve.tensor_scalar(masks[h][:], bucket[:], k.iota[:, ds(i * 2 + h, 1)], 0.0, ALU.is_equal, ALU.add,
                                  accum_out=total[:, ds(i * 2 + h, 1)])
            dve.drain()
        dve.drain().then_inc(S.totals, 1)
        dve.wait_ge(S.prefix, 1)
        dve.tensor_scalar(cnti[:], psx[:, 1, :], float(P - 1), None, ALU.add)
        dve.drain()
        dve.tensor_scalar(cnti[:], cnti[:], 7, None, ALU.arith_shift_right)
        dve.drain()
        dve.tensor_scalar(ntile[:], cnti[:], 1.0, None, ALU.max)
        dve.drain()
        dve.tensor_tensor_scan(tincl[:], one[:, 0:NB], ntile[:], 0.0, ALU.mult, ALU.add)
        dve.drain()
        dve.tensor_tensor(S.start[:], tincl[:], ntile[:], ALU.subtract)
        dve.drain()
        dve.scalar_tensor_tensor(out=base[:], in0=S.start[:], scalar=float(P), in1=psx[:, 0, :],
                                 op0=ALU.mult, op1=ALU.add)
        dve.drain()
        with dve.Fori(0, NB // 2) as i:
            for h in range(2):
                dve.tensor_scalar(masks[h][:], bucket[:], k.iota[:, ds(i * 2 + h, 1)], None, ALU.is_equal)
            dve.drain()
            for h in range(2):
                dve.tensor_tensor_scan(incls[h][:], one[:], masks[h][:], base[:, ds(i * 2 + h, 1)], ALU.mult, ALU.add)
            dve.drain()
            for h in range(2):
                dve.tensor_tensor(masks[h][:], masks[h][:], incls[h][:], ALU.mult)
            dve.drain()
            for h in range(2):
                dve.tensor_tensor(within[:], within[:], masks[h][:], ALU.add)
                dve.drain()
        dve.tensor_copy(bint[:], within[:])
        dve.drain()
        dve.tensor_scalar(S.row[:], bint[:], P - 1, None, ALU.bitwise_and)
        dve.tensor_scalar(coli[:], bint[:], 7, None, ALU.arith_shift_right)
        dve.drain()
        dve.scalar_tensor_tensor(out=S.row[:], in0=S.row[:], scalar=float(COLS), in1=coli[:],
                                 op0=ALU.mult, op1=ALU.add)
    return {"sync": sync, "tensor": tensor, "vector": vector}


def place_tiles(k, ctx, S):
    sb, _ = tensors(k.nc, ctx)
    bt = sb("bt", [1, COLS])

    def vector(dve):
        dve.memset(bt[:], 0.0)
        dve.drain()
        with dve.Fori(1, NT) as b:
            dve.scalar_tensor_tensor(out=bt[:], in0=k.tile_iota[0:1, :], scalar=S.start[0:1, ds(b, 1)], in1=bt[:],
                                     op0=ALU.is_ge, op1=ALU.add)
            dve.drain()
        dve.tensor_copy(S.btile[:], bt[:])
    return {"vector": vector}


def scatter_edges(k, S):
    def gpsimd(pool):
        pool.wait_ge(S.blank, 16)

        def step(i):
            for h in range(2):
                c = i * (2 * SCB) + h * SCB
                wait(pool, S.scattered[h], i * (16 * SCB))
                pool.tensor_copy(S.stage[h][:], S.pay[:, ds(c, SCB), :])
                pool.tensor_copy(S.sidx[h][:], S.row[:, ds(c, SCB)]).then_inc(S.staged, 1)
                pool.wait_ge(S.staged, i * 2 + h + 1)
                pool.sem_inc(S.gate, 1)
                for c in range(SCB):
                    pool.indirect_dma_start(
                        out=S.slots, out_offset=bass.IndirectOffsetOnAxis(ap=S.sidx[h][:, c:c + 1], axis=0),
                        in_=S.stage[h][:, c, :], in_offset=None).then_inc(S.scattered[h], 16)
        peeled(pool, SCL, step)

    def sync(sp):
        sp.wait_ge(S.blank, 16)
        for h in range(2):
            sp.wait_ge(S.scattered[h], 16 * SCB * SCL)
        sp.dma_start(S.meta[:], S.slots.rearrange("(p c) f -> p c f", p=P)).then_inc(S.back, 16)
        sp.wait_ge(S.back, 16)
    return {"gpsimd": gpsimd, "sync": sync}


def count_types(k, ctx, S, raw, inv):
    sb, ps = tensors(k.nc, ctx)
    W = NT * NTYPE
    B = 8
    typed = sb("typed", [P, EC])
    bint = sb("tbint", [P, EC], I32)
    iob = sb("iob", [P, 2 * P], BF16)
    oh = [sb(f"coh{h}", [P, B, P], BF16) for h in range(2)]
    th = [sb(f"cth{h}", [P, B, W], BF16) for h in range(2)]
    zero = sb("zero", [P, P], BF16)
    pc = ps("pcount", [P, 512])
    hot, used = k.sem("count_hot"), k.sem("count_used")

    def tensor(pe):
        pe.wait_ge(hot, 1)
        pe.matmul(pc[:, 0:W], zero[:], th[0][:, 0, :], start=True, stop=False).then_inc(used, 2)
        with pe.Fori(0, EC // (2 * B)) as i:
            for h in range(2):
                pe.wait_ge(hot, i * 2 + h + 2)
                for j in range(B):
                    mm = pe.matmul(pc[:, 0:W], oh[h][:, j, :], th[h][:, j, :], start=False, stop=False)
                mm.then_inc(used, 1)
        pe.matmul(pc[:, 0:W], zero[:], th[0][:, 0, :], start=False, stop=True).then_inc(used, 1)

    def vector(dve):
        dve.tensor_scalar(bint[:], raw[:, 0, :], 7, None, ALU.arith_shift_right)
        dve.memset(zero[:], 0.0)
        dve.memset(th[0][:], 0.0)
        dve.tensor_copy(iob[:], k.iota256)
        dve.drain().then_inc(hot, 1)
        dve.scalar_tensor_tensor(out=typed[:], in0=bint[:], scalar=float(NTYPE), in1=raw[:, 2, :],
                                 op0=ALU.mult, op1=ALU.add)
        dve.drain()
        with dve.Fori(0, EC // (2 * B)) as i:
            for h in range(2):
                dve.wait_ge(used, i * 2 + h + 1)
                for j in range(B):
                    c = i * (2 * B) + h * B + j
                    dve.tensor_scalar(oh[h][:, j, :], iob[:, 0:P], S.local[:, ds(c, 1)], None, ALU.is_equal)
                    mm = dve.tensor_scalar(th[h][:, j, :], iob[:, 0:W], typed[:, ds(c, 1)], None, ALU.is_equal)
                mm.then_inc(hot, 1)
        dve.wait_ge(used, EC // B + 3)
        dve.tensor_scalar(inv[:].rearrange("p t c -> p (t c)"), pc[:, 0:W], 1.0, None, ALU.max)
        dve.drain()
        dve.reciprocal(inv[:], inv[:])
    return {"tensor": tensor, "vector": vector}


class Hyper:

    def __init__(self, k, ctx, sums, bias_name, A):
        sb, _ = tensors(k.nc, ctx)
        self.sums, self.inputs = sums, (A[bias_name], A["g3_a"])
        self.loaded = k.dma_sem("hyper_loaded")
        self.rc = sb("rc", [P, NT, 1])
        self.bias = sb("bias", [P, 1, D])
        self.slope = sb("slope", [P, 1])
        self.low = [sb(f"low{h}", [P, 1, D]) for h in range(2)]

    def load(self, sp):
        sp.dma_start(self.bias[:, 0, :], self.inputs[0]).then_inc(self.loaded, 16)
        sp.dma_start(self.slope[:], self.inputs[1]).then_inc(self.loaded, 16)

    def start(self, dve):
        inverse_counts(dve, self.rc[:], self.sums)
        dve.wait_ge(self.loaded, 32)

    def activate(self, dve, out, t, h):
        dve.scalar_tensor_tensor(out=out, in0=self.sums[:, ds(t, 1), 0:D], scalar=self.rc[:, ds(t, 1), 0],
                                 in1=self.bias[:], op0=ALU.mult, op1=ALU.add)
        dve.drain()
        dve.tensor_scalar(self.low[h][:], out, 0.0, self.slope[:], ALU.min, ALU.mult)
        dve.drain()
        return dve.scalar_tensor_tensor(out=out, in0=out, scalar=0.0, in1=self.low[h][:], op0=ALU.max, op1=ALU.add)


def hyper_to_x(k, ctx, A, sums, bias_name):
    H = Hyper(k, ctx, sums, bias_name, A)
    sb, _ = tensors(k.nc, ctx)
    FEW = 5
    some, low = sb("some", [P, FEW, D]), sb("low", [P, FEW, D])

    def vector(dve):
        H.start(dve)
        with dve.Fori(0, NT // FEW) as i:
            for j in range(FEW):
                t = i * FEW + j
                dve.scalar_tensor_tensor(out=some[:, j:j + 1, :], in0=sums[:, ds(t, 1), 0:D],
                                         scalar=H.rc[:, ds(t, 1), 0], in1=H.bias[:], op0=ALU.mult, op1=ALU.add)
            dve.drain()
            dve.tensor_tensor(some[:], some[:], k.y[:, ds(i * FEW, FEW), :], ALU.add)
            dve.drain()
            dve.tensor_scalar(low[:], some[:], 0.0, H.slope[:], ALU.min, ALU.mult)
            dve.drain()
            dve.scalar_tensor_tensor(out=some[:], in0=some[:], scalar=0.0, in1=low[:], op0=ALU.max, op1=ALU.add)
            dve.drain()
            dve.tensor_tensor(k.x[:, ds(i * FEW, FEW), :], k.x[:, ds(i * FEW, FEW), :], some[:], ALU.add)
            dve.drain()
    return {"sync": H.load, "vector": vector}


def norm_product(k, ctx, weights, bias, width, y=False, yT=False, out=None, table=None, attention=None,
                 last_one=False, hyper=None):
    norm, turned, taken, prod, kept = (k.sem(f"np_{s}") for s in ("norm", "turned", "taken", "prod", "kept"))
    var, root, moved = (k.sem(f"np_{s}") for s in ("var", "root", "moved"))
    loaded, stored = k.dma_sem("np_loaded"), [k.dma_sem(f"np_stored{h}") for h in range(2)]
    sb, ps = tensors(k.nc, ctx)
    stats = sb("stats", [P, NT, 6])
    aggr = sb("aggr", [P, NT, 2])
    rstd = sb("rstd", [P, NT])
    tile = [sb(f"tile{h}", [P, 1, D]) for h in range(2)]
    yt = [sb(f"yt{h}", [P, KC, P]) for h in range(2)]
    w = sb("w", [P, KC, width])
    b = sb("b", [1, width]) if bias is not None else None
    tw = TW if (attention is not None or last_one) else width
    row = [sb(f"row{h}", [P, tw]) for h in range(2)] if table is not None else None
    if attention is not None:
        att = sb("att", [P, 2, D])
        prodt = sb("prodt", [P, 2, D])
    loads = 1 + (bias is not None) + (attention is not None)
    nblk = -(-width // 512)
    bw = width // nblk
    banks = 2 if nblk == 1 else nblk
    ahead = 2 * nblk
    pst = ps("pst", [P, 2, 4, P])
    acc = ps("acc", [P, banks, 512])
    scalar_keeps = table is not None and attention is None
    filled = k.sem("np_filled")
    if hyper is not None:
        H = Hyper(k, ctx, *hyper)

    def sync(sp):
        sp.dma_start(w[:], weights).then_inc(loaded, 16)
        if bias is not None:
            sp.dma_start(b[:], bias).then_inc(loaded, 16)
        if attention is not None:
            sp.dma_start(att[:], attention).then_inc(loaded, 16)
        if hyper is not None:
            H.load(sp)
        if table is None:
            return
        with sp.Fori(0, NT // 2) as i:
            for h in range(2):
                sp.wait_ge(kept, (i * 2 + h + 1) * nblk + banks)
                sp.dma_start(table[ds((i * 2 + h) * P, P), :], row[h][:]).then_inc(stored[h], 16)
        sp.wait_ge(kept, NT * nblk + banks)
        sp.dma_start(table[(NT - 1) * P:NT * P, :], row[0][:]).then_inc(stored[0], 16)
        sp.wait_ge(stored[0], 16 * (NT // 2 + 1))
        sp.wait_ge(stored[1], 16 * (NT // 2))

    def gpsimd(pool):
        pool.sem_inc(moved, 2)

        def move(t, h):
            pool.wait_ge(norm, t + 1)
            pool.tensor_copy(k.y[:, ds(t, 1), :], tile[h][:]).then_inc(moved, 1)
        by_parity(pool, move)

    def tensor(pe):
        def turn(t, h):
            pe.wait_ge(norm, t + 1)
            pe.wait_ge(taken, t + 1)
            for c in range(KC):
                mm = pe.transpose(pst[:, h, c, :], tile[h][:, 0, c * P:(c + 1) * P], k.ident)
            mm.then_inc(turned, 1)

        def product(t, h):
            pe.wait_ge(taken, t + 3)
            for j in range(nblk):
                into = acc[:, h if nblk == 1 else j, 0:bw]
                part = slice(j * bw, (j + 1) * bw)
                pe.wait_ge(kept, t * nblk + j + 1)
                for c in range(KC):
                    mm = pe.matmul(into, yt[h][:, c, :], w[:, c, part], start=(c == 0),
                                   stop=(c == KC - 1 and bias is None))
                if bias is not None:
                    mm = pe.matmul(into, k.ones[0:1, :], b[:, part], start=False, stop=True)
                mm.then_inc(prod, 1)
        pe.sem_inc(turned, 2)
        pe.sem_inc(prod, ahead)
        pe.wait_ge(loaded, 16 * loads)
        turn(0, 0)
        with pe.Fori(0, NT // UNROLL) as i:
            for j in range(UNROLL):
                turn(i * UNROLL + j + 1, (j + 1) % 2)
                product(i * UNROLL + j, j % 2)
        product(NT - 1, 0)

    def scalar(act):
        if hyper is None:
            act.wait_ge(var, 1)
            act.activation(rstd[:], rstd[:], ACT.Sqrt).then_inc(root, 1)
        act.sem_inc(taken, 2)
        if scalar_keeps:
            act.sem_inc(kept, banks)

        def take(t, h):
            act.wait_ge(turned, t + 3)
            act.wait_ge(prod, (t + 1) * nblk)
            if yT:
                act.activation(k.yT[:, :, ds(t * P, P)], pst[:, h, 0:KC, :], ACT.Copy)
            act.activation(yt[h][:], pst[:, h, 0:KC, :], ACT.Copy).then_inc(taken, 1)
        if not scalar_keeps:
            by_parity(act, take)
            return

        def keep(i, h):
            t = i * 2 + h
            wait(act, stored[h], i * 16)
            for j in range(nblk):
                act.wait_ge(prod, t * nblk + j + 1 + ahead)
                act.activation(row[h][:, j * bw:(j + 1) * bw],
                               acc[:, h if nblk == 1 else j, 0:bw], ACT.Copy).then_inc(kept, 1)

        def pair(i):
            for h in range(2):
                take(i * 2 + h + 1, 1 - h)
                keep(i, h)
        act.wait_ge(filled, 1)
        take(0, 0)
        pair(0)
        with act.Fori(0, (NT // 2 - 2) // 2) as i:
            for q in (1, 2):
                pair(i * 2 + q)
        pair(NT // 2 - 1)
        keep(NT // 2, 0)

    def statistics(dve):
        with dve.Fori(0, NT // 5) as i:
            for j in range(5):
                dve.bn_stats(stats[:, ds(i * 5 + j, 1), :], k.x[:, ds(i * 5 + j, 1), :])
        dve.drain()
        dve.tensor_tensor(aggr[:, :, 0], stats[:, :, 1], stats[:, :, 4], ALU.add)
        dve.tensor_tensor(aggr[:, :, 1], stats[:, :, 1], stats[:, :, 4], ALU.subtract)
        dve.tensor_tensor(rstd[:], stats[:, :, 2], stats[:, :, 5], ALU.add)
        dve.drain()
        dve.tensor_scalar(aggr[:, :, 0], aggr[:, :, 0], 0.5, None, ALU.mult)
        dve.scalar_tensor_tensor(out=aggr[:, :, 1], in0=aggr[:, :, 1], scalar=0.25, in1=aggr[:, :, 1],
                                 op0=ALU.mult, op1=ALU.mult)
        dve.drain()
        dve.scalar_tensor_tensor(out=rstd[:], in0=rstd[:], scalar=1.0 / D, in1=aggr[:, :, 1],
                                 op0=ALU.mult, op1=ALU.add)
        dve.drain()
        dve.tensor_scalar(rstd[:], rstd[:], 1e-5, None, ALU.add).then_inc(var, 1)
        dve.wait_ge(root, 1)
        dve.reciprocal(rstd[:], rstd[:])
        dve.drain()

    def vector(dve):
        if last_one:
            for h in range(2):
                dve.memset(row[h][:, D:TW], 1.0)
        if hyper is None:
            statistics(dve)
        else:
            H.start(dve)

        def normalize(t, h):
            dve.wait_ge(turned, t + 1)
            if hyper is not None:
                H.activate(dve, tile[h][:], t, h).then_inc(norm, 1)
                return
            if y:
                dve.wait_ge(moved, t + 1)
            dve.tensor_scalar(tile[h][:], k.x[:, ds(t, 1), :], aggr[:, ds(t, 1), 0:1],
                              rstd[:, ds(t, 1)], ALU.subtract, ALU.mult).then_inc(norm, 1)

        def keep(i, h):
            t = i * 2 + h
            if table is None:
                dve.wait_ge(prod, t + 1 + ahead)
                dve.tensor_copy(out[:, ds(t, 1), 0:width], acc[:, h:h + 1, 0:width]).then_inc(kept, 1)
                return
            wait(dve, stored[h], i * 16)
            dve.wait_ge(prod, t + 1 + ahead)
            dve.tensor_copy(row[h][:, 0:D], acc[:, h, 0:D])
            for s in range(2):
                dve.tensor_tensor(prodt[:, s, :], acc[:, h, 0:D], att[:, s, :], ALU.mult)
            dve.drain()
            dve.tensor_reduce(row[h][:, D:TW], prodt[:, 0, :].rearrange("p (a b) -> p a b", a=HEADS), AX.X, ALU.add)
            dve.tensor_reduce(k.ad[:, ds(t, 1), :], prodt[:, 1, :].rearrange("p (a b) -> p a b", a=HEADS), AX.X, ALU.add)
            dve.drain().then_inc(kept, 1)
        if scalar_keeps:
            dve.drain().then_inc(filled, 1)
            by_parity(dve, normalize)
            return
        dve.sem_inc(kept, banks)
        if attention is not None:
            dve.wait_ge(loaded, 16 * loads)

        def pair(i):
            for h in range(2):
                normalize(i * 2 + h + 2, h)
                keep(i, h)
        normalize(0, 0)
        normalize(1, 1)
        pair(0)
        with dve.Fori(0, (NT // 2 - 2) // 2) as i:
            for q in (1, 2):
                pair(i * 2 + q)
        normalize(NT - 1, 0)
        keep(NT // 2 - 1, 0)
        keep(NT // 2 - 1, 1)
        keep(NT // 2, 0)
    parts = {"vector": vector, "tensor": tensor, "scalar": scalar, "sync": sync}
    return parts | ({"gpsimd": gpsimd} if y else {})


def onehots(k, dve, out, meta, first):
    mf = meta[:].bitcast(F32)
    local = mf[:, ds(first, HALF), F_LOCAL:F_LOCAL + 1]
    return dve.tensor_tensor(out, k.iota.unsqueeze(1).broadcast_to([P, HALF, P]),
                             local.broadcast_to([P, HALF, P]), ALU.is_equal)


def distances(k, act, out, meta, first, count=HALF):
    mf = meta[:].bitcast(F32)
    for j in range(count):
        act.activation(out[:, j, :], k.iota, ACT.Abs, scale=-1.0, bias=mf[:, ds(first + j, 1), F_LOCAL])


def node_tiles(k, engine, btile, first, count):
    return k.nc.values_load_multi_w_load_instructions(
        btile[0:1, ds(first, count)], engines=(engine,), min_val=0, max_val=NT - 1,
        skip_runtime_bounds_check_because="a node tile is a count of NT - 1 comparisons that hold")[1]


def gather_loop(k, pool, idx, field, rows, table, rows_done, got, gate, staged, half=HALF):
    def step(i):
        for lot in range(2):
            first = i * (2 * GROUP) + lot * GROUP
            if half == GROUP:
                wait(pool, got[lot], i * (16 * half))
            pool.tensor_copy(k.gidx[lot][:], idx[:, ds(first, GROUP), field]).then_inc(staged, 1)
            pool.wait_ge(staged, i * 2 + lot + 1)
            for j in range(GROUP):
                slot = (lot * GROUP + j) % (2 * half)
                pool.wait_ge(rows_done, first + j + 1)
                pool.sem_inc(gate, 1)
                pool.indirect_dma_start(
                    out=rows[:, slot, :], out_offset=None, in_=table,
                    in_offset=bass.IndirectOffsetOnAxis(ap=k.gidx[lot][:, j:j + 1], axis=0)
                ).then_inc(got[slot // half], 16)
    peeled(pool, TILES // (2 * GROUP), step)


def aggregate(k, meta, btile, field, table, weights, acc):
    nc = k.nc
    width = table.shape[1]
    hot, rdone, added, gate, staged, zero = (k.sem(f"agg_{s}") for s in ("onehots", "rows_done", "added", "gate", "staged", "zeroed"))
    got = [k.dma_sem(f"agg_got{h}") for h in range(2)]
    with ExitStack() as ctx:
        sb, ps = tensors(nc, ctx)
        rows = sb("rows", [P, GROUP, width])
        oh = [sb(f"oh{h}", [P, HALF, P]) for h in range(2)]
        away = sb("away", [P, HALF, P])
        if weights is not None:
            minus = sb("minus", [P, COLS])
        k.gidx = [sb(f"gidx{h}", [P, GROUP], I32) for h in range(2)]
        pacc = ps("pacc", [P, 4, 512])
        with nc.Block() as block:
            @block.gpsimd
            def _(pool):
                gather_loop(k, pool, meta, field, rows, table, rdone, got, gate, staged)

            @block.tensor
            def _(pe):
                pe.sem_inc(rdone, GROUP)
                with pe.Fori(0, STEPS) as i:
                    for h in range(2):
                        pe.wait_ge(hot, i * 2 + h + 1)
                        pe.wait_ge(got[h], (i + 1) * (16 * HALF))
                        for j in range(HALF):
                            n = h * HALF + j
                            pe.wait_ge(added, i * GROUP + n + 1)
                            pe.matmul(pacc[:, n % 4, 0:width], oh[h][:, j, :], rows[:, n, :],
                                      start=True, stop=True).then_inc(rdone, 1)

            @block.scalar
            def _(act):
                if weights is not None:
                    act.activation(minus[:], weights[:], ACT.Copy, scale=-1.0)
                with act.Fori(0, STEPS) as i:
                    for h in range(2):
                        g = i * 2 + h
                        act.drain()
                        distances(k, act, away, meta, g * HALF)
                        act.drain()
                        act.wait_ge(rdone, g * HALF + HALF)
                        if weights is None:
                            mm = act.activation(oh[h][:], away[:], ACT.Relu, scale=-1.0, bias=1.0)
                        else:
                            for j in range(HALF):
                                mm = act.activation(oh[h][:, j, :], away[:, j, :], ACT.Relu,
                                                    scale=minus[:, ds(g * HALF + j, 1)],
                                                    bias=weights[:, ds(g * HALF + j, 1)])
                        mm.then_inc(hot, 1)

            @block.vector
            def _(dve):
                dve.memset(acc[:], 0.0)
                dve.sem_inc(added, 4)
                dve.drain()
                with dve.Fori(0, STEPS) as i:
                    for h in range(2):
                        bs = node_tiles(k, mybir.EngineType.DVE, btile, i * GROUP + h * HALF, HALF)
                        for j in range(HALF):
                            n = h * HALF + j
                            dve.wait_ge(rdone, i * GROUP + n + 1 + GROUP)
                            dve.wait_ge(added, i * GROUP + n + 4)
                            dve.tensor_tensor(acc[:, ds(bs[j], 1), 0:width], acc[:, ds(bs[j], 1), 0:width],
                                              pacc[:, n % 4:n % 4 + 1, 0:width], ALU.add).then_inc(added, 1)


def look_up_weights(k, ctx, meta, btile, inv, wedge):
    sb, ps = tensors(k.nc, ctx)
    hot, turn, copied, look, used = (k.sem(f"look_{s}") for s in ("hot", "turned", "copied", "looked", "used"))
    oh = [sb(f"loh{h}", [P, HALF, P]) for h in range(2)]
    th = [sb(f"lth{h}", [P, HALF, NTYPE]) for h in range(2)]
    ohT = [sb(f"lohT{h}", [P, HALF, P]) for h in range(2)]
    sel = sb("sel", [P, HALF, NTYPE])
    pc = [ps(f"plook{h}", [P, 512]) for h in range(2)]
    pT = [ps(f"plT{h}", [P, 3, 4, P]) for h in range(2)]
    mf = meta[:].bitcast(F32)

    def tensor(pe):
        def turn_group(h, g):
            pe.wait_ge(hot, g + 1)
            pe.wait_ge(copied, g + 1)
            for j in range(HALF):
                mm = pe.transpose(pT[h][:, j // 4, j % 4, :], oh[h][:, j, :], k.ident)
            mm.then_inc(turn, 1)

        def body(i, last):
            for h in range(2):
                g = i * 2 + h
                if not (last and h == 1):
                    turn_group(1 - h, g + 1)
                pe.wait_ge(copied, g + 3)
                pe.wait_ge(used, g + 1)
                bs = node_tiles(k, mybir.EngineType.PE, btile, g * HALF, HALF)
                for j in range(HALF):
                    mm = pe.matmul(pc[h][:, j * NTYPE:(j + 1) * NTYPE], ohT[h][:, j, :], inv[:, ds(bs[j], 1), :],
                                   start=True, stop=True)
                mm.then_inc(look, 1)
        pe.sem_inc(look, 2)
        turn_group(0, 0)
        with pe.Fori(0, STEPS - 1) as i:
            body(i, False)
        body(STEPS - 1, True)

    def scalar(act):
        act.sem_inc(copied, 2)
        with act.Fori(0, STEPS) as i:
            for h in range(2):
                g = i * 2 + h
                act.wait_ge(turn, g + 1)
                act.wait_ge(look, g + 1)
                copy_turned(act, ohT[h], pT[h])
                act.drain().then_inc(copied, 1)

    def vector(dve):
        def hots(h, g):
            onehots(k, dve, oh[h][:], meta, g * HALF)
            dve.tensor_tensor(th[h][:], k.iota[:, 0:NTYPE].unsqueeze(1).broadcast_to([P, HALF, NTYPE]),
                              mf[:, ds(g * HALF, HALF), F_TYPE:F_TYPE + 1].broadcast_to([P, HALF, NTYPE]),
                              ALU.is_equal).then_inc(hot, 1)

        def body(i, last):
            for h in range(2):
                g = i * 2 + h
                dve.wait_ge(look, g + 3)
                dve.tensor_tensor(sel[:], pc[h][:, 0:HALF * NTYPE].rearrange("p (j c) -> p j c", c=NTYPE),
                                  th[h][:], ALU.mult)
                dve.drain().then_inc(used, 1)
                dve.tensor_reduce(wedge[:, ds(g * HALF, HALF)], sel[:], AX.X, ALU.add)
                if not last:
                    hots(h, g + 2)
                dve.drain()
        dve.memset(wedge[:], 0.0)
        dve.drain()
        dve.sem_inc(used, 2)
        hots(0, 0)
        hots(1, 1)
        with dve.Fori(0, STEPS - 1) as i:
            body(i, False)
        body(STEPS - 1, True)
    return {"tensor": tensor, "scalar": scalar, "vector": vector}


def copy_turned(act, out, banks):
    for q in range(2):
        act.activation(out[:, 4 * q:4 * q + 4, :], banks[:, q, :, :], ACT.Copy)
    act.activation(out[:, 8:HALF, :], banks[:, 2, 0:HALF - 8, :], ACT.Copy)


def attention_aggregate(k, meta, btile, start, table, acc):
    nc = k.nc
    rdone, added, gate, staged = (k.sem(f"att_{s}") for s in ("rows_done", "added", "gate", "staged"))
    coded, hot, turn, copied, look, eused = (
        k.sem(f"att_{s}") for s in ("coded", "hot", "turned", "copied", "looked", "eused"))
    top, topT, topr, topb, newtop, prob, msg = (
        k.sem(f"att_{s}") for s in ("top", "topT", "topr", "topb", "newtop", "prob", "msg"))
    split, last_top, factors = k.sem("att_split"), k.sem("att_last_top"), k.sem("att_factors")
    got = [k.dma_sem(f"att_got{h}") for h in range(2)]
    AH = 2 * HALF
    AG = 2 * AH
    ASTEPS = TILES // AG
    GROUPS = ASTEPS * 2
    PARTS = 3
    TERMS = PARTS * HEADS
    with ExitStack() as ctx:
        sb, ps = tensors(nc, ctx)
        rows = sb("rows", [P, AG, TW])
        oh = [sb(f"oh{h}", [P, AH, P]) for h in range(2)]
        away = sb("away", [P, AH, P], BF16)
        code = [sb(f"code{h}", [P, AH, P], BF16) for h in range(2)]
        codeT = sb("codeT", [P, AH, P], BF16)
        idb = sb("idb", [P, P], BF16)
        adb = sb("adb", [P, NT, TERMS], BF16)
        rest = sb("rest", [P, NT, HEADS])
        k.gidx = [sb(f"gidx{h}", [P, GROUP], I32) for h in range(2)]
        term = sb("term", [P, AH, HEADS])
        e = sb("e", [P, AH, HEADS])
        pen = sb("pen", [P, AH])
        mx = sb("mx", [P, 1])
        mrow = sb("mrow", [1, 1])
        ref = [sb(f"ref{h}", [P, 1]) for h in range(2)]
        nref = sb("nref", [P, 1])
        drop = sb("drop", [P, 1])
        fac = [sb(f"fac{h}", [P, 1]) for h in range(2)]
        tops = sb("tops", [P, GROUPS])
        before = sb("before", [P, NT, GROUPS])
        scale = sb("scale", [P, NT])
        rden = sb("rden", [P, NT, HEADS])
        pT = ps("pT", [P, 2, 8, P], BF16)
        pterm = ps("pterm", [P, 512])
        ptop = ps("ptop", [P, 512])
        pacc = ps("pacc", [P, 4, 512])
        mf = meta[:].bitcast(F32)

        def gpsimd(pool):
            gather_loop(k, pool, meta, F_OTHER, rows, table, rdone, got, gate, staged, half=AH)

        def tensor(pe):
            def turn_half(h, g, q):
                pe.wait_ge(coded, g + 1)
                pe.wait_ge(copied, g * 2 + q + 1)
                for j in range(HALF):
                    mm = pe.transpose(pT[:, j // 8, j % 8, :], code[h][:, q * HALF + j, :], idb[:])
                mm.then_inc(turn, 1)

            def destinations(h, g):
                for q in range(2):
                    bs = node_tiles(k, mybir.EngineType.PE, btile, g * AH + q * HALF, HALF)
                    pe.wait_ge(copied, g * 2 + 3)
                    pe.wait_ge(eused, g + 1)
                    for j in range(HALF):
                        n = q * HALF + j
                        mm = pe.matmul(pterm[:, n * TERMS:(n + 1) * TERMS], codeT[:, n, :],
                                       adb[:, ds(bs[j], 1), :], start=True, stop=True)
                mm.then_inc(look, 1)

            def partition_tops(g):
                pe.wait_ge(top, g + 1)
                pe.transpose(ptop[0:1, 0:P], mx[:], k.ident).then_inc(topT, 1)

            def spread_top(g):
                pe.wait_ge(topr, g + 1)
                pe.matmul(ptop[:, 0:1], k.ones[0:1, :], mrow[:], start=True, stop=True).then_inc(topb, 1)

            def body(i, last):
                for h in range(2):
                    g = i * 2 + h
                    second = not (last and h == 1)
                    third = not last
                    for j in range(AH):
                        n = h * AH + j
                        if j == 0:
                            pe.wait_ge(hot, g + 1)
                            pe.wait_ge(msg, g * 4 + 4)
                        pe.wait_ge(added, i * AG + n + 1)
                        pe.matmul(pacc[:, n % 4, 0:TW], oh[h][:, j, :], rows[:, n, :],
                                  start=True, stop=True).then_inc(rdone, 1)
                        if third and j in (0, 4):
                            turn_half(h, g + 2, j // 4)
                        if second and j == 6:
                            partition_tops(g + 1)
                        if second and j == 9:
                            spread_top(g + 1)
                        if third and j == 15:
                            destinations(h, g + 2)
            pe.sem_inc(rdone, AG)
            pe.sem_inc(look, 1)
            for q in range(2):
                turn_half(0, 0, q)
            pe.wait_ge(split, 1)
            destinations(0, 0)
            for q in range(2):
                turn_half(1, 1, q)
            partition_tops(0)
            spread_top(0)
            destinations(1, 1)
            with pe.Fori(0, ASTEPS - 1) as i:
                body(i, False)
            body(ASTEPS - 1, True)

        def scalar(act):
            def encode(h, g):
                distances(k, act, away, meta, g * AH, AH)
                act.drain()
                act.activation(code[h][:], away[:], ACT.Relu, scale=-1.0, bias=1.0)
                act.drain().then_inc(coded, 1)

            def widen(h):
                act.activation(oh[h][:], code[h][:], ACT.Copy).then_inc(hot, 1)

            def copy_group(g):
                act.wait_ge(look, g + 1)
                for q in range(2):
                    act.wait_ge(turn, g * 2 + q + 1)
                    act.activation(codeT[:, q * HALF:q * HALF + 8, :], pT[:, 0, :, :], ACT.Copy)
                    act.activation(codeT[:, q * HALF + 8:(q + 1) * HALF, :], pT[:, 1, 0:HALF - 8, :], ACT.Copy)
                    act.drain().then_inc(copied, 1)

            def powers(h, g):
                act.wait_ge(newtop, g + 1)
                act.activation(rows[:, h * AH:(h + 1) * AH, D:TW], e[:], ACT.Exp, bias=nref[:])
                act.activation(fac[h][:], drop[:], ACT.Exp)
                act.drain().then_inc(prob, 1)

            def body(i, last):
                for h in range(2):
                    g = i * 2 + h
                    if not last:
                        copy_group(g + 2)
                    if not (last and h == 1):
                        powers(1 - h, g + 1)
                    if not last:
                        encode(1 - h, g + 3)
                    if not last:
                        act.wait_ge(rdone, i * AG + (h + 1) * AH + AG)
                        widen(h)
            act.activation(idb[:], k.ident, ACT.Copy)
            act.sem_inc(copied, 1)
            encode(0, 0)
            widen(0)
            copy_group(0)
            encode(1, 1)
            widen(1)
            copy_group(1)
            encode(0, 2)
            powers(0, 0)
            with act.Fori(0, ASTEPS - 1) as i:
                body(i, False)
            body(ASTEPS - 1, True)
            act.wait_ge(last_top, 1)
            act.activation(scale[:], scale[:], ACT.Exp).then_inc(factors, 1)

        def vector(dve):
            def scores(i, h, g):
                dve.tensor_scalar(pen[:], mf[:, ds(g * AH, AH), F_LOCAL], 0.0, -LOWEST, ALU.min, ALU.mult)
                dve.wait_ge(look, g + 2)
                dve.tensor_reduce(term[:], pterm[:, 0:AH * TERMS].rearrange("p (j s c) -> p j c s", s=PARTS, c=HEADS),
                                  AX.X, ALU.add)
                dve.drain().then_inc(eused, 1)
                dve.wait_ge(got[h], (i + 1) * (16 * AH))
                dve.tensor_tensor(e[:], rows[:, h * AH:(h + 1) * AH, D:TW], term[:], ALU.add)
                dve.drain()
                dve.scalar_tensor_tensor(out=e[:], in0=e[:], scalar=0.2, in1=e[:], op0=ALU.mult, op1=ALU.max)
                dve.drain()
                dve.tensor_tensor(e[:], e[:], mf[:, ds(g * AH, AH), F_WEIGHT:F_WEIGHT + 1]
                                  .broadcast_to([P, AH, HEADS]), ALU.mult)
                dve.drain()
                dve.tensor_tensor(e[:], e[:], pen[:].unsqueeze(2).broadcast_to([P, AH, HEADS]), ALU.add)
                dve.drain()
                dve.tensor_reduce(mx[:], e[:], AX.XY, ALU.max).then_inc(top, 1)

            def group_top(g):
                dve.wait_ge(topT, g + 1)
                dve.tensor_reduce(mrow[:], ptop[0:1, 0:P], AX.X, ALU.max).then_inc(topr, 1)

            def new_top(h, g):
                dve.wait_ge(topb, g + 1)
                dve.tensor_tensor(ref[h][:], ref[1 - h][:], ptop[:, 0:1], ALU.max)
                dve.drain()
                dve.tensor_tensor(drop[:], ref[1 - h][:], ref[h][:], ALU.subtract)
                dve.tensor_copy(tops[:, ds(g, 1)], ref[h][:])
                dve.tensor_scalar(nref[:], ref[h][:], -1.0, None, ALU.mult)
                dve.drain().then_inc(newtop, 1)

            def messages(h, g, q):
                dve.wait_ge(prob, g + 1)
                part = rows[:, h * AH + q * (AH // 4):h * AH + (q + 1) * (AH // 4), :]
                dve.tensor_tensor(part[:, :, 0:D].rearrange("p j (a b) -> p j a b", a=HEADS),
                                  part[:, :, 0:D].rearrange("p j (a b) -> p j a b", a=HEADS),
                                  part[:, :, D:TW].unsqueeze(3).broadcast_to([P, AH // 4, HEADS, HD]),
                                  ALU.mult).then_inc(msg, 1)

            def add(i, h, j, b):
                n = h * AH + j
                dve.wait_ge(rdone, i * AG + n + 1 + AG)
                dve.wait_ge(added, i * AG + n + 4)
                into, sums = acc[:, ds(b, 1), :], pacc[:, n % 4:n % 4 + 1, 0:TW]
                if j == 0:
                    dve.scalar_tensor_tensor(out=into, in0=into, scalar=fac[h][:], in1=sums,
                                             op0=ALU.mult, op1=ALU.add).then_inc(added, 1)
                else:
                    dve.tensor_tensor(into, into, sums, ALU.add).then_inc(added, 1)

            def body(i, last):
                for h in range(2):
                    g = i * 2 + h
                    ahead = not (last and h == 1)
                    for j in range(AH):
                        if j % HALF == 0:
                            bs = node_tiles(k, mybir.EngineType.DVE, btile, i * AG + h * AH + j, HALF)
                        add(i, h, j, bs[j % HALF])
                        if ahead and j == 2:
                            scores(i + h, 1 - h, g + 1)
                        if ahead and j == 6:
                            group_top(g + 1)
                        if ahead and j == 9:
                            new_top(1 - h, g + 1)
                        if ahead and j in (12, 14, 16, 18):
                            messages(1 - h, g + 1, j // 2 - 6)
            dve.tensor_copy(rest[:], k.ad[:])
            dve.memset(acc[:], 0.0)
            for s in range(PARTS):
                part = adb[:, :, s * HEADS:(s + 1) * HEADS]
                dve.drain()
                dve.tensor_copy(part, rest[:])
                dve.drain()
                if s < PARTS - 1:
                    dve.tensor_tensor(rest[:], rest[:], part, ALU.subtract)
            dve.memset(ref[1][:], LOWEST)
            dve.sem_inc(added, 4)
            dve.sem_inc(eused, 1)
            dve.drain().then_inc(split, 1)
            scores(0, 0, 0)
            group_top(0)
            new_top(0, 0)
            for q in range(4):
                messages(0, 0, q)
            with dve.Fori(0, ASTEPS - 1) as i:
                body(i, False)
            body(ASTEPS - 1, True)
            dve.drain()
            dve.tensor_tensor(before[:], k.tile_iota[:, 0:TILES:AH].unsqueeze(1).broadcast_to([P, NT, GROUPS]),
                              start[:, 1:NT + 1].unsqueeze(2).broadcast_to([P, NT, GROUPS]), ALU.is_lt)
            dve.drain()
            dve.tensor_scalar(before[:], before[:], 1.0, 3.0e38, ALU.subtract, ALU.mult)
            dve.drain()
            dve.tensor_tensor(before[:], before[:], tops[:].unsqueeze(1).broadcast_to([P, NT, GROUPS]), ALU.add)
            dve.drain()
            dve.tensor_reduce(scale[:], before[:], AX.X, ALU.max)
            dve.drain()
            dve.tensor_scalar(scale[:], scale[:], tops[:, GROUPS - 1:GROUPS], None, ALU.subtract).then_inc(last_top, 1)
            dve.wait_ge(factors, 1)
            dve.tensor_tensor(rden[:], acc[:, :, D:TW], scale[:].unsqueeze(2).broadcast_to([P, NT, HEADS]), ALU.mult)
            dve.drain()
            dve.tensor_scalar(rden[:], rden[:], 1e-10, None, ALU.add)
            dve.drain()
            dve.reciprocal(rden[:], rden[:])
            dve.drain()
            dve.tensor_tensor(rden[:], rden[:], scale[:].unsqueeze(2).broadcast_to([P, NT, HEADS]), ALU.mult)
            dve.drain()
            sums = acc[:, :, 0:D].rearrange("p t (a b) -> p t a b", a=HEADS)
            dve.tensor_tensor(sums, sums, rden[:].unsqueeze(3).broadcast_to([P, NT, HEADS, HD]), ALU.mult)
            dve.drain()
            dve.tensor_tensor(k.x[:], k.x[:], acc[:, :, 0:D], ALU.add)
        run(k, {"gpsimd": gpsimd, "tensor": tensor, "scalar": scalar, "vector": vector})


GATE_PARTS = {"top1": 1, "soft2": 3, "share2": 3}


def gates(k, ctx, lg, experts, kind):
    nc = k.nc
    sb, ps = tensors(nc, ctx)
    EP = experts
    rows = experts * GATE_PARTS[kind]
    WR = 32
    BANK = 4
    part = sb("part", [P, NT, EP], BF16)
    top = sb("top", [P, NT, 2])
    second = sb("second", [P, NT, EP])
    w = sb("w", [P, NT, WR])
    tmp = sb("tmp", [P, NT, EP])
    one = sb("one", [P, NT, 2])
    pt = ps("pt", [P, 2, 512])
    shift, powered, diff, powd, ready, turned, taken = (
        k.sem(f"gate_{s}") for s in ("shift", "powered", "diff", "powd", "ready", "turned", "taken"))
    def vector(dve):
        dve.memset(k.gates[:, NP_:], 0.0)
        def both(a, n):
            return a.broadcast_to([P, NT, n])
        dve.memset(w[:], 0.0)
        if kind != "top1":
            dve.tensor_reduce(one[:, :, 0:1], lg[:], AX.X, ALU.max)
            dve.drain()
            dve.tensor_tensor(lg[:], lg[:], both(one[:, :, 0:1], EP), ALU.subtract)
            dve.drain().then_inc(shift, 1)
            dve.wait_ge(powered, 1)
            dve.tensor_reduce(one[:, :, 0:1], lg[:], AX.X, ALU.add)
            dve.drain()
            dve.reciprocal(one[:, :, 1:2], one[:, :, 0:1])
            dve.drain()
            dve.tensor_tensor(lg[:], lg[:], both(one[:, :, 1:2], EP), ALU.mult)
        dve.drain()
        iota = k.iota[:, 0:experts].unsqueeze(1).broadcast_to([P, NT, experts])

        def first_largest(n, values, out):
            dve.tensor_reduce(top[:, :, n:n + 1], values, AX.X, ALU.max)
            dve.drain()
            dve.tensor_tensor(tmp[:], values, both(top[:, :, n:n + 1], EP), ALU.is_equal)
            dve.drain()
            dve.tensor_scalar(tmp[:], tmp[:], -float(P), None, ALU.mult)
            dve.drain()
            dve.tensor_tensor(tmp[:], tmp[:], iota, ALU.add)
            dve.drain()
            dve.tensor_reduce(one[:, :, 0:1], tmp[:], AX.X, ALU.min)
            dve.drain()
            dve.tensor_tensor(out, tmp[:], both(one[:, :, 0:1], EP), ALU.is_equal)
            dve.drain()
        first_largest(0, lg[:], w[:, :, 0:experts])
        if kind != "top1":
            dve.scalar_tensor_tensor(out=lg[:], in0=w[:, :, 0:experts], scalar=-2.0, in1=lg[:],
                                     op0=ALU.mult, op1=ALU.add)
            dve.drain()
            first_largest(1, lg[:], second[:])
        if kind == "soft2":
            dve.tensor_tensor(one[:, :, 1:2], top[:, :, 1:2], top[:, :, 0:1], ALU.subtract)
            dve.drain().then_inc(diff, 1)
            dve.wait_ge(powd, 1)
            dve.tensor_scalar(one[:, :, 0:1], one[:, :, 1:2], 1.0, None, ALU.add)
            dve.drain()
            dve.reciprocal(one[:, :, 0:1], one[:, :, 0:1])
            dve.drain()
            dve.tensor_tensor(one[:, :, 1:2], one[:, :, 1:2], one[:, :, 0:1], ALU.mult)
        elif kind == "share2":
            dve.tensor_tensor(one[:, :, 0:1], top[:, :, 0:1], top[:, :, 1:2], ALU.add)
            dve.drain()
            dve.tensor_scalar(one[:, :, 0:1], one[:, :, 0:1], 1e-12, None, ALU.max)
            dve.drain()
            dve.reciprocal(one[:, :, 0:1], one[:, :, 0:1])
            dve.drain()
            dve.tensor_tensor(one[:, :, 1:2], top[:, :, 1:2], one[:, :, 0:1], ALU.mult)
            dve.tensor_tensor(one[:, :, 0:1], top[:, :, 0:1], one[:, :, 0:1], ALU.mult)
        dve.drain()
        if kind != "top1":
            dve.tensor_tensor(w[:, :, 0:experts], w[:, :, 0:experts], both(one[:, :, 0:1], experts), ALU.mult)
            dve.tensor_tensor(second[:], second[:], both(one[:, :, 1:2], experts), ALU.mult)
            dve.drain()
            dve.tensor_tensor(w[:, :, 0:experts], w[:, :, 0:experts], second[:], ALU.add)
            dve.drain()
            dve.tensor_copy(part[:], w[:, :, 0:experts])
            dve.drain()
            dve.tensor_tensor(second[:], w[:, :, 0:experts], part[:], ALU.subtract)
            dve.drain()
            dve.tensor_copy(w[:, :, 0:experts], part[:])
            dve.drain()
            dve.tensor_copy(part[:], second[:])
            dve.drain()
            dve.tensor_copy(w[:, :, experts:2 * experts], part[:])
            dve.tensor_tensor(w[:, :, 2 * experts:rows], second[:], part[:], ALU.subtract)
            dve.drain()

        dve.drain().then_inc(ready, 1)

    def scalar(act):
        if kind != "top1":
            act.wait_ge(shift, 1)
            act.activation(lg[:], lg[:], ACT.Exp).then_inc(powered, 1)
        if kind == "soft2":
            act.wait_ge(diff, 1)
            act.activation(one[:, :, 1:2], one[:, :, 1:2], ACT.Exp).then_inc(powd, 1)
        act.sem_inc(taken, 2)
        for q, t in enumerate(range(0, NT, BANK)):
            n = min(BANK, NT - t) * P
            act.wait_ge(turned, q + 1)
            act.activation(k.gates[0:rows, t * P:t * P + n], pt[0:rows, q % 2, 0:n], ACT.Copy).then_inc(taken, 1)

    def tensor(pe):
        pe.wait_ge(ready, 1)
        for q, t in enumerate(range(0, NT, BANK)):
            pe.wait_ge(taken, q + 1)
            for j in range(min(BANK, NT - t)):
                mm = pe.transpose(pt[0:WR, q % 2, j * P:(j + 1) * P], w[:, t + j, :], k.ident)
            mm.then_inc(turned, 1)
    return {"vector": vector, "scalar": scalar, "tensor": tensor}


class Network:

    def __init__(self, k, ctx, chunks, experts, w1d, b1d, w2d, b2d, seld=None):
        sb, _ = tensors(k.nc, ctx)
        self.chunks, self.experts = chunks, experts
        self.loaded = k.dma_sem("ff_loaded")
        self.w1 = sb("w1", [P, KC, chunks * P])
        self.b1 = sb("b1", [P, chunks])
        self.w2 = sb("w2", [P, chunks, D])
        self.rows = seld.shape[0] if seld is not None else 1
        self.b2 = sb("b2", [self.rows, D])
        self.sel = sb("sel", [self.rows, chunks * P], BF16) if seld is not None else None
        pairs = [(self.w1, w1d), (self.b1, b1d), (self.w2, w2d)]
        pairs += [(self.b2[r:r + experts], b2d) for r in range(0, self.rows, experts)]
        if seld is not None:
            pairs.append((self.sel, seld))
        self.bytes_in = 16 * len(pairs)

        def sync(sp):
            for a, b in pairs:
                sp.dma_start(a[:], b).then_inc(self.loaded, 16)
        self.part = {"sync": sync}


def feed_forward(k, F, func, finish, rank=None):
    nc = k.nc
    G = 4
    ng = F.chunks // G
    w1, b1, w2, b2, sel, experts, loaded = F.w1, F.b1, F.w2, F.b2, F.sel, F.rows, F.loaded
    gstaged = k.sem("ff_gates")
    hid, act_, gated, osum, fin = (k.sem(f"ff_{s}") for s in ("hidden", "active", "gated", "summed", "finished"))
    with ExitStack() as ctx:
        sb, ps = tensors(nc, ctx)
        gt = [sb(f"gt{i}", [experts, P]) for i in range(2)]
        h = [sb(f"h{i}", [P, G, P]) for i in range(2)]
        hm = [sb(f"hm{i}", [P, G, P]) for i in range(2)] if sel is not None else h
        ph = [ps(f"ph{i}", [P, G, P]) for i in range(2)]
        pm = [ps(f"pm{i}", [P, G, P]) for i in range(2)] if sel is not None else None
        po = ps("po", [P, 2, 512])
        used = gated if sel is not None else act_
        with nc.Block() as block:
            @block.tensor
            def _(pe):
                def hidden(t, g, s):
                    pe.wait_ge(act_, s + 1)
                    if sel is not None:
                        pe.wait_ge(gated, s + 1)
                    for j in range(G):
                        n = g * G + j
                        for c in range(KC):
                            mm = pe.matmul(ph[g % 2][:, j, :], w1[:, c, n * P:(n + 1) * P], k.yT[:, c, ds(t * P, P)],
                                           start=(c == 0), stop=(c == KC - 1))
                    if sel is not None:
                        for j in range(G):
                            n = g * G + j
                            mm = pe.matmul(pm[g % 2][:, j, :], sel[:, n * P:(n + 1) * P],
                                           k.gates[0:experts, ds(t * P, P)], start=True, stop=True)
                    mm.then_inc(hid, 1)
                pe.sem_inc(osum, 2)
                pe.wait_ge(loaded, F.bytes_in)
                hidden(0, 0, 0)

                def tile(t, q):
                    for g in range(ng):
                        s = t * ng + g
                        hidden(t + (g + 1) // ng, (g + 1) % ng, s + 1)
                        pe.wait_ge(used, s + 3)
                        if g == 0:
                            pe.wait_ge(fin, t + 1)
                        for j in range(G):
                            mm = pe.matmul(po[:, q, 0:D], hm[g % 2][:, j, :], w2[:, g * G + j, :],
                                           start=(g == 0 and j == 0), stop=False)
                        if g < ng - 1:
                            mm.then_inc(osum, 1)
                    lhs = gt[q][:] if experts > 1 else k.ones[0:1, :]
                    if experts > 1:
                        pe.wait_ge(gstaged, t + 1)
                    pe.matmul(po[:, q, 0:D], lhs, b2[:], start=False, stop=True).then_inc(osum, 1)
                by_turns(pe, tile)

            @block.scalar
            def _(act):
                act.sem_inc(act_, 2)
                if rank is not None:
                    act.sem_inc(fin, 2)
                act.wait_ge(loaded, F.bytes_in)

                def keep(t, q):
                    act.wait_ge(osum, t * ng + ng + 2)
                    act.activation(k.z[:, ds(t, 1), 0:D], po[:, q, 0:D].unsqueeze(1), ACT.Copy).then_inc(fin, 1)

                def tile(t, q):
                    for g in range(ng):
                        s = t * ng + g
                        act.wait_ge(hid, s + 1)
                        act.wait_ge(gated if sel is not None else osum, s + 1)
                        for j in range(G):
                            mm = act.activation(h[g % 2][:, j, :], ph[g % 2][:, j, :], func,
                                                bias=b1[:, g * G + j:g * G + j + 1])
                        mm.then_inc(act_, 1)
                        if g == 0 and rank is not None and not isinstance(t, int):
                            keep(t - 1, 1 - q)
                by_turns(act, tile)
                if rank is not None:
                    keep(NT - 1, 0)

            if rank is not None:
                @block.gpsimd
                def _(pool):
                    pool.tensor_tensor(k.x[:], k.x[:], k.y[:], ALU.add)

            @block.vector
            def _(dve):
                if rank is not None:
                    rank(dve)
                    return
                dve.sem_inc(gated, 2)
                dve.sem_inc(fin, 2)

                def end(t, q):
                    dve.wait_ge(osum, t * ng + ng + 2)
                    finish(dve, t, po[:, q, 0:D].unsqueeze(1))
                    dve.drain().then_inc(fin, 1)

                def tile(t, q):
                    dve.tensor_copy(gt[q][:], k.gates[0:experts, ds(t * P, P)]).then_inc(gstaged, 1)
                    for g in range(ng):
                        s = t * ng + g
                        dve.wait_ge(act_, s + 3)
                        dve.wait_ge(osum, s + 1)
                        dve.tensor_tensor(hm[g % 2][:], h[g % 2][:], pm[g % 2][:], ALU.mult).then_inc(gated, 1)
                        if g == 0 and not isinstance(t, int):
                            end(t - 1, 1 - q)
                by_turns(dve, tile)
                end(NT - 1, 0)


def shared_and_experts(k, A):
    nc = k.nc
    loaded = k.dma_sem("moe1_loaded")
    l1, a1, l2, a2, gt, osum, fin = (k.sem(f"moe1_{s}") for s in (
        "first", "act1", "second", "act2", "gated", "out", "fin"))
    NX = 4
    ROWS = NX * GATE_PARTS["soft2"]
    gstaged = k.sem("moe1_gates")
    with ExitStack() as ctx:
        sb, ps = tensors(nc, ctx)
        w1 = sb("w1", [P, KC, 6 * P])
        w2 = sb("w2", [P, 6, P])
        w3 = sb("w3", [P, 3, D])
        b1 = sb("b1", [P, 6])
        b2 = sb("b2", [P, 3])
        b3 = sb("b3", [ROWS, D])
        sb3 = sb("sb3", [1, D])
        sel = sb("sel", [ROWS, 2 * P], BF16)
        gtile = sb("gtile", [ROWS, P])
        h1 = [sb(f"h1{i}", [P, 6, P]) for i in range(2)]
        h2 = [sb(f"h2{i}", [P, 3, P]) for i in range(2)]
        p1 = ps("p1", [P, 2, 4, P])
        p2 = ps("p2", [P, 4, P])
        pm = ps("pm", [P, 4, P])
        po = ps("po", [P, 512])
        with nc.Block() as block:
            @block.sync
            def _(sp):
                for a, n in ((w1, "m1_w1"), (w2, "m1_w2"), (w3, "m1_w3"), (b1, "m1_b1"), (b2, "m1_b2"),
                             *((b3[r:r + NX], "m1_b3") for r in range(0, ROWS, NX)), (sb3, "m1_sb3"), (sel, "sel1")):
                    sp.dma_start(a[:], A[n]).then_inc(loaded, 16)

            @block.tensor
            def _(pe):
                def first(t):
                    pe.wait_ge(a1, t + 1)
                    for n in range(6):
                        for c in range(KC):
                            mm = pe.matmul(p1[:, n // 4, n % 4, :], w1[:, c, n * P:(n + 1) * P],
                                           k.yT[:, c, ds(t * P, P)], start=(c == 0), stop=(c == KC - 1))
                    mm.then_inc(l1, 1)
                pe.sem_inc(osum, 1)
                pe.wait_ge(loaded, 16 * 10)
                first(0)
                with pe.Fori(0, NT) as t:
                    pe.wait_ge(a1, t + 2)
                    pe.wait_ge(gt, t + 1)
                    for n, of in ((0, 0), (1, 0), (2, 1), (3, 1), (4, 2), (5, 2)):
                        mm = pe.matmul(p2[:, of, :], w2[:, n, :], h1[0][:, n, :], start=(n % 2 == 0), stop=(n % 2 == 1))
                    for n in range(2):
                        mm = pe.matmul(pm[:, n, :], sel[:, n * P:(n + 1) * P], k.gates[0:ROWS, ds(t * P, P)],
                                       start=True, stop=True)
                    mm.then_inc(l2, 1)
                    first(t + 1)
                    pe.wait_ge(gt, t + 2)
                    pe.wait_ge(fin, t + 1)
                    for n in range(3):
                        pe.matmul(po[:, 0:D], h2[1][:, n, :], w3[:, n, :], start=(n == 0), stop=False)
                    pe.wait_ge(gstaged, t + 1)
                    pe.matmul(po[:, 0:D], gtile[:], b3[:], start=False, stop=False)
                    pe.matmul(po[:, 0:D], k.ones[0:1, :], sb3[:], start=False, stop=True).then_inc(osum, 1)

            @block.scalar
            def _(act):
                act.sem_inc(a1, 1)
                act.wait_ge(loaded, 16 * 10)
                with act.Fori(0, NT) as t:
                    act.wait_ge(l1, t + 1)
                    act.wait_ge(l2, t + 1)
                    for n in range(6):
                        mm = act.activation(h1[0][:, n, :], p1[:, n // 4, n % 4, :], ACT.Relu, bias=b1[:, n:n + 1])
                    mm.then_inc(a1, 1)
                    act.wait_ge(l2, t + 2)
                    act.wait_ge(gt, t + 1)
                    for n in range(3):
                        mm = act.activation(h2[0][:, n, :], p2[:, n, :], ACT.Relu, bias=b2[:, n:n + 1])
                    mm.then_inc(a2, 1)

            @block.vector
            def _(dve):
                dve.sem_inc(gt, 1)
                dve.sem_inc(fin, 1)
                dve.sem_inc(l2, 1)
                with dve.Fori(0, NT) as t:
                    dve.wait_ge(a2, t + 1)
                    dve.wait_ge(osum, t + 1)
                    dve.tensor_copy(gtile[:], k.gates[0:ROWS, ds(t * P, P)]).then_inc(gstaged, 1)
                    dve.tensor_copy(h2[1][:, 0, :], h2[0][:, 0, :])
                    dve.tensor_tensor(h2[1][:, 1:3, :], h2[0][:, 1:3, :], pm[:, 0:2, :], ALU.mult)
                    dve.drain().then_inc(gt, 1)
                    dve.wait_ge(osum, t + 2)
                    dve.tensor_tensor(k.x[:, ds(t, 1), :], k.x[:, ds(t, 1), :], po[:, 0:D].unsqueeze(1), ALU.add)
                    dve.drain().then_inc(fin, 1)


def add_sums(k, acc):
    def vector(dve):
        dve.tensor_tensor(k.x[:], k.x[:], acc[:, :, 0:D], ALU.add)
    return {"vector": vector}


def inverse_counts(dve, rc, acc):
    dve.tensor_scalar(rc, acc[:, :, D:D + 1], 1.0, None, ALU.max)
    dve.drain()
    dve.reciprocal(rc, rc)
    dve.drain()


def means_to_table(k, acc, table):
    stored, ready = k.dma_sem("means_stored"), k.sem("means_ready")
    FEW = 5
    with ExitStack() as ctx:
        sb, _ = tensors(k.nc, ctx)
        rc = sb("rc", [P, NT, 1])

        def vector(dve):
            inverse_counts(dve, rc[:], acc)
            dve.memset(acc[:, :, D:TW], 1.0)
            for t in range(0, NT, FEW):
                some = acc[:, t:t + FEW, 0:D]
                dve.tensor_tensor(some, some, rc[:, t:t + FEW, :].broadcast_to([P, FEW, D]), ALU.mult)
                dve.drain().then_inc(ready, 1)

        def sync(sp):
            rows = table.rearrange("(t p) w -> p t w", p=P)
            for i, t in enumerate(range(0, NT, FEW)):
                sp.wait_ge(ready, i + 1)
                sp.dma_start(rows[:, t:t + FEW, :], acc[:, t:t + FEW, :]).then_inc(stored, 16)
            sp.wait_ge(stored, 16 * NT // FEW)
        run(k, {"vector": vector, "sync": sync})


def store_weights(k, wt, wrow_d):
    nc = k.nc
    turned, copied, stored = k.sem("rank_turned"), k.sem("rank_copied"), k.dma_sem("rank_stored")
    with ExitStack() as ctx:
        sb, ps = tensors(nc, ctx)
        pad = sb("pad", [P, P])
        rowt = sb("rowt", [NT, P])
        pt = ps("pt", [P, P])
        with nc.Block() as block:
            @block.vector
            def _(dve):
                dve.memset(pad[:], 0.0)
                dve.drain()
                dve.tensor_copy(pad[:, 0:NT], wt[:, :, 0])
                dve.drain().then_inc(copied, 1)
                dve.wait_ge(turned, 1)
                dve.tensor_copy(rowt[:], pt[0:NT, :]).then_inc(copied, 1)

            @block.tensor
            def _(pe):
                pe.wait_ge(copied, 1)
                pe.transpose(pt[:], pad[:], k.ident).then_inc(turned, 1)

            @block.sync
            def _(sp):
                sp.wait_ge(copied, 2)
                sp.dma_start(wrow_d, rowt[:]).then_inc(stored, 16)
                sp.wait_ge(stored, 16)


CHOSEN = max(1, N // 2) - 1


def build(nc, A, out):
    with ExitStack() as ctx:
        k = Kit(nc, ctx)
        sb, _ = tensors(nc, ctx)
        k.const = sb("const", [P, C_END])
        k.x = sb("x", [P, NT, D])
        k.yT = sb("yT", [P, KC, NP_ + P])
        graph = ctx.enter_context(ExitStack())
        gsb, _ = tensors(nc, graph)
        meta_d = gsb("meta_dst", [P, COLS, NF], I32)
        meta_s = gsb("meta_src", [P, COLS, NF], I32)
        bt_d = gsb("bt_dst", [1, COLS], I32)
        bt_s = gsb("bt_src", [1, COLS], I32)
        k.ad = gsb("ad", [P, NT, HEADS])
        wedge = gsb("wedge", [P, COLS])
        c = k.const
        k.ident, k.iota, k.tri, k.ones = (c[:, o:o + P] for o in (C_ID, C_IOTA, C_TRI, C_ONES))
        k.iota256 = c[:, C_IOTA:C_IOTA + 2 * P]
        k.tile_iota = c[:, C_TILE:C_TILE + COLS]
        slots_d, slots_s = k.dram("slots_dst", [P * COLS, NF], I32), k.dram("slots_src", [P * COLS, NF], I32)
        table = k.dram("table", [NP_, TW])
        table7 = k.dram("table7", [NP_, NTYPE * D])
        wrow_d = k.dram("wrow", [NT, P])

        start_s, start_d = gsb("start_src", [P, NT + 1]), gsb("start_dst", [P, NT + 1])
        inv = gsb("inv", [P, NT, NTYPE])

        with ExitStack() as part:
            psb, _ = tensors(nc, part)
            scratch = (psb("raw", [P, 4, EC], I32), psb("bint", [P, EC], I32), psb("coli", [P, EC], I32),
                       psb("bucket", [P, EC]), psb("one", [P, EC]), psb("mask", [P, EC]), psb("incl", [P, EC]),
                       psb("within", [P, EC]), psb("mask1", [P, EC]), psb("incl1", [P, EC]))
            by_dst = Sorting(k, part, "dst", slots_d, meta_d, bt_d, start_d)
            with ExitStack() as inner:
                by_src = Sorting(k, inner, "src", slots_s, meta_s, bt_s, start_s)
                by_src.renew(k)
                with ExitStack() as c1:
                    load_constants, load_x = load_state(k, A)
                    run(k, load_constants, rank_edges(k, c1, A, by_src, A["src"], A["dst"], scratch), load_x)
                by_src.renew(k)
                by_dst.renew(k)
                with ExitStack() as c2:
                    run(k, place_tiles(k, c2, by_src), count_types(k, c2, by_src, scratch[0], inv),
                        rank_edges(k, c2, A, by_dst, A["dst"], A["src"], scratch),
                        norm_product(k, c2, A["g0_w"], None, D, table=table, attention=A["g0_a"]),
                        scatter_edges(k, by_src))
            by_dst.renew(k)
            with ExitStack() as c3:
                run(k, look_up_weights(k, c3, meta_s, bt_s, inv, wedge), place_tiles(k, c3, by_dst),
                    scatter_edges(k, by_dst))

        with ExitStack() as part:
            psb, _ = tensors(nc, part)
            attention_aggregate(k, meta_d, bt_d, start_d, table, psb("acc", [P, NT, TW]))
        keep_y = ctx.enter_context(ExitStack())
        k.y = tensors(nc, keep_y)[0]("y", [P, NT, D])
        with ExitStack() as part:
            psb, _ = tensors(nc, part)
            k.gates = psb("gates", [32, NP_ + P], BF16)
            F = Network(k, part, 16, 32, A["f0_w1"], A["f0_b1"], A["f0_w2"], A["f0_b2"], A["sel0"])
            with ExitStack() as c:
                lg = tensors(nc, c)[0]("lg", [P, NT, 32])
                run(k, norm_product(k, c, A["f0_rw"], A["f0_rb"], 32, yT=True, out=lg),
                    gates(k, c, lg, 32, "top1"), F.part)

            def finish0(dve, t, po):
                dve.scalar_tensor_tensor(out=k.x[:, ds(t, 1), :], in0=po, scalar=0.0, in1=k.x[:, ds(t, 1), :],
                                         op0=ALU.max, op1=ALU.add)
            feed_forward(k, F, ACT.Relu, finish0)
            k.end_stage()

        with ExitStack() as c:
            run(k, norm_product(k, c, A["g1_w"], None, NTYPE * D, table=table7))
        with ExitStack() as part:
            psb, _ = tensors(nc, part)
            acc = psb("acc", [P, NT, TW])
            aggregate(k, meta_s, bt_s, F_TYPED, table7.rearrange("n (t d) -> (n t) d", t=NTYPE), wedge, acc)
            k.end_stage()
            k.gates = psb("gates", [32, NP_ + P], BF16)
            with ExitStack() as c:
                lg = tensors(nc, c)[0]("lg", [P, NT, 4])
                run(k, add_sums(k, acc), norm_product(k, c, A["m1_gw"], A["m1_gb"], 4, yT=True, out=lg),
                    gates(k, c, lg, 4, "soft2"))
            shared_and_experts(k, A)
            k.end_stage()

        with ExitStack() as c:
            run(k, norm_product(k, c, A["g2_w"], A["g2_b"], D, table=table, last_one=True))
        with ExitStack() as part:
            psb, _ = tensors(nc, part)
            acc = psb("acc", [P, NT, TW])
            aggregate(k, meta_s, bt_s, F_OTHER, table, None, acc)
            k.end_stage()
            run(k, add_sums(k, acc))
        with ExitStack() as part:
            psb, _ = tensors(nc, part)
            k.gates = psb("gates", [32, NP_ + P], BF16)
            F = Network(k, part, 16, 8, A["f2_w1"], A["f2_b1"], A["f2_w2"], A["f2_b2"], A["sel2"])
            with ExitStack() as c:
                lg = tensors(nc, c)[0]("lg", [P, NT, 8])
                run(k, norm_product(k, c, A["f2_rw"], None, 8, y=True, yT=True, out=lg),
                    gates(k, c, lg, 8, "share2"), F.part)

            def finish2(dve, t, po):
                dve.tensor_tensor(k.y[:, ds(t, 1), :], k.y[:, ds(t, 1), :], po, ALU.add)
                dve.drain()
                dve.tensor_tensor(k.x[:, ds(t, 1), :], k.x[:, ds(t, 1), :], k.y[:, ds(t, 1), :], ALU.add)
            feed_forward(k, F, ACT.Gelu, finish2)
            k.end_stage()

        with ExitStack() as part:
            psb, _ = tensors(nc, part)
            acc = psb("acc", [P, NT, TW])
            for last in range(2):
                with ExitStack() as c:
                    if last:
                        run(k, norm_product(k, c, A["g3_w2"], None, D, table=table, last_one=True,
                                            hyper=(acc, "g3_b1", A)))
                    else:
                        run(k, norm_product(k, c, A["g3_w1"], None, D, y=True, table=table, last_one=True))
                aggregate(k, meta_d, bt_d, F_OTHER, table, None, acc)
                k.end_stage()
                means_to_table(k, acc, table)
                aggregate(k, meta_s, bt_s, F_OTHER, table, None, acc)
                k.end_stage()
            with ExitStack() as c:
                run(k, hyper_to_x(k, c, A, acc, "g3_b2"))

        keep_y.close()
        graph.close()
        k.y = sb("y", [P, NT, D])

        with ExitStack() as part:
            psb, _ = tensors(nc, part)
            wt = psb("wt", [P, NT, 1])
            F = Network(k, part, 8, 1, A["f3_w1"], A["f3_b1"], A["f3_w2"], A["f3_b2"])
            with ExitStack() as c:
                run(k, norm_product(k, c, A["f3_wr"], A["f3_br"], 1, y=True, yT=True, out=wt), F.part)
            k.z = psb("z", [P, NT, D])
            store_weights(k, wt, wrow_d)
            k.end_stage()
            wall = psb("wall", [P, N])
            lower = psb("lower", [P, P])
            mask = psb("mask", [P, N], BF16)
            own = psb("own", [P, P], BF16)
            above = psb("above", [P, NT, 4])
            rank_of = psb("rank_of", [P, NT])
            got = k.dma_sem("rank_got")
            with nc.Block() as block:
                @block.sync
                def _(sp):
                    sp.dma_start(wall[:], wrow_d.rearrange("t p -> (t p)").unsqueeze(0)[:, 0:N].broadcast_to([P, N])).then_inc(got, 16)
                    sp.dma_start(lower[:], A["lower"]).then_inc(got, 16)

            def rank(dve):
                dve.wait_ge(got, 32)
                dve.memset(above[:], 0.0)
                dve.drain()
                for t in range(NT):
                    a, b = t * P, min((t + 1) * P, N)
                    weight = wt[:, t, :]
                    if a > 0:
                        dve.tensor_scalar(mask[:, 0:a], wall[:, 0:a], weight, 0.0, ALU.is_ge, ALU.add,
                                          accum_out=above[:, t, 0:1])
                    if b < N:
                        dve.tensor_scalar(mask[:, b:N], wall[:, b:N], weight, 0.0, ALU.is_gt, ALU.add,
                                          accum_out=above[:, t, 1:2])
                    dve.tensor_scalar(mask[:, a:b], wall[:, a:b], weight, 0.0, ALU.is_gt, ALU.add,
                                      accum_out=above[:, t, 2:3])
                    dve.scalar_tensor_tensor(out=own[:, 0:b - a], in0=wall[:, a:b], scalar=weight,
                                             in1=lower[:, 0:b - a], op0=ALU.is_equal, op1=ALU.mult,
                                             accum_out=above[:, t, 3:4])
                    dve.drain()
                dve.tensor_reduce(rank_of[:], above[:], AX.X, ALU.add)
                dve.drain()
                dve.tensor_scalar(rank_of[:], rank_of[:], float(CHOSEN), None, ALU.is_lt)
                dve.drain()
                dve.tensor_tensor(wt[:, :, 0], wt[:, :, 0], rank_of[:], ALU.mult)
            feed_forward(k, F, ACT.Gelu_apprx_tanh, None, rank=rank)
            k.end_stage()
            FEW = 5
            whole = N // (P * FEW)
            summed, stored = k.sem("summed"), k.dma_sem("stored")
            with nc.Block() as block:
                @block.vector
                def _(dve):
                    for t in range(NT):
                        mm = dve.scalar_tensor_tensor(out=k.x[:, t, :], in0=k.z[:, t, :], scalar=wt[:, t, :],
                                                      in1=k.x[:, t, :], op0=ALU.mult, op1=ALU.add)
                        if t % FEW == FEW - 1:
                            mm.then_inc(summed, 1)

                @block.sync
                def _(sp):
                    for i in range(whole):
                        sp.wait_ge(summed, i + 1)
                        sp.dma_start(out[i * FEW * P:(i + 1) * FEW * P, :].rearrange("(t p) d -> p t d", p=P),
                                     k.x[:, i * FEW:(i + 1) * FEW, :]).then_inc(stored, 16)
                    sp.wait_ge(summed, NT // FEW)
                    sp.dma_start(out[whole * FEW * P:(NT - 1) * P, :].rearrange("(t p) d -> p t d", p=P),
                                 k.x[:, whole * FEW:NT - 1, :]).then_inc(stored, 16)
                    sp.dma_start(out[(NT - 1) * P:N, :], k.x[0:NTAIL, NT - 1, :]).then_inc(stored, 16)
                    sp.wait_ge(stored, 16 * (whole + 2))


def constants():
    c = np.zeros((P, C_END), np.float32)
    c[:, C_ID:C_ID + P] = np.eye(P)
    c[:, C_IOTA:C_IOTA + 2 * P] = np.arange(2 * P)
    c[:, C_TRI:C_TRI + P] = np.triu(np.ones((P, P)), 1)
    c[:, C_ONES:C_ONES + P] = 1.0
    c[:, C_TILE:C_TILE + COLS] = np.arange(COLS)
    return c


def selector(experts, width):
    return np.arange(experts * width)[None, :] // width == np.arange(experts)[:, None]


def kernel(**inputs):
    import concourse.bacc as _bacc
    import ml_dtypes
    from concourse.bass_utils import run_bass_kernel_spmd as _run

    g = {n: np.asarray(v) for n, v in inputs.items()}

    def rows(w):
        return w.reshape(-1, P, w.shape[-1]).transpose(1, 0, 2)

    def column(b):
        return b.reshape(-1, P).T

    def spread(b):
        return np.broadcast_to(b.reshape(1, -1), (P, b.size))

    ew2 = np.zeros((P, 6, P), np.float32)
    ew2[:, 0:2] = rows(g["L1_ffn_sW2"])
    for e in range(4):
        ew2[:, 2 + e, 64 * (e % 2):64 * (e % 2) + 64] = g["L1_ffn_eW2"][e]
    arrays = {
        "consts": constants(),
        "lower": np.tril(np.ones((P, P), np.float32), -1),
        "sel0": selector(32, 64).astype(ml_dtypes.bfloat16),
        "sel1": np.tile(selector(4, 64), (GATE_PARTS["soft2"], 1)).astype(ml_dtypes.bfloat16),
        "sel2": np.tile(selector(8, D), (GATE_PARTS["share2"], 1)).astype(ml_dtypes.bfloat16),
        "x": g["x"], "src": g["src"], "dst": g["dst"], "etype": g["edge_type_7"],
        "eweight": g["edge_weight"].view(np.int32),
        "g0_w": rows(g["L0_gnn_W"].transpose(1, 0, 2).reshape(D, D)),
        "g0_a": np.stack([spread(g["L0_gnn_a_src"]), spread(g["L0_gnn_a_dst"])], 1),
        "f0_rw": rows(g["L0_ffn_router_w"].T), "f0_rb": g["L0_ffn_router_b"][None],
        "f0_w1": rows(g["L0_ffn_W1"].transpose(1, 0, 2).reshape(D, -1)), "f0_b1": column(g["L0_ffn_b1"]),
        "f0_w2": rows(g["L0_ffn_W2"].reshape(-1, D)), "f0_b2": g["L0_ffn_b2"],
        "g1_w": rows(g["L1_gnn_weights"].reshape(NTYPE, D, D).transpose(1, 0, 2).reshape(D, -1)),
        "m1_w1": rows(np.concatenate([g["L1_ffn_sW1"], g["L1_ffn_eW1"].transpose(1, 0, 2).reshape(D, -1)], 1)),
        "m1_b1": column(np.concatenate([g["L1_ffn_sb1"], g["L1_ffn_eb1"].reshape(-1)])),
        "m1_w2": ew2, "m1_b2": column(np.concatenate([g["L1_ffn_sb2"], g["L1_ffn_eb2"].reshape(-1)])),
        "m1_w3": rows(np.concatenate([g["L1_ffn_sW3"], g["L1_ffn_eW3"].reshape(-1, D)], 0)),
        "m1_b3": g["L1_ffn_eb3"], "m1_sb3": g["L1_ffn_sb3"][None],
        "m1_gw": rows(g["L1_ffn_gW"]), "m1_gb": g["L1_ffn_gb"][None],
        "g2_w": rows(g["L2_gnn_W"].T), "g2_b": g["L2_gnn_b"][None],
        "f2_rw": rows(g["L2_ffn_router_w"].T),
        "f2_w1": rows(g["L2_ffn_w1"].transpose(1, 0, 2).reshape(D, -1)), "f2_b1": column(g["L2_ffn_b1"]),
        "f2_w2": rows(g["L2_ffn_w2"].reshape(-1, D)), "f2_b2": g["L2_ffn_b2"],
        "g3_w1": rows(g["L3_gnn_W1"]), "g3_w2": rows(g["L3_gnn_W2"]),
        "g3_b1": spread(g["L3_gnn_b1"]), "g3_b2": spread(g["L3_gnn_b2"]), "g3_a": spread(g["L3_gnn_a"]),
        "f3_wr": rows(g["L3_ffn_wr"]), "f3_br": g["L3_ffn_br"][None],
        "f3_w1": rows(g["L3_ffn_w1"]), "f3_b1": column(g["L3_ffn_b1"]),
        "f3_w2": rows(g["L3_ffn_w2"]), "f3_b2": g["L3_ffn_b2"][None],
    }
    nc = _bacc.Bacc("TRN2", target_bir_lowering=False, num_devices=1)
    args = {}
    for name, a in arrays.items():
        arrays[name] = a = np.ascontiguousarray(a)
        args[name] = nc.dram_tensor(f"in_{name}", a.shape, mybir.dt.from_np(a.dtype), kind="ExternalInput").ap()
    out = nc.dram_tensor("out", (N, D), F32, kind="ExternalOutput").ap()
    build(nc, args, out)
    r = _run(nc, [{f"in_{n}": a for n, a in arrays.items()}], core_ids=[0])
    return r.results[0]["out"]
```
